# Optimizing a Trainium2 kernel written in Bass

```python
import numpy as np
import jax
import jax.numpy as jnp

def _softmax(x, axis=-1):
    return jax.nn.softmax(x, axis=axis)

def _gelu(x):
    return jax.nn.gelu(x, approximate=True)

def _silu(x):
    return jax.nn.silu(x)

def _sigmoid(x):
    return jax.nn.sigmoid(x)

def _layernorm(x, axis=-1, eps=1e-05):
    m = jnp.mean(x, axis=axis, keepdims=True)
    v = jnp.var(x, axis=axis, keepdims=True)
    return (x - m) / jnp.sqrt(v + eps)

def _scatter_add(tgt, idx, src, axis=0):
    return tgt.at[idx].add(src)

def _segment_sum(src, seg, n):
    return jax.ops.segment_sum(src, seg, n)
kernel_name = 'mk_gps_d2_gnn_r32_a9047e'

def setup_inputs(seed: int=0):
    np.random.seed(seed)
    _w = jnp.asarray

    def _rec_inputs():
        import jax
        import jax.numpy as jnp
        _gk = jax.random.key(seed)
        x = -0.0003713 + 1 * jax.random.normal(jax.random.fold_in(_gk, 1), (3125, 256), jnp.float32)
        _s = jax.random.randint(jax.random.fold_in(_gk, 2), (25000,), 0, 3125, jnp.int32)
        _d = jax.random.randint(jax.random.fold_in(_gk, 3), (25000,), 0, 3125, jnp.int32)
        _loop = jnp.arange(3125, dtype=jnp.int32)
        src = jnp.concatenate([_s, _d, _loop])
        dst = jnp.concatenate([_d, _s, _loop])
        _o = jnp.argsort(dst, stable=True)
        src = src[_o]
        dst = dst[_o]
        edge_attr_32 = 0.000189758 + 1.00013 * jax.random.normal(jax.random.fold_in(_gk, 11), (53125, 32), jnp.float32)
        return (x, src, dst, edge_attr_32)
    x, src, dst, edge_attr_32 = _rec_inputs()

    def _L0_gnn_setup():
        import jax, jax.numpy as jnp
        import numpy as np
        N_NODES = 50000
        N_EDGES = 50000
        IN_DIM, OUT_DIM, N_HEADS = (256, 64, 4)
        EPS = 1e-12
        key = jax.random.key(seed)
        k1, k2, k3, k4, k5 = jax.random.split(key, 5)
        h = jax.random.normal(k1, (N_NODES, IN_DIM), dtype=jnp.float32)
        edge_index = jax.random.randint(k2, (2, N_EDGES), 0, N_NODES, dtype=jnp.int32)
        W = jax.random.normal(k3, (IN_DIM, OUT_DIM), dtype=jnp.float32) * 0.05
        Wl = jax.random.normal(k4, (N_HEADS, OUT_DIM), dtype=jnp.float32) * 0.05
        Wr = jax.random.normal(k5, (N_HEADS, OUT_DIM), dtype=jnp.float32) * 0.05
        b = jnp.zeros((OUT_DIM,), dtype=jnp.float32)
        return {'h': h, 'W': W, 'Wl': Wl, 'Wr': Wr, 'b': b, 'edge_index': edge_index}
    _L0_gnn_all = _L0_gnn_setup()
    _L0_gnn_in = {k: v for k, v in _L0_gnn_all.items() if k in ('W', 'Wl', 'Wr', 'b')}
    del _L0_gnn_all

    def _L0_mix_setup():
        import jax, jax.numpy as jnp
        import numpy as np
        DIM = 256
        HEADS = 4
        HEAD_DIM = DIM // HEADS
        MLP_HIDDEN = DIM * 3
        B, N = (8, 128)
        EPS = 1e-05

        def _layernorm(x, g, b):
            mu = jnp.mean(x, axis=-1, keepdims=True)
            var = jnp.mean(jnp.square(x - mu), axis=-1, keepdims=True)
            return (x - mu) * jax.lax.rsqrt(var + EPS) * g + b
        key = jax.random.key(seed)
        ks = jax.random.split(key, 8)
        s = 0.02
        return {'x': jax.random.normal(ks[0], (B, N, DIM), dtype=jnp.float32), 'w_qkv': jax.random.normal(ks[1], (DIM, 3 * DIM), dtype=jnp.float32) * s, 'b_qkv': jnp.zeros((3 * DIM,), dtype=jnp.float32), 'norm_g': jnp.ones((DIM,), dtype=jnp.float32), 'norm_b': jnp.zeros((DIM,), dtype=jnp.float32), 'w_fc1': jax.random.normal(ks[2], (DIM, MLP_HIDDEN), dtype=jnp.float32) * s, 'b_fc1': jnp.zeros((MLP_HIDDEN,), dtype=jnp.float32), 'w_fc2': jax.random.normal(ks[3], (MLP_HIDDEN, DIM), dtype=jnp.float32) * s, 'b_fc2': jnp.zeros((DIM,), dtype=jnp.float32)}
    _L0_mix_all = _L0_mix_setup()
    _L0_mix_in = {k: v for k, v in _L0_mix_all.items() if k in ('w_qkv', 'b_qkv', 'norm_g', 'norm_b', 'w_fc1', 'b_fc1', 'w_fc2', 'b_fc2')}
    del _L0_mix_all

    def _L0_ffn_setup():
        import jax, jax.numpy as jnp
        import numpy as np
        B, S, D, H, E, K = (8, 256, 256, 1024, 8, 2)
        key = jax.random.key(seed)
        ks = jax.random.split(key, 7)
        s_in = 1.0 / np.sqrt(D)
        s_hid = 1.0 / np.sqrt(H)
        return {'x': jax.random.normal(ks[0], (B, S, D), dtype=jnp.float32), 'Wg': jax.random.uniform(ks[1], (E, D), jnp.float32, -s_in, s_in), 'bg': jax.random.uniform(ks[2], (E,), jnp.float32, -s_in, s_in), 'W1': jax.random.uniform(ks[3], (E, H, D), jnp.float32, -s_in, s_in), 'b1': jax.random.uniform(ks[4], (E, H), jnp.float32, -s_in, s_in), 'W2': jax.random.uniform(ks[5], (E, D, H), jnp.float32, -s_hid, s_hid), 'b2': jax.random.uniform(ks[6], (E, D), jnp.float32, -s_hid, s_hid)}
    _L0_ffn_all = _L0_ffn_setup()
    _L0_ffn_in = {k: v for k, v in _L0_ffn_all.items() if k in ('Wg', 'bg', 'W1', 'b1', 'W2', 'b2')}
    del _L0_ffn_all

    def _L1_gnn_setup():
        import jax, jax.numpy as jnp
        import numpy as np
        N_NODES = 50000
        N_EDGES = 50000
        IN_CH = 256
        ADAPTER = 64
        EDGE_DIM = 32
        key = jax.random.key(seed)
        ks = jax.random.split(key, 12)
        s = lambda k, shape: jax.random.normal(k, shape, dtype=jnp.float32) * 0.05
        x = jax.random.normal(ks[0], (N_NODES, IN_CH), dtype=jnp.float32)
        edge_index = jax.random.randint(ks[1], (2, N_EDGES), 0, N_NODES, dtype=jnp.int64)
        edge_attr = jax.random.normal(ks[2], (N_EDGES, EDGE_DIM), dtype=jnp.float32)
        return {'x': x, 'edge_index': edge_index, 'edge_attr': edge_attr, 'W_down': s(ks[3], (ADAPTER, IN_CH)), 'b_down': jnp.zeros((ADAPTER,), jnp.float32), 'W_time': s(ks[4], (ADAPTER, EDGE_DIM)), 'b_time': jnp.zeros((ADAPTER,), jnp.float32), 'W_fusion': s(ks[5], (ADAPTER, 2 * ADAPTER)), 'b_fusion': jnp.zeros((ADAPTER,), jnp.float32), 'W_up': s(ks[6], (IN_CH, ADAPTER)), 'b_up': jnp.zeros((IN_CH,), jnp.float32)}
    _L1_gnn_all = _L1_gnn_setup()
    _L1_gnn_in = {k: v for k, v in _L1_gnn_all.items() if k in ('W_down', 'b_down', 'W_time', 'b_time', 'W_fusion', 'b_fusion', 'W_up', 'b_up')}
    del _L1_gnn_all

    def _L1_mix_setup():
        import jax, jax.numpy as jnp
        import numpy as np
        HEADS, DIM_HEAD = (8, 64)
        EPS = 1e-05

        def instance_norm(t):
            mu = jnp.mean(t, axis=-1, keepdims=True)
            var = jnp.mean((t - mu) ** 2, axis=-1, keepdims=True)
            return (t - mu) * jax.lax.rsqrt(var + EPS)
        key = jax.random.key(seed)
        k1, k2, k3, k4 = jax.random.split(key, 4)
        B, N, D = (8, 256, 256)
        inner = HEADS * DIM_HEAD
        x = jax.random.normal(k1, (B, N, D), jnp.float32)
        w_qkv = jax.random.normal(k2, (3 * inner, D), jnp.float32) / np.sqrt(D).astype(np.float32)
        w_out = jax.random.normal(k3, (D, inner), jnp.float32) / np.sqrt(inner).astype(np.float32)
        b_out = 0.01 * jax.random.normal(k4, (D,), jnp.float32)
        return {'x': x, 'w_qkv': w_qkv, 'w_out': w_out, 'b_out': b_out}
    _L1_mix_all = _L1_mix_setup()
    _L1_mix_in = {k: v for k, v in _L1_mix_all.items() if k in ('w_qkv', 'w_out', 'b_out')}
    del _L1_mix_all

    def _L1_ffn_setup():
        import jax, jax.numpy as jnp
        import numpy as np
        N_EXPERTS = 8
        TOP_K = 2
        key = jax.random.key(seed)
        ks = jax.random.split(key, 5)
        B, T, C, E, H = (8, 64, 256, 8, 682)
        scale = 1.0 / np.sqrt(C)
        return {'x': jax.random.normal(ks[0], (B, T, C), dtype=jnp.float32), 'router_w': jax.random.normal(ks[1], (E, C), dtype=jnp.float32) * scale, 'w1': jax.random.normal(ks[2], (E, H, C), dtype=jnp.float32) * scale, 'w2': jax.random.normal(ks[3], (E, C, H), dtype=jnp.float32) * (1.0 / np.sqrt(H)), 'w3': jax.random.normal(ks[4], (E, H, C), dtype=jnp.float32) * scale}
    _L1_ffn_all = _L1_ffn_setup()
    _L1_ffn_in = {k: v for k, v in _L1_ffn_all.items() if k in ('router_w', 'w1', 'w2', 'w3')}
    del _L1_ffn_all
    return {'x': x, 'src': src, 'dst': dst, 'edge_attr_32': edge_attr_32, 'L0_gnn_W': _L0_gnn_in['W'], 'L0_gnn_Wl': _L0_gnn_in['Wl'], 'L0_gnn_Wr': _L0_gnn_in['Wr'], 'L0_gnn_b': _L0_gnn_in['b'], 'L0_mix_w_qkv': _L0_mix_in['w_qkv'], 'L0_mix_b_qkv': _L0_mix_in['b_qkv'], 'L0_mix_norm_g': _L0_mix_in['norm_g'], 'L0_mix_norm_b': _L0_mix_in['norm_b'], 'L0_mix_w_fc1': _L0_mix_in['w_fc1'], 'L0_mix_b_fc1': _L0_mix_in['b_fc1'], 'L0_mix_w_fc2': _L0_mix_in['w_fc2'], 'L0_mix_b_fc2': _L0_mix_in['b_fc2'], 'L0_ffn_Wg': _L0_ffn_in['Wg'], 'L0_ffn_bg': _L0_ffn_in['bg'], 'L0_ffn_W1': _L0_ffn_in['W1'], 'L0_ffn_b1': _L0_ffn_in['b1'], 'L0_ffn_W2': _L0_ffn_in['W2'], 'L0_ffn_b2': _L0_ffn_in['b2'], 'L1_gnn_W_down': _L1_gnn_in['W_down'], 'L1_gnn_b_down': _L1_gnn_in['b_down'], 'L1_gnn_W_time': _L1_gnn_in['W_time'], 'L1_gnn_b_time': _L1_gnn_in['b_time'], 'L1_gnn_W_fusion': _L1_gnn_in['W_fusion'], 'L1_gnn_b_fusion': _L1_gnn_in['b_fusion'], 'L1_gnn_W_up': _L1_gnn_in['W_up'], 'L1_gnn_b_up': _L1_gnn_in['b_up'], 'L1_mix_w_qkv': _L1_mix_in['w_qkv'], 'L1_mix_w_out': _L1_mix_in['w_out'], 'L1_mix_b_out': _L1_mix_in['b_out'], 'L1_ffn_router_w': _L1_ffn_in['router_w'], 'L1_ffn_w1': _L1_ffn_in['w1'], 'L1_ffn_w2': _L1_ffn_in['w2'], 'L1_ffn_w3': _L1_ffn_in['w3']}

def reference(x, src, dst, edge_attr_32, L0_gnn_W, L0_gnn_Wl, L0_gnn_Wr, L0_gnn_b, L0_mix_w_qkv, L0_mix_b_qkv, L0_mix_norm_g, L0_mix_norm_b, L0_mix_w_fc1, L0_mix_b_fc1, L0_mix_w_fc2, L0_mix_b_fc2, L0_ffn_Wg, L0_ffn_bg, L0_ffn_W1, L0_ffn_b1, L0_ffn_W2, L0_ffn_b2, L1_gnn_W_down, L1_gnn_b_down, L1_gnn_W_time, L1_gnn_b_time, L1_gnn_W_fusion, L1_gnn_b_fusion, L1_gnn_W_up, L1_gnn_b_up, L1_mix_w_qkv, L1_mix_w_out, L1_mix_b_out, L1_ffn_router_w, L1_ffn_w1, L1_ffn_w2, L1_ffn_w3):
    import jax
    import jax.numpy as jnp

    def _L0_gnn_ref(h, W, Wl, Wr, b, edge_index):
        import jax, jax.numpy as jnp
        import numpy as np
        N_NODES = 50000
        N_EDGES = 50000
        IN_DIM, OUT_DIM, N_HEADS = (256, 64, 4)
        EPS = 1e-12
        N = h.shape[0]
        H = Wl.shape[0]
        x = h @ W
        el = x @ Wl.T
        er = x @ Wr.T
        src, dst = (edge_index[0], edge_index[1])
        e = el[src] + er[dst]
        e = jnp.exp(jax.nn.leaky_relu(e, negative_slope=0.2))
        rowsum = jax.ops.segment_sum(e, src, num_segments=N)
        w = e / jnp.maximum(rowsum, EPS)[src]
        heads = [jax.ops.segment_sum(w[:, hd:hd + 1] * x[dst], src, num_segments=N) for hd in range(H)]
        out = jnp.stack(heads, axis=1)
        out = jax.nn.elu(out + b)
        return out.reshape(N, H * x.shape[1])

    def _L0_mix_ref(x, w_qkv, b_qkv, norm_g, norm_b, w_fc1, b_fc1, w_fc2, b_fc2):
        import jax, jax.numpy as jnp
        import numpy as np
        DIM = 256
        HEADS = 4
        HEAD_DIM = DIM // HEADS
        MLP_HIDDEN = DIM * 3
        B, N = (8, 128)
        EPS = 1e-05

        def _layernorm(x, g, b):
            mu = jnp.mean(x, axis=-1, keepdims=True)
            var = jnp.mean(jnp.square(x - mu), axis=-1, keepdims=True)
            return (x - mu) * jax.lax.rsqrt(var + EPS) * g + b
        Bx, Nx, C = x.shape
        scale = HEAD_DIM ** (-0.5)
        qkv = (x @ w_qkv + b_qkv).reshape(Bx, Nx, 3, HEADS, HEAD_DIM)
        qkv = jnp.transpose(qkv, (2, 0, 3, 1, 4))
        q, k, v = (qkv[0], qkv[1], qkv[2])
        k = k * scale
        attn = jnp.einsum('bhnd,bhne->bhde', k, v)
        attn = jax.nn.softmax(attn, axis=-1)
        xf = jnp.einsum('bhde,bhne->bhnd', attn, q)
        xf = jnp.transpose(xf, (0, 2, 1, 3)).reshape(Bx, Nx, C)
        x = x + xf
        h = _layernorm(x, norm_g, norm_b)
        h = jax.nn.gelu(h @ w_fc1 + b_fc1, approximate=False) @ w_fc2 + b_fc2
        return x + h

    def _L0_ffn_ref(x, Wg, bg, W1, b1, W2, b2):
        import jax, jax.numpy as jnp
        import numpy as np
        B, S, D, H, E, K = (8, 256, 256, 1024, 8, 2)
        gate_scores = jnp.einsum('bsd,ed->bse', x, Wg) + bg
        topk_scores, topk_idx = jax.lax.top_k(gate_scores, K)
        topk_probs = jax.nn.softmax(topk_scores, axis=-1)
        combine = jnp.sum(topk_probs[..., None] * jax.nn.one_hot(topk_idx, E, dtype=x.dtype), axis=-2)
        out = jnp.zeros_like(x)
        for e in range(E):
            h = jax.nn.relu(jnp.einsum('bsd,hd->bsh', x, W1[e]) + b1[e])
            y = jnp.einsum('bsh,dh->bsd', h, W2[e]) + b2[e]
            out = out + combine[..., e:e + 1] * y
        return out

    def _L1_gnn_ref(x, edge_index, edge_attr, W_down, b_down, W_time, b_time, W_fusion, b_fusion, W_up, b_up):
        import jax, jax.numpy as jnp
        import numpy as np
        N_NODES = 50000
        N_EDGES = 50000
        IN_CH = 256
        ADAPTER = 64
        EDGE_DIM = 32
        n = x.shape[0]
        node_feat = jax.nn.relu(x @ W_down.T + b_down)
        time_feat = jax.nn.relu(edge_attr @ W_time.T + b_time)
        src = edge_index[0]
        sums = jax.ops.segment_sum(time_feat, src, num_segments=n)
        counts = jax.ops.segment_sum(jnp.ones((time_feat.shape[0],), jnp.float32), src, num_segments=n)
        node_time_feat = sums / jnp.maximum(counts, 1.0)[:, None]
        combined = jnp.concatenate([node_feat, node_time_feat], axis=-1)
        fused = jax.nn.relu(combined @ W_fusion.T + b_fusion)
        out = fused @ W_up.T + b_up
        return x + out

    def _L1_mix_ref(x, w_qkv, w_out, b_out):
        import jax, jax.numpy as jnp
        import numpy as np
        HEADS, DIM_HEAD = (8, 64)
        EPS = 1e-05

        def instance_norm(t):
            mu = jnp.mean(t, axis=-1, keepdims=True)
            var = jnp.mean((t - mu) ** 2, axis=-1, keepdims=True)
            return (t - mu) * jax.lax.rsqrt(var + EPS)
        B, N, _ = x.shape
        H, Dh = (HEADS, DIM_HEAD)
        qkv = jnp.einsum('bnd,ed->bne', x, w_qkv)
        q, k, v = jnp.split(qkv, 3, axis=-1)

        def to_heads(t):
            return t.reshape(B, N, H, Dh).transpose(0, 2, 1, 3)
        q, k, v = (to_heads(q), to_heads(k), to_heads(v))
        k = instance_norm(k)
        v = instance_norm(v)
        dots = jnp.einsum('bhnd,bhne->bhde', k, v)
        out = jnp.einsum('bhnd,bhde->bhne', q, dots) / N
        out = out.transpose(0, 2, 1, 3).reshape(B, N, H * Dh)
        return jnp.einsum('bne,de->bnd', out, w_out) + b_out

    def _L1_ffn_ref(x, router_w, w1, w2, w3):
        import jax, jax.numpy as jnp
        import numpy as np
        N_EXPERTS = 8
        TOP_K = 2
        B, T, C = x.shape
        flat = x.reshape(-1, C)
        logits = flat @ router_w.T
        probs = jax.nn.softmax(logits, axis=-1)
        topk_probs, topk_idx = jax.lax.top_k(probs, TOP_K)
        topk_probs = topk_probs / (jnp.sum(topk_probs, axis=-1, keepdims=True) + 1e-09)
        onehot = jax.nn.one_hot(topk_idx, N_EXPERTS, dtype=flat.dtype)
        gates = jnp.einsum('nk,nke->ne', topk_probs, onehot)
        h1 = jnp.einsum('nc,ehc->neh', flat, w1)
        h3 = jnp.einsum('nc,ehc->neh', flat, w3)
        h = jax.nn.silu(h1) * h3
        y = jnp.einsum('neh,ech->nec', h, w2)
        out = jnp.einsum('ne,nec->nc', gates, y)
        return out.reshape(B, T, C)
    edge_index = jnp.stack([src, dst])
    xn = _layernorm(x, axis=-1)
    x = x + _L0_gnn_ref(xn, L0_gnn_W, L0_gnn_Wl, L0_gnn_Wr, L0_gnn_b, edge_index) + _L0_mix_ref(xn[None], L0_mix_w_qkv, L0_mix_b_qkv, L0_mix_norm_g, L0_mix_norm_b, L0_mix_w_fc1, L0_mix_b_fc1, L0_mix_w_fc2, L0_mix_b_fc2)[0]
    x = x + _L0_ffn_ref(_layernorm(x, axis=-1)[None], L0_ffn_Wg, L0_ffn_bg, L0_ffn_W1, L0_ffn_b1, L0_ffn_W2, L0_ffn_b2)[0]
    xn = _layernorm(x, axis=-1)
    x = x + _L1_gnn_ref(xn, edge_index, edge_attr_32, L1_gnn_W_down, L1_gnn_b_down, L1_gnn_W_time, L1_gnn_b_time, L1_gnn_W_fusion, L1_gnn_b_fusion, L1_gnn_W_up, L1_gnn_b_up) + _L1_mix_ref(xn[None], L1_mix_w_qkv, L1_mix_w_out, L1_mix_b_out)[0]
    x = x + _L1_ffn_ref(_layernorm(x, axis=-1)[None], L1_ffn_router_w, L1_ffn_w1, L1_ffn_w2, L1_ffn_w3)[0]
    return x

_drawn_inputs = setup_inputs


def setup_inputs(seed=0):
    import zlib

    import numpy as np

    out = dict(_drawn_inputs(seed))
    spreads = {'L0_gnn_b': (0.0, 0.1),
     'L0_mix_b_qkv': (0.0, 0.1),
     'L0_mix_norm_g': (1.0, 0.6),
     'L0_mix_norm_b': (0.0, 0.679),
     'L0_mix_b_fc1': (0.0, 0.32),
     'L0_mix_b_fc2': (0.0, 0.1),
     'L1_gnn_b_down': (0.0, 2.0),
     'L1_gnn_b_time': (0.0, 2.0),
     'L1_gnn_b_fusion': (0.0, 0.498),
     'L1_gnn_b_up': (0.0, 0.1)}
    factors = {'edge_attr_32': 8.0,
     'L0_gnn_Wl': 13.729,
     'L0_ffn_bg': 2.881,
     'L0_ffn_b1': 6.791,
     'L0_ffn_b2': 5.494,
     'L1_gnn_W_down': 3.025,
     'L1_gnn_W_time': 8.0,
     'L1_mix_b_out': 8.0}
    for name, (base, spread) in spreads.items():
        noise = np.random.default_rng([zlib.crc32(name.encode()), seed]).standard_normal(out[name].shape)
        drawn = base * np.exp(spread * noise) if base else spread * noise
        out[name] = jnp.asarray(drawn.astype(out[name].dtype))
    for name, factor in factors.items():
        out[name] = (out[name] * factor).astype(out[name].dtype)
    return out
```

```python
from contextlib import ExitStack

import concourse.bass as bass
from concourse import mybir

F32 = mybir.dt.float32
I32 = mybir.dt.int32
U32 = mybir.dt.uint32
ALU = mybir.AluOpType
ACT = mybir.ActivationFunctionType
AXX = mybir.AxisListType.X

N = 3125
D = 256
P = 125
T = N // P
KC = D // 128
E = 53125
EC = E // P
EU = 5
SLOT = 128
ET = 448
PAY = 34
AT = 32
HD = 64
NH = 4
TAB = HD + NH
VW = NH * HD + NH + HD + 1
O_W, O_T, O_C = NH * HD, NH * HD + NH, NH * HD + NH + HD
MLP = 768
NE = 8
TOPK = 2
FT = 56
H0 = 1024
H1 = 682
H1C = 6
EPS = 1e-5
assert T * P == N and EC * P == E and EC % (2 * EU) == 5 and ET % 16 == 0
assert (E + T * (SLOT - 1)) // SLOT <= ET and (N * TOPK + NE * (SLOT - 1)) // SLOT == FT


def over_tiles(eng, body, count=T):
    with eng.Fori(0, count // 2) as j:
        body(j * 2, 0)
        body(j * 2 + 1, 1)
    if count % 2:
        body(count - 1, 0)


def over_tiles_summed(eng, body, count=T):
    body(0, 0, True, False)
    with eng.Fori(0, (count - 2) // 2) as j:
        body(j * 2 + 1, 1, False, False)
        body(j * 2 + 2, 0, False, False)
    if count % 2:
        body(count - 2, 1, False, False)
    body(count - 1, (count - 1) % 2, False, True)


class Stage:

    def __init__(self, nc, name):
        self.nc, self.name = nc, name

    def __enter__(self):
        self.ctx, self.used = ExitStack(), []
        return self

    def __exit__(self, *a):
        self.ctx.close()
        if self.used:
            self.nc.clear_and_free_semaphores(self.used)
            self.nc.all_engine_barrier(sem_only=True)

    def sb(self, name, shape, dt=F32):
        return self.ctx.enter_context(self.nc.sbuf_tensor(f"{self.name}_{name}", shape, dt))

    def sem(self, name):
        self.used.append(self.nc.alloc_semaphore(f"{self.name}_{name}"))
        return self.used[-1]

    def sems(self, name, n=2):
        return [self.sem(f"{name}{k}") for k in range(n)]

    def block(self):
        return self.ctx.enter_context(self.nc.Block())


def layer_stats(v, x, stats, mv, rstd, done, ready):
    with v.Fori(0, T) as t:
        v.bn_stats(tile_of(stats, t), tile_of(x, t)).then_inc(done, 1)
    v.wait_ge(done, T)
    v.tensor_tensor(mv[:, :, 0], stats[:, :, 1], stats[:, :, 4], ALU.add).then_inc(done, 1)
    v.tensor_tensor(mv[:, :, 1], stats[:, :, 1], stats[:, :, 4], ALU.subtract).then_inc(done, 1)
    v.tensor_tensor(rstd[:, :], stats[:, :, 2], stats[:, :, 5], ALU.add).then_inc(done, 1)
    v.wait_ge(done, T + 3)
    v.tensor_scalar(mv[:, :, 0], mv[:, :, 0], 0.5, None, ALU.mult).then_inc(done, 1)
    v.tensor_tensor(mv[:, :, 1], mv[:, :, 1], mv[:, :, 1], ALU.mult).then_inc(done, 1)
    v.tensor_scalar(rstd[:, :], rstd[:, :], 1.0 / D, EPS, ALU.mult, ALU.add).then_inc(done, 1)
    v.wait_ge(done, T + 6)
    v.scalar_tensor_tensor(out=rstd[:, :], in0=mv[:, :, 1], scalar=0.25, in1=rstd[:, :],
                           op0=ALU.mult, op1=ALU.add).then_inc(done, 1)
    v.wait_ge(done, T + 7)
    v.reciprocal(rstd[:, :], rstd[:, :]).then_inc(ready, 1)


def bins_buffers(st, B, C):
    return dict(
        onehot=st.sb("onehot", [P, B + 1, C]), cum=st.sb("cum", [P, B, C]), cnt=st.sb("cnt", [P, B + 1]),
        part=st.sb("part", [P, B]), tot=st.sb("tot", [P, B]), toti=st.sb("toti", [P, B], I32),
        pad=st.sb("pad", [P, B]), start=st.sb("start", [P, B + 1]), posf=st.sb("posf", [P, C]),
        done=st.sem("bin_done"), counted=st.sem("bin_counted"), summed=st.sem("bin_summed"))


def bins_vector(v, k, value, bound, one, B, C, psum, rows, map_out, map_n, tile_at, two, wide, ready):
    oh, cum, cnt, done = k["onehot"], k["cum"], k["cnt"], k["done"]
    v.tensor_tensor(oh[:, :, :], value.unsqueeze(1).broadcast_to([P, B + 1, C]),
                    bound[0:P, 0:B + 1].unsqueeze(2).broadcast_to([P, B + 1, C]), ALU.is_ge).then_inc(done, 1)
    v.wait_ge(done, 1)
    v.tensor_tensor(oh[:, 0:B, :], oh[:, 0:B, :], oh[:, 1:B + 1, :], ALU.subtract).then_inc(done, 1)
    v.wait_ge(done, 2)
    flat = oh[:, 0:B, :].rearrange("p b c -> p (b c)")
    v.tensor_tensor_scan(cum[:, :, :].rearrange("p b c -> p (b c)"), one[0:P, 0:1].broadcast_to([P, B * C]),
                         flat, 0.0, ALU.mult, ALU.add).then_inc(done, 1)
    v.memset(cnt[:, 0:1], 0.0).then_inc(done, 1)
    v.wait_ge(done, 4)
    v.tensor_copy(cnt[:, 1:B + 1], cum[:, :, C - 1]).then_inc(done, 1)
    v.wait_ge(done, 5)
    v.tensor_tensor(k["part"][:, :], cnt[:, 1:B + 1], cnt[:, 0:B], ALU.subtract).then_inc(k["counted"], 1)
    v.wait_ge(k["summed"], 1)
    v.tensor_scalar(k["toti"][:, :], psum[0:P, B:2 * B], float(SLOT - 1), None, ALU.add).then_inc(done, 1)
    v.wait_ge(done, 6)
    v.tensor_scalar(k["toti"][:, :], k["toti"][:, :], 7, 7, ALU.logical_shift_right,
                    ALU.logical_shift_left).then_inc(done, 1)
    v.wait_ge(done, 7)
    v.tensor_copy(k["pad"][:, :], k["toti"][:, :]).then_inc(done, 1)
    v.memset(k["start"][:, 0:1], 0.0).then_inc(done, 1)
    v.wait_ge(done, 9)
    v.tensor_tensor_scan(k["start"][:, 1:B + 1], one[0:P, 0:1].broadcast_to([P, B]), k["pad"][:, :], 0.0,
                         ALU.mult, ALU.add).then_inc(done, 1)
    v.wait_ge(done, 10)
    v.tensor_tensor(k["tot"][:, :], psum[0:P, 0:B], k["start"][:, 0:B], ALU.add).then_inc(done, 1)
    v.wait_ge(done, 11)
    v.scalar_tensor_tensor(out=k["tot"][:, :], in0=k["tot"][:, :], scalar=-1.0, in1=cnt[:, 0:B],
                           op0=ALU.add, op1=ALU.subtract).then_inc(done, 1)
    v.wait_ge(done, 12)
    v.tensor_tensor(cum[:, :, :], cum[:, :, :], k["tot"][:, :].unsqueeze(2).broadcast_to([P, B, C]),
                    ALU.add).then_inc(done, 1)
    v.wait_ge(done, 13)
    v.tensor_tensor(cum[:, :, :], cum[:, :, :], oh[:, 0:B, :], ALU.mult).then_inc(done, 1)
    v.wait_ge(done, 14)
    v.tensor_reduce(k["posf"][:, :], cum[:, :, :].rearrange("p b c -> p c b"), AXX, ALU.add).then_inc(done, 1)
    v.wait_ge(done, 15)
    n = 15
    if rows is not None:
        pi, lane, tile, row = rows
        v.tensor_copy(pi[:, :], k["posf"][:, :]).then_inc(done, 1)
        v.wait_ge(done, 16)
        v.tensor_scalar(lane[:, :], pi[:, :], SLOT - 1, None, ALU.bitwise_and).then_inc(done, 1)
        v.tensor_scalar(tile[:, :], pi[:, :], 7, None, ALU.logical_shift_right).then_inc(done, 1)
        v.wait_ge(done, 18)
        v.scalar_tensor_tensor(out=row[:, :], in0=lane[:, :], scalar=float(ET), in1=tile[:, :],
                               op0=ALU.mult, op1=ALU.add).then_inc(done, 1)
        v.wait_ge(done, 19)
        n = 19
    v.sem_inc(ready, 1)
    v.tensor_tensor(wide, tile_at[0:1, 0:map_n].unsqueeze(2).broadcast_to([1, map_n, B - 1]),
                    k["start"][0:1, 1:B].unsqueeze(1).broadcast_to([1, map_n, B - 1]), ALU.is_ge).then_inc(done, 1)
    v.wait_ge(done, n + 1)
    v.tensor_reduce(two, wide, AXX, ALU.add).then_inc(done, 1)
    v.wait_ge(done, n + 2)
    v.tensor_copy(map_out, two).then_inc(done, 1)
    v.wait_ge(done, n + 3)


def bins_tensor(pe, k, before, ones, B, psum):
    pe.wait_ge(k["counted"], 1)
    pe.matmul(psum[0:P, 0:B], before[0:P, 0:P], k["part"][:, :], start=True, stop=True)
    pe.matmul(psum[0:P, B:2 * B], ones[0:P, 0:P], k["part"][:, :], start=True, stop=True).then_inc(k["summed"], 1)


def tile_of(x, t):
    return x[:, bass.ds(t, 1), :].rearrange("p o f -> p (o f)")


def build(nc, a, out):
    with ExitStack() as ctx:
        def sb(name, shape, dt=F32):
            return ctx.enter_context(nc.sbuf_tensor(name, shape, dt))

        g = {
            "table": nc.dram_tensor("table", (N, TAB), F32).ap(),
            "slots": nc.dram_tensor("slots", (SLOT * ET, PAY), F32).ap(),
            "xs": nc.dram_tensor("xs", (FT * SLOT, D), F32).ap(),
            "ys": nc.dram_tensor("ys", (FT * SLOT, D), F32).ap(),
        }
        g["x"] = sb("x_nodes", [P, T, D])
        g["mv"] = sb("mv", [P, T, 2])
        g["rstd"] = sb("rstd", [P, T])
        g["ident"] = sb("ident", [128, 128])
        g["ones"] = sb("ones", [128, 128])
        g["before"] = sb("before", [128, 128])
        g["bound"] = sb("bound", [128, T + 1])
        g["bin_no"] = sb("bin_no", [128, T + 1])
        g["tile_at"] = sb("tile_at", [1, ET])
        g["time"] = sb("time", [P, T, HD + 1])
        g["el"] = sb("el", [P, T, NH])
        g["edge_map"] = sb("edge_map", [1, ET], I32)
        g["bank"] = [ctx.enter_context(nc.psum_tensor(f"bank{k}", [128, 512], F32)) for k in range(8)]
        front(nc, a, g)
        with Stage(nc, "G") as agg:
            g["agg"] = agg.sb("agg", [P, T, VW])
            edge_aggregation(nc, a, g)
            gat_finish(nc, a, g)
        moe(nc, a, g, 0)
        with Stage(nc, "L") as l1:
            g["c1"] = l1.sb("c1", [128, KC, D])
            l1_keys_values(nc, a, g)
            l1_update(nc, a, g)
        moe(nc, a, g, 1, out)


def front(nc, a, g):
    bank = g["bank"]
    table_rows = g["table"].rearrange("(t p) f -> t p f", p=P)
    attr = a["edge_attr_32"].rearrange("(p c) f -> p c f", c=EC)
    slots_pf = g["slots"].rearrange("(p t) f -> p (t f)", p=SLOT)
    FILLS = 8
    ROUNDS = EC // EU
    MC = MLP // 128
    with Stage(nc, "A") as st:
        src_i = st.sb("src_i", [P, EC], I32)
        dst_i = st.sb("dst_i", [P, EC], I32)
        src_f = st.sb("src_f", [P, EC])
        ends = st.sb("ends", [P, EC, 2], I32)
        k = bins_buffers(st, T, EC)
        pos_i = st.sb("pos_i", [P, EC], I32)
        lane_i = st.sb("lane_i", [P, EC], I32)
        tile_i = st.sb("tile_i", [P, EC], I32)
        row_i = st.sb("row_i", [P, EC], I32)
        narrow = st.sb("narrow", [1, ET])
        fill = st.sb("fill", [128, ET // FILLS, PAY])
        pay = st.sb("pay", [P, 2, EU, PAY])
        ids = st.sb("ids", [P, 2, EU], I32)
        w72 = st.sb("w72", [128, KC, TAB + NH])
        wT = st.sb("wT", [HD, D])
        wlrT = st.sb("wlrT", [HD, 2 * NH])
        stats = st.sb("stats", [P, T, 6])
        xn = st.sb("xn", [P, 2, D + 1])
        xT = st.sb("xT", [128, 2, KC, P])
        tab = st.sb("tab", [P, 2, TAB + NH])
        wkv = st.sb("wkv", [128, KC, 2 * D])
        bkv = st.sb("bkv", [1, 2 * D])
        wqT = st.sb("wqT", [128, KC, D])
        bq = st.sb("bq", [128, KC])
        nn = st.sb("nn", [1, 1])
        gram = st.sb("gram", [128, KC, D + 1])
        grow = st.sb("grow", [1, D])
        gwv = st.sb("gwv", [128, KC, D])
        gwv_row = st.sb("gwv_row", [1, D])
        logit = st.sb("logit", [128, KC, HD])
        lmax = st.sb("lmax", [128, KC])
        lsum = st.sb("lsum", [128, KC])
        diag = st.sb("diag", [128, KC, 128])
        attnT = st.sb("attnT", [128, KC, 128])
        c0 = st.sb("c0", [128, KC, D])
        c0_row = st.sb("c0_row", [1, D])
        x1 = k["cum"][:, :, :].rearrange("p b c -> p (b c)")[:, 0:T * D].rearrange("p (t f) -> p t f", f=D)
        mv1 = st.sb("mv1", [P, T, 2])
        rstd1 = st.sb("rstd1", [P, T])
        lnT = st.sb("lnT", [128, 2, KC])
        fc1 = st.sb("fc1", [128, KC, MLP])
        fb1 = st.sb("fb1", [128, MC])
        fc2 = st.sb("fc2", [128, MC, D])
        fb2 = st.sb("fb2", [1, D])
        gT = st.sb("gT", [128, 2, MC, P])
        s_edges, s_w, s_x, s_wm = st.sem("edges"), st.sem("weights"), st.sem("x_loaded"), st.sem("mix_weights")
        s_const, s_ones = st.sem("const"), st.sem("ones")
        s_fill, s_filled = st.sem("fill"), st.sem("filled")
        s_rows, s_ends = st.sem("rows_ready"), st.sem("round_ends")
        s_go = st.sem("round_go")
        s_attr, s_scat = st.sems("attr_loaded"), st.sems("scattered")
        s_ln = st.sem("ln")
        s_stat, s_rstd, s_var = st.sem("stat"), st.sem("rstd"), st.sem("var")
        s_xn, s_tr, s_xT, s_h, s_tab, s_wa, s_waT = (st.sem(n) for n in (
            "xn_ready", "transposed", "xT_ready", "h_ready", "tab_ready", "wa", "wa_ready"))
        s_st = st.sems("table_stored")
        ps_bin, ps_g = bank[0], [bank[1], bank[2]]
        ps_t, ps_h = [bank[3], bank[4]], [bank[5], bank[6]]
        s_gram, s_fold_pe, s_fold = st.sem("gram"), st.sem("fold_pe"), st.sem("fold")
        s_b_xn, s_b_tr, s_b_xT, s_b_mm, s_b_x1, s_b_st = (st.sem("b_" + n) for n in (
            "xn", "tr", "xT", "mm", "x1", "stat"))
        s_m_xn, s_m_tr, s_m_xT, s_m_h, s_m_g, s_m_y, s_m_out, s_m_var, s_m_rstd = (st.sem("m_" + n) for n in (
            "xn", "tr", "xT", "h", "g", "y", "out", "var", "rstd"))
        block = st.block()

        @block.sync
        def _(sp):
            sp.dma_start(src_i[:, :], a["src"].rearrange("(p c) -> p c", c=EC)).then_inc(s_edges, 16)
            sp.dma_start(dst_i[:, :], a["dst"].rearrange("(p c) -> p c", c=EC)).then_inc(s_edges, 16)
            sp.dma_start(g["x"][:, :, :], a["x"].rearrange("(t p) f -> p t f", p=P)).then_inc(s_x, 16)
            sp.dma_start(w72[:, :, 0:HD], a["L0_gnn_W"].rearrange("(k p) f -> p k f", p=128)).then_inc(s_w, 16)
            sp.dma_start(wT[:, :], a["L0_gnn_W_T"]).then_inc(s_w, 16)
            sp.dma_start(wlrT[:, 0:NH], a["L0_gnn_Wr_T"]).then_inc(s_w, 16)
            sp.dma_start(wlrT[:, NH:2 * NH], a["L0_gnn_Wl_T"]).then_inc(s_w, 16)
            mix = [(wkv[:, :, :], a["L0_mix_w_qkv"].rearrange("(k p) f -> p k f", p=128)[:, :, D:3 * D]),
                   (bkv[:, :], a["L0_mix_b_qkv"][D:3 * D].unsqueeze(0)),
                   (wqT[:, :, :], a["L0_mix_w_q_T"].rearrange("(k p) f -> p k f", p=128)),
                   (bq[:, :], a["L0_mix_b_q_cols"]),
                   (lnT[:, 0, :], a["L0_mix_norm_g_cols"]), (lnT[:, 1, :], a["L0_mix_norm_b_cols"]),
                   (fc1[:, :, :], a["L0_mix_w_fc1"].rearrange("(k p) f -> p k f", p=128)),
                   (fb1[:, :], a["L0_mix_b_fc1_cols"]),
                   (fc2[:, :, :], a["L0_mix_w_fc2"].rearrange("(k p) f -> p k f", p=128)),
                   (fb2[:, :], a["L0_mix_b_fc2"].unsqueeze(0))]
            for dst, src in mix:
                sp.dma_start(dst, src).then_inc(s_wm, 16)
            sp.wait_ge(s_fill, 3)
            w = ET // FILLS * PAY
            for q in range(FILLS):
                sp.dma_start(slots_pf[:, q * w:(q + 1) * w],
                             fill[:, :, :].rearrange("p t f -> p (t f)")).then_inc(s_filled, 16)
            with sp.Fori(0, ROUNDS // 2) as j:
                for b in range(2):
                    sp.wait_ge(s_scat[b], j * (16 * EU))
                    sp.dma_start(pay[:, b, :, 0:AT], attr[:, bass.ds((j * 2 + b) * EU, EU), :]).then_inc(s_attr[b], 16)
            sp.wait_ge(s_scat[0], ROUNDS // 2 * 16 * EU)
            sp.dma_start(pay[:, 0, :, 0:AT], attr[:, EC - EU:EC, :]).then_inc(s_attr[0], 16)

        @block.gpsimd
        def _(gp):
            gp.iota(g["bound"][:, :], [[P, T + 1]], base=0, channel_multiplier=0,
                    allow_small_or_imprecise_dtypes=True).then_inc(s_const, 1)
            gp.iota(g["bin_no"][:, :], [[1, T + 1]], base=0, channel_multiplier=0,
                    allow_small_or_imprecise_dtypes=True).then_inc(s_const, 1)
            gp.iota(g["tile_at"][:, :], [[SLOT, ET]], base=0, channel_multiplier=0,
                    allow_small_or_imprecise_dtypes=True).then_inc(s_const, 1)
            gp.memset(g["ones"][:, :], 1.0).then_inc(s_ones, 1)
            gp.wait_ge(s_ones, 1)
            gp.affine_select(out=g["ident"][:, :], in_=g["ones"][:, :], compare_op=ALU.is_equal, fill=0.0, base=0,
                             pattern=[[1, 128]], channel_multiplier=-1).then_inc(s_const, 1)
            gp.affine_select(out=g["before"][:, :], in_=g["ones"][:, :], compare_op=ALU.is_gt, fill=0.0, base=0,
                             pattern=[[1, 128]], channel_multiplier=-1).then_inc(s_const, 1)
            gp.memset(xn[:, :, D:D + 1], 1.0).then_inc(s_const, 1)
            gp.memset(nn[:, :], float(N)).then_inc(s_const, 1)
            gp.memset(diag[:, :, :], 0.0).then_inc(s_const, 1)
            gp.wait_ge(s_rows, 1)
            gp.wait_ge(s_filled, 16 * FILLS)

            def scatter(r, b, cols):
                gp.tensor_copy(pay[:, b, :, AT:PAY].bitcast(I32), ends[:, cols, :]).then_inc(s_ends, 1)
                gp.tensor_copy(ids[:, b, :], row_i[:, cols]).then_inc(s_ends, 1)
                gp.wait_ge(s_ends, r * 2 + 2)
                gp.wait_ge(s_attr[b], (r - b + 2) * 8 if b == 0 else (r + 1) * 8)
                gp.sem_inc(s_go, 1)
                for u in range(EU):
                    gp.indirect_dma_start(g["slots"], bass.IndirectOffsetOnAxis(ap=ids[:, b, u:u + 1], axis=0),
                                          pay[:, b, u, :], None).then_inc(s_scat[b], 16)
            with gp.Fori(0, ROUNDS // 2) as j:
                for b in range(2):
                    gp.wait_ge(s_scat[b], j * (16 * EU))
                    scatter(j * 2 + b, b, bass.ds((j * 2 + b) * EU, EU))
            gp.wait_ge(s_scat[0], ROUNDS // 2 * 16 * EU)
            scatter(ROUNDS - 1, 0, slice(EC - EU, EC))
            gp.wait_ge(s_scat[0], (ROUNDS // 2 + 1) * 16 * EU)
            gp.wait_ge(s_scat[1], ROUNDS // 2 * 16 * EU)

        @block.vector
        def _(v):
            v.memset(fill[:, :, 0:AT], 0.0).then_inc(s_fill, 1)
            v.memset(fill[:, :, AT:AT + 1], -1.0).then_inc(s_fill, 1)
            v.memset(fill[:, :, AT + 1:PAY], 0.0).then_inc(s_fill, 1)
            v.wait_ge(s_edges, 32)
            v.tensor_copy(src_f[:, :], src_i[:, :]).then_inc(s_stat, 1)
            v.tensor_copy(ends[:, :, 1], dst_i[:, :]).then_inc(s_stat, 1)
            v.wait_ge(s_stat, 1)
            v.tensor_copy(ends[:, :, 0].bitcast(F32), src_f[:, :]).then_inc(s_stat, 1)
            v.wait_ge(s_const, 8)
            wide = k["onehot"][0:1, :, :].rearrange("o b c -> o (b c)")[:, 0:ET * (T - 1)].rearrange(
                "o (t b) -> o t b", b=T - 1)
            bins_vector(v, k, src_f[:, :], g["bound"], g["ones"], T, EC, ps_bin,
                        (pos_i, lane_i, tile_i, row_i), g["edge_map"][:, :], ET, g["tile_at"],
                        narrow[:, :], wide, s_rows)
            v.wait_ge(s_x, 16)
            layer_stats(v, g["x"], stats, g["mv"], g["rstd"], s_ln, s_var)
            v.wait_ge(s_wa, 1)
            v.tensor_copy(w72[:, :, HD:TAB + NH],
                          bank[7][:, 0:4 * NH].rearrange("p (k f) -> p k f", k=2)).then_inc(s_waT, 1)
            v.wait_ge(s_rstd, 1)

            def normalise(t, b):
                v.wait_ge(s_tr, t)
                v.tensor_scalar(xn[:, b, 0:D], tile_of(g["x"], t), tile_of(g["mv"], t)[:, 0:1],
                                g["rstd"][:, bass.ds(t, 1)], ALU.subtract, ALU.mult).then_inc(s_xn, 1)
            over_tiles(v, normalise)

            for c in range(KC):
                v.wait_ge(s_fold_pe, 4)
                for h in range(2):
                    r = slice(h * HD, h * HD + HD)
                    v.tensor_copy(logit[r, c, :], bank[5][r, c * 128 + h * HD:c * 128 + h * HD + HD]).then_inc(s_fold, 1)
            v.wait_ge(s_fold, 4)
            v.tensor_reduce(lmax[:, :], logit[:, :, :], AXX, ALU.max).then_inc(s_fold, 1)
            v.wait_ge(s_fold, 5)
            v.tensor_tensor(logit[:, :, :], logit[:, :, :], lmax[:, :].unsqueeze(2).broadcast_to([128, KC, HD]),
                            ALU.subtract).then_inc(s_fold, 1)
            v.wait_ge(s_fold, 7)
            v.tensor_reduce(lsum[:, :], logit[:, :, :], AXX, ALU.add).then_inc(s_fold, 1)
            v.wait_ge(s_fold, 8)
            v.reciprocal(lsum[:, :], lsum[:, :]).then_inc(s_fold, 1)
            v.wait_ge(s_fold, 9)
            for c in range(KC):
                for h in range(2):
                    r = slice(h * HD, h * HD + HD)
                    v.tensor_scalar(diag[r, c, h * HD:h * HD + HD], logit[r, c, :], lsum[r, c:c + 1], None,
                                    ALU.mult).then_inc(s_fold, 1)

            def attend(t, b):
                v.wait_ge(s_b_tr, t)
                v.wait_ge(s_b_x1, t)
                v.tensor_scalar(xn[:, b, 0:D], tile_of(g["x"], t), tile_of(g["mv"], t)[:, 0:1],
                                g["rstd"][:, bass.ds(t, 1)], ALU.subtract, ALU.mult).then_inc(s_b_xn, 1)
                v.wait_ge(s_b_mm, t + 1)
                v.wait_ge(s_b_xn, t + 1)
                v.tensor_tensor(tile_of(x1, t), ps_h[b][0:P, 0:D], xn[:, b, 0:D], ALU.add).then_inc(s_b_x1, 1)
            over_tiles(v, attend)
            v.wait_ge(s_b_x1, T)
            layer_stats(v, x1, stats, mv1, rstd1, s_b_st, s_m_var)
            v.wait_ge(s_m_rstd, 1)

            def mlp_in(t, b):
                v.wait_ge(s_m_tr, t)
                v.tensor_scalar(xn[:, b, 0:D], tile_of(x1, t), tile_of(mv1, t)[:, 0:1],
                                rstd1[:, bass.ds(t, 1)], ALU.subtract, ALU.mult).then_inc(s_m_xn, 1)
                v.tensor_tensor(tile_of(g["x"], t), tile_of(g["x"], t), tile_of(x1, t), ALU.add).then_inc(s_m_out, 1)
                v.wait_ge(s_m_out, t * 2 + 1)
                v.wait_ge(s_m_y, t + 1)
                v.tensor_tensor(tile_of(g["x"], t), tile_of(g["x"], t), ps_h[b][0:P, 0:D], ALU.add).then_inc(s_m_out, 1)
            over_tiles(v, mlp_in)

        @block.tensor
        def _(pe):
            pe.wait_ge(s_w, 64)
            pe.matmul(bank[7][:, 0:2 * NH], wT[:, 0:128], wlrT[:, :], start=True, stop=True)
            pe.matmul(bank[7][:, 2 * NH:4 * NH], wT[:, 128:256], wlrT[:, :], start=True, stop=True).then_inc(s_wa, 1)
            pe.wait_ge(s_const, 8)
            bins_tensor(pe, k, g["before"], g["ones"], T, ps_bin)
            pe.wait_ge(s_waT, 1)

            def body(t, b, first, last):
                pe.wait_ge(s_xn, t + 1)
                if not first:
                    pe.wait_ge(s_xT, t)
                for c in range(KC):
                    pe.transpose(ps_t[b][:, c * 128:c * 128 + P], xn[:, b, c * 128:(c + 1) * 128], g["ident"][0:P, 0:P])
                for c in range(KC):
                    mm = pe.matmul(ps_g[c][:, 0:D + 1], xn[:, b, c * 128:(c + 1) * 128], xn[:, b, :], start=first, stop=last)
                mm.then_inc(s_tr, 1)
                pe.wait_ge(s_xT, t + 1)
                if not first:
                    pe.wait_ge(s_tab, t)
                for c in range(KC):
                    mm = pe.matmul(ps_h[b][0:P, 0:TAB + NH], xT[:, b, c, :], w72[:, c, :], start=c == 0, stop=c == 1)
                mm.then_inc(s_h, 1)
            over_tiles_summed(pe, body)

            pe.wait_ge(s_gram, 1)
            pe.wait_ge(s_wm, 160)
            for c in range(KC):
                mm = pe.transpose(bank[0][0:1, c * 128:(c + 1) * 128], gram[:, c, D:D + 1], g["ident"][:, :])
            mm.then_inc(s_fold_pe, 1)
            pe.wait_ge(s_gram, 2)
            for m in range(KC):
                for c in range(KC):
                    pe.matmul(bank[1 + m][:, 0:D], gram[:, c, m * 128:(m + 1) * 128], wkv[:, c, D:2 * D], start=c == 0, stop=False)
                mm = pe.matmul(bank[1 + m][:, 0:D], grow[:, m * 128:(m + 1) * 128], bkv[:, D:2 * D], start=False, stop=True)
            mm.then_inc(s_fold_pe, 1)
            for c in range(KC):
                pe.matmul(bank[7][0:1, 0:D], gram[:, c, D:D + 1], wkv[:, c, D:2 * D], start=c == 0, stop=False)
            pe.matmul(bank[7][0:1, 0:D], nn[:, :], bkv[:, D:2 * D], start=False, stop=True).then_inc(s_fold_pe, 1)
            pe.wait_ge(s_gram, 4)
            for m in range(KC):
                cols = slice(m * 128, (m + 1) * 128)
                for c in range(KC):
                    pe.matmul(bank[5][:, cols], wkv[:, c, cols], gwv[:, c, cols], start=c == 0, stop=False)
                mm = pe.matmul(bank[5][:, cols], bkv[:, cols], gwv_row[:, cols], start=False, stop=True)
            mm.then_inc(s_fold_pe, 1)
            pe.wait_ge(s_fold, 13)
            for c in range(KC):
                mm = pe.transpose(bank[0][:, c * 128:(c + 1) * 128], diag[:, c, :], g["ident"][:, :])
            mm.then_inc(s_fold_pe, 1)
            pe.wait_ge(s_gram, 5)
            for m in range(KC):
                for j in range(KC):
                    pe.matmul(bank[1 + m][:, j * 128:(j + 1) * 128], wqT[:, j, m * 128:(m + 1) * 128], attnT[:, j, :],
                              start=True, stop=True)
            for j in range(KC):
                mm = pe.matmul(bank[7][0:1, j * 128:(j + 1) * 128], bq[:, j:j + 1], attnT[:, j, :], start=True, stop=True)
            mm.then_inc(s_fold_pe, 1)
            pe.wait_ge(s_gram, 6)

            def attend(t, b):
                pe.wait_ge(s_b_xn, t + 1)
                for c in range(KC):
                    mm = pe.transpose(ps_t[b][:, c * 128:c * 128 + P], xn[:, b, c * 128:(c + 1) * 128], g["ident"][0:P, 0:P])
                mm.then_inc(s_b_tr, 1)
                pe.wait_ge(s_b_xT, t + 1)
                for c in range(KC):
                    pe.matmul(ps_h[b][0:P, 0:D], xT[:, b, c, :], c0[:, c, :], start=c == 0, stop=False)
                pe.matmul(ps_h[b][0:P, 0:D], g["ones"][0:1, 0:P], c0_row[:, :], start=False, stop=True).then_inc(s_b_mm, 1)
            over_tiles(pe, attend)

            def mlp(t, b):
                pe.wait_ge(s_m_xn, t + 1)
                for c in range(KC):
                    mm = pe.transpose(ps_t[b][:, c * 128:c * 128 + P], xn[:, b, c * 128:(c + 1) * 128], g["ident"][0:P, 0:P])
                mm.then_inc(s_m_tr, 1)
                pe.wait_ge(s_m_xT, t + 1)
                for m in range(MC):
                    hb = [bank[1], bank[2], bank[0], bank[7]][2 * b + m // 3]
                    for c in range(KC):
                        mm = pe.matmul(hb[:, m % 3 * P:m % 3 * P + P], fc1[:, c, m * 128:(m + 1) * 128], xT[:, b, c, :],
                                       start=c == 0, stop=c == 1)
                mm.then_inc(s_m_h, 1)
                pe.wait_ge(s_m_g, t + 1)
                for m in range(MC):
                    pe.matmul(ps_h[b][0:P, 0:D], gT[:, b, m, :], fc2[:, m, :], start=m == 0, stop=False)
                pe.matmul(ps_h[b][0:P, 0:D], g["ones"][0:1, 0:P], fb2[:, :], start=False, stop=True).then_inc(s_m_y, 1)
            over_tiles(pe, mlp)

        @block.scalar
        def _(act):
            act.wait_ge(s_var, 1)
            act.activation(g["rstd"][:, :], g["rstd"][:, :], ACT.Sqrt).then_inc(s_rstd, 1)

            def body(t, b):
                act.wait_ge(s_tr, t + 1)
                act.copy(xT[:, b, :, :], ps_t[b][:, 0:256].rearrange("p (c q) -> p c q", c=2)[:, :, 0:P]).then_inc(s_xT, 1)
                act.wait_ge(s_st[b], (t - b) * 8)
                act.wait_ge(s_h, t + 1)
                act.copy(tab[:, b, :], ps_h[b][0:P, 0:TAB + NH])
                act.copy(tile_of(g["el"], t), ps_h[b][0:P, TAB:TAB + NH]).then_inc(s_tab, 1)
                act.wait_ge(s_tab, t + 1)
                act.dma_start(table_rows[bass.ds(t, 1), :, :].rearrange("o p f -> (o p) f"), tab[:, b, 0:TAB]).then_inc(s_st[b], 16)
            over_tiles(act, body)
            act.wait_ge(s_tr, T)
            for c in range(KC):
                cp = act.copy(gram[:, c, :], ps_g[c][:, 0:D + 1])
            cp.then_inc(s_gram, 1)
            act.wait_ge(s_fold_pe, 1)
            act.copy(grow[:, :], bank[0][0:1, 0:D]).then_inc(s_gram, 1)
            act.wait_ge(s_fold_pe, 2)
            for m in range(KC):
                cp = act.copy(gwv[:, m, :], bank[1 + m][:, 0:D])
            cp.then_inc(s_gram, 1)
            act.wait_ge(s_fold_pe, 3)
            act.copy(gwv_row[:, :], bank[7][0:1, 0:D]).then_inc(s_gram, 1)
            act.wait_ge(s_fold, 6)
            act.activation(logit[:, :, :], logit[:, :, :], ACT.Exp, scale=HD ** -0.5).then_inc(s_fold, 1)
            act.wait_ge(s_fold_pe, 5)
            act.copy(attnT[:, :, :], bank[0][:, 0:D].rearrange("p (c q) -> p c q", c=2)).then_inc(s_gram, 1)
            act.wait_ge(s_fold_pe, 6)
            for m in range(KC):
                act.copy(c0[:, m, :], bank[1 + m][:, 0:D])
            act.copy(c0_row[:, :], bank[7][0:1, 0:D]).then_inc(s_gram, 1)

            def attend(t, b):
                act.wait_ge(s_b_tr, t + 1)
                act.copy(xT[:, b, :, :], ps_t[b][:, 0:256].rearrange("p (c q) -> p c q", c=2)[:, :, 0:P]).then_inc(s_b_xT, 1)
            over_tiles(act, attend)
            act.wait_ge(s_m_var, 1)
            act.activation(rstd1[:, :], rstd1[:, :], ACT.Sqrt).then_inc(s_m_rstd, 1)

            def mlp(t, b):
                act.wait_ge(s_m_tr, t + 1)
                for c in range(KC):
                    cp = act.activation(xT[:, b, c, :], ps_t[b][:, c * 128:c * 128 + P], ACT.Identity,
                                        bias=lnT[:, 1, c:c + 1], scale=lnT[:, 0, c:c + 1])
                cp.then_inc(s_m_xT, 1)
                act.wait_ge(s_m_h, t + 1)
                for m in range(MC):
                    hb = [bank[1], bank[2], bank[0], bank[7]][2 * b + m // 3]
                    cp = act.activation(gT[:, b, m, :], hb[:, m % 3 * P:m % 3 * P + P], ACT.Gelu, bias=fb1[:, m:m + 1])
                cp.then_inc(s_m_g, 1)
            over_tiles(act, mlp)
            act.wait_ge(s_st[0], (T + 1) // 2 * 16)
            act.wait_ge(s_st[1], T // 2 * 16)


def edge_aggregation(nc, a, g):
    bank = g["bank"]
    G = 4
    RING = 4
    NG = ET // G
    agg = g["agg"]
    slots = g["slots"].rearrange("(p t) f -> p t f", p=SLOT)
    with Stage(nc, "D") as st:
        node_id = st.sb("node_id", [128, T, P])
        pay = st.sb("pay", [128, RING, G, PAY])
        hg = st.sb("hg", [128, RING, G, TAB])
        hot = st.sb("hot", [128, 2, G, P])
        hotT = st.sb("hotT", [P, 2, G, 128])
        attr = st.sb("attr", [128, 2, G * AT])
        attrT = st.sb("attrT", [128, 2, 128])
        wt = st.sb("wt", [128, G, HD])
        bt = st.sb("bt", [1, G, HD])
        z = st.sb("z", [128, 2, G, NH])
        val = st.sb("val", [128, 2, G, VW])
        blank = st.sb("blank", [128, FT * D // 8])
        s_blank, s_blanked = st.sem("blank"), st.sem("blanked")
        s_w, s_zero, s_node = st.sem("weights"), st.sem("zero"), st.sem("node_id")
        s_pay = st.sems("pay", RING)
        s_hg = st.sems("hg", RING)
        s_go, s_attr = st.sem("go"), st.sem("attr")
        s_hot, s_hotT_ps, s_hotT, s_at_ps, s_at, s_time, s_relu, s_el, s_z0, s_z, s_w_exp, s_val, s_main, s_agg = (
            st.sem(n) for n in ("hot", "hotT_psum", "hotT", "attrT_psum", "attrT", "time", "relu", "el",
                                "z_sum", "z", "w_exp", "val", "summed", "agg"))
        block = st.block()

        @block.sync
        def _(sp):
            sp.wait_ge(s_zero, 1)
            for j in range(G):
                sp.dma_start(wt[AT * j:AT * j + AT, j, :], a["L1_gnn_W_time_T"]).then_inc(s_w, 16)
                sp.dma_start(bt[:, j, :], a["L1_gnn_b_time"].unsqueeze(0)).then_inc(s_w, 16)
            sp.wait_ge(s_blank, 1)
            for c in range(8):
                sp.dma_start(g["xs"].rearrange("(p t) f -> p (t f)", p=SLOT)[:, c * (FT * D // 8):(c + 1) * (FT * D // 8)],
                             blank[:, :]).then_inc(s_blanked, 16)
            with sp.Fori(0, NG // RING) as r:
                for b in range(RING):
                    q = r * RING + b
                    sp.wait_ge(s_val, q)
                    sp.dma_start(pay[:, b, :, :], slots[:, bass.ds(q * G, G), :]).then_inc(s_pay[b], 16)
            sp.wait_ge(s_blanked, 16 * 8)

        @block.gpsimd
        def _(gp):
            gp.memset(wt[:, :, :], 0.0).then_inc(s_zero, 1)
            gp.memset(blank[:, :], 0.0).then_inc(s_blank, 1)
            gp.iota(node_id[:, :, :], [[P, T], [1, P]], base=0, channel_multiplier=0,
                    allow_small_or_imprecise_dtypes=True).then_inc(s_node, 1)
            gp.memset(agg[:, :, :], 0.0).then_inc(s_node, 1)
            gp.memset(val[:, :, :, O_C:O_C + 1], 1.0).then_inc(s_node, 1)
            with gp.Fori(0, NG // RING) as r:
                for b in range(RING):
                    gp.wait_ge(s_val, r * RING + b)
                    gp.wait_ge(s_pay[b], r * 16 + 16)
                    gp.sem_inc(s_go, 1)
                    for j in range(G):
                        gp.indirect_dma_start(hg[:, b, j, :], None, g["table"],
                                              bass.IndirectOffsetOnAxis(ap=pay[:, b, j, AT + 1:PAY].bitcast(I32), axis=0)
                                              ).then_inc(s_hg[b], 16)

        @block.vector
        def _(v):
            v.sem_inc(s_val, RING - 1)
            v.sem_inc(s_agg, G)
            v.wait_ge(s_node, 3)

            def make_hot(q, r, b):
                v.wait_ge(s_pay[b], r * 16 + 16)
                for j in range(G):
                    w = v.value_load(g["edge_map"][0:1, bass.ds(q * G + j, 1)], min_val=0, max_val=T - 1)
                    o = v.tensor_scalar(hot[:, b % 2, j, :], tile_of(node_id, w), pay[:, b, j, AT:AT + 1], None,
                                        ALU.is_equal)
                o.then_inc(s_hot, 1)

            def add(q):
                for j in range(G):
                    w = v.value_load(g["edge_map"][0:1, bass.ds(q * G + j, 1)], min_val=0, max_val=T - 1)
                    v.wait_ge(s_main, q * G + j + 1)
                    v.wait_ge(s_agg, q * G + j + G)
                    v.tensor_tensor(tile_of(agg, w), tile_of(agg, w), bank[4 + j][0:P, 0:VW], ALU.add).then_inc(s_agg, 1)

            def group(q, r, b, first):
                p = b % 2
                make_hot(q, r, b)
                if not first:
                    add(q - 1)
                v.wait_ge(s_hg[b], r * (16 * G) + 16 * G)
                v.wait_ge(s_el, q + 1)
                v.tensor_tensor(z[:, p, :, :], bank[3][:, 0:G * NH].rearrange("p (j h) -> p j h", j=G),
                                hg[:, b, :, HD:TAB], ALU.add).then_inc(s_z0, 1)
                v.wait_ge(s_z0, q + 1)
                v.scalar_tensor_tensor(out=z[:, p, :, :], in0=z[:, p, :, :], scalar=0.2, in1=z[:, p, :, :],
                                       op0=ALU.mult, op1=ALU.max).then_inc(s_z, 1)
                v.wait_ge(s_w_exp, q + 1)
                v.tensor_tensor(val[:, p, :, 0:O_W].rearrange("p j (h f) -> p j h f", h=NH),
                                hg[:, b, :, 0:HD].unsqueeze(2).broadcast_to([128, G, NH, HD]),
                                val[:, p, :, O_W:O_T].unsqueeze(3).broadcast_to([128, G, NH, HD]),
                                ALU.mult).then_inc(s_val, 1)
            for b in range(RING):
                group(b, 0, b, b == 0)
            with v.Fori(1, NG // RING) as r:
                for b in range(RING):
                    group(r * RING + b, r, b, False)
            add(NG - 1)

        @block.tensor
        def _(pe):
            pe.wait_ge(s_w, 32 * G)

            def sum_slots(q, p):
                pe.wait_ge(s_val, q + RING)
                pe.wait_ge(s_relu, q + 1)
                pe.wait_ge(s_agg, q * G + G)
                for j in range(G):
                    pe.matmul(bank[4 + j][0:P, 0:VW], hot[:, p, j, :], val[:, p, j, :], start=True, stop=True).then_inc(s_main, 1)

            def group(q, r, b, first):
                p = b % 2
                pe.wait_ge(s_hotT, q)
                pe.wait_ge(s_hot, q + 1)
                for j in range(G):
                    mm = pe.transpose(bank[0][0:P, j * 128:(j + 1) * 128], hot[:, p, j, :], g["ident"][:, :])
                mm.then_inc(s_hotT_ps, 1)
                pe.wait_ge(s_at, q)
                pe.wait_ge(s_attr, q + 1)
                pe.transpose(bank[1][:, 0:128], attr[:, p, :], g["ident"][:, :]).then_inc(s_at_ps, 1)
                if not first:
                    sum_slots(q - 1, (b + 1) % 2)
                pe.wait_ge(s_relu, q)
                pe.wait_ge(s_at, q + 1)
                pe.matmul(bank[2][:, 0:G * HD], g["ones"][0:1, :], bt[:, :, :].rearrange("p j f -> p (j f)"), start=True, stop=False)
                pe.matmul(bank[2][:, 0:G * HD], attrT[:, p, :], wt[:, :, :].rearrange("p j f -> p (j f)"),
                          start=False, stop=True).then_inc(s_time, 1)
                pe.wait_ge(s_z0, q)
                pe.wait_ge(s_hotT, q + 1)
                for j in range(G):
                    w = pe.value_load(g["edge_map"][0:1, bass.ds(q * G + j, 1)], min_val=0, max_val=T - 1)
                    mm = pe.matmul(bank[3][:, j * NH:(j + 1) * NH], hotT[:, p, j, :], tile_of(g["el"], w), start=True, stop=True)
                mm.then_inc(s_el, 1)
            for b in range(RING):
                group(b, 0, b, b == 0)
            with pe.Fori(1, NG // RING) as r:
                for b in range(RING):
                    group(r * RING + b, r, b, False)
            sum_slots(NG - 1, 1)

        @block.scalar
        def _(act):
            act.wait_ge(s_node, 3)

            def group(q, r, b):
                p = b % 2
                act.wait_ge(s_pay[b], r * 16 + 16)
                act.copy(attr[:, p, :].rearrange("p (j f) -> p j f", j=G), pay[:, b, :, 0:AT]).then_inc(s_attr, 1)
                act.wait_ge(s_hotT_ps, q + 1)
                act.copy(hotT[:, p, :, :], bank[0][0:P, :].rearrange("p (j s) -> p j s", j=G)).then_inc(s_hotT, 1)
                act.wait_ge(s_at_ps, q + 1)
                act.copy(attrT[:, p, :], bank[1][:, 0:128]).then_inc(s_at, 1)
                act.wait_ge(s_time, q + 1)
                act.activation(val[:, p, :, O_T:O_C], bank[2][:, 0:G * HD].rearrange("p (j f) -> p j f", j=G),
                               ACT.Relu).then_inc(s_relu, 1)
                act.wait_ge(s_z, q + 1)
                act.activation(val[:, p, :, O_W:O_T], z[:, p, :, :], ACT.Exp).then_inc(s_w_exp, 1)
            with act.Fori(0, NG // RING) as r:
                for b in range(RING):
                    group(r * RING + b, r, b)


def gat_finish(nc, a, g):
    CH = 5
    agg, x = g["agg"], g["x"]
    with Stage(nc, "F") as st:
        den = st.sb("den", [P, T, NH])
        bias = st.sb("bias", [P, HD])
        low = st.sb("low", [P, T, NH * HD])
        s_b, s_den, s_o, s_low, s_exp, s_x = (st.sem(n) for n in ("bias", "den", "o", "low", "exp", "x"))
        block = st.block()

        @block.sync
        def _(sp):
            sp.dma_start(bias[:, :], a["L0_gnn_b"].unsqueeze(0).broadcast_to([P, HD])).then_inc(s_b, 16)

        @block.vector
        def _(v):
            v.tensor_copy(g["time"][:, :, :], agg[:, :, O_T:VW])
            v.tensor_scalar(den[:, :, :], agg[:, :, O_W:O_T], 1e-12, None, ALU.max).then_inc(s_den, 1)
            v.wait_ge(s_den, 1)
            v.reciprocal(den[:, :, :], den[:, :, :]).then_inc(s_den, 1)
            v.wait_ge(s_den, 2)
            v.wait_ge(s_b, 16)
            for c in range(T // CH):
                t = slice(c * CH, (c + 1) * CH)
                o = agg[:, t, 0:O_W].rearrange("p t (h f) -> p t h f", h=NH)
                v.tensor_tensor(o, o, den[:, t, :].unsqueeze(3).broadcast_to([P, CH, NH, HD]), ALU.mult).then_inc(s_o, 1)
                v.wait_ge(s_o, c * 2 + 1)
                v.tensor_tensor(o, o, bias[:, :].unsqueeze(1).unsqueeze(1).broadcast_to([P, CH, NH, HD]), ALU.add).then_inc(s_o, 1)
                v.wait_ge(s_o, c * 2 + 2)
                v.tensor_scalar(low[:, t, :], agg[:, t, 0:O_W], 0.0, None, ALU.min).then_inc(s_low, 1)
            for c in range(T // CH):
                t = slice(c * CH, (c + 1) * CH)
                v.wait_ge(s_exp, c + 1)
                v.scalar_tensor_tensor(out=low[:, t, :], in0=agg[:, t, 0:O_W], scalar=0.0, in1=low[:, t, :],
                                       op0=ALU.max, op1=ALU.add).then_inc(s_x, 1)
                v.wait_ge(s_x, c * 2 + 1)
                v.scalar_tensor_tensor(out=x[:, t, :], in0=low[:, t, :], scalar=-1.0, in1=x[:, t, :],
                                       op0=ALU.add, op1=ALU.add).then_inc(s_x, 1)

        @block.scalar
        def _(act):
            for c in range(T // CH):
                t = slice(c * CH, (c + 1) * CH)
                act.wait_ge(s_low, c + 1)
                act.activation(low[:, t, :], low[:, t, :], ACT.Exp).then_inc(s_exp, 1)


def moe(nc, a, g, layer, out=None):
    with Stage(nc, f"M{layer}") as keep:
        if layer == 0:
            w_in = keep.sb("w1", [128, NE, KC, H0])
            w_out = keep.sb("w2", [128, NE, H0 // 128, D])
        else:
            w_in = keep.sb("w13", [128, NE, KC, 2 * H1])
            w_out = keep.sb("w2", [128, NE, H1C, D])
        slot = keep.sb("slot", [P, T, TOPK], I32)
        prob = keep.sb("prob", [P, T, TOPK])
        tile_map = keep.sb("tile_map", [1, FT], I32)
        route(nc, a, g, layer, slot, prob, tile_map)
        experts(nc, a, g, layer, w_in, w_out, tile_map)
        combine(nc, g, slot, prob, out)


def route(nc, a, g, layer, slot, prob, tile_map):
    bank, x = g["bank"], g["x"]
    with Stage(nc, f"R{layer}") as st:
        stats = st.sb("stats", [P, T, 6])
        xn = st.sb("xn", [P, 2, D])
        xT = st.sb("xT", [128, 2, KC, P])
        wg = st.sb("wg", [128, KC, NE])
        bg = st.sb("bg", [1, NE])
        score = st.sb("score", [P, T, NE])
        best = st.sb("best", [P, T, NE])
        rest = st.sb("rest", [P, T, NE])
        top = st.sb("top", [P, T, TOPK])
        expert = st.sb("expert", [P, T, TOPK])
        psum_p = st.sb("psum_p", [P, T])
        k = bins_buffers(st, NE, T * TOPK)
        narrow = st.sb("narrow", [1, FT])
        wide = st.sb("wide", [1, FT, NE - 1])
        xr = st.sb("xr", [P, 4, D])
        ids = st.sb("ids", [P, 4, TOPK], I32)
        s_w = st.sem("weights")
        s_ln, s_var, s_rstd, s_xn, s_tr, s_xT, s_sc, s_sb, s_top, s_p, s_exp, s_ready, s_row, s_go = (
            st.sem(n) for n in ("ln", "var", "rstd", "xn", "transposed", "xT", "scored", "score_sb", "top", "prob",
                                "exp", "ready", "row", "go"))
        s_sent = st.sems("sent", 4)
        block = st.block()

        @block.sync
        def _(sp):
            if layer == 0:
                sp.dma_start(wg[:, :, :], a["L0_ffn_Wg_T"].rearrange("(k p) f -> p k f", p=128)).then_inc(s_w, 16)
                sp.dma_start(bg[:, :], a["L0_ffn_bg"].unsqueeze(0)).then_inc(s_w, 16)
            else:
                sp.dma_start(wg[:, :, :], a["L1_ffn_router_w_T"].rearrange("(k p) f -> p k f", p=128)).then_inc(s_w, 16)

        @block.gpsimd
        def _(gp):
            def send(t, b):
                gp.wait_ge(s_row, t + 1)
                gp.sem_inc(s_go, 1)
                for c in range(TOPK):
                    gp.indirect_dma_start(g["xs"], bass.IndirectOffsetOnAxis(ap=ids[:, b, c:c + 1], axis=0),
                                          xr[:, b, :], None).then_inc(s_sent[b], 16)
            with gp.Fori(0, T // 4) as r:
                for b in range(4):
                    send(r * 4 + b, b)
            send(T - 1, 0)
            for b in range(4):
                gp.wait_ge(s_sent[b], (T // 4 + (b == 0)) * 16 * TOPK)

        @block.vector
        def _(v):
            layer_stats(v, x, stats, g["mv"], g["rstd"], s_ln, s_var)
            v.wait_ge(s_rstd, 1)

            def score_tile(t, b):
                v.wait_ge(s_tr, t)
                v.tensor_scalar(xn[:, b, :], tile_of(x, t), tile_of(g["mv"], t)[:, 0:1], g["rstd"][:, bass.ds(t, 1)],
                                ALU.subtract, ALU.mult).then_inc(s_xn, 1)
                v.wait_ge(s_sc, t + 1)
                v.tensor_copy(tile_of(score, t), bank[2 + b][0:P, 0:NE]).then_inc(s_sb, 1)
            over_tiles(v, score_tile)

            v.wait_ge(s_sb, T)
            number = g["bin_no"][0:P, 0:NE].unsqueeze(1).broadcast_to([P, T, NE])
            for c in range(TOPK):
                from_ = score if c == 0 else rest
                n = c * 7
                v.tensor_reduce(top[:, :, c], from_[:, :, :], AXX, ALU.max).then_inc(s_top, 1)
                v.wait_ge(s_top, n + 1)
                v.tensor_tensor(best[:, :, :], from_[:, :, :], top[:, :, c].unsqueeze(2).broadcast_to([P, T, NE]),
                                ALU.is_equal).then_inc(s_top, 1)
                v.wait_ge(s_top, n + 2)
                v.scalar_tensor_tensor(out=best[:, :, :], in0=best[:, :, :], scalar=-float(2 * NE), in1=number,
                                       op0=ALU.mult, op1=ALU.add).then_inc(s_top, 1)
                v.wait_ge(s_top, n + 3)
                v.tensor_reduce(expert[:, :, c], best[:, :, :], AXX, ALU.min).then_inc(s_top, 1)
                v.wait_ge(s_top, n + 4)
                v.tensor_scalar(expert[:, :, c], expert[:, :, c], float(2 * NE), None, ALU.add).then_inc(s_top, 1)
                v.wait_ge(s_top, n + 5)
                if c == 0:
                    v.tensor_tensor(best[:, :, :], number, expert[:, :, c].unsqueeze(2).broadcast_to([P, T, NE]),
                                    ALU.is_equal).then_inc(s_top, 1)
                    v.wait_ge(s_top, n + 6)
                    v.scalar_tensor_tensor(out=rest[:, :, :], in0=best[:, :, :], scalar=-3e38, in1=score[:, :, :],
                                           op0=ALU.mult, op1=ALU.add).then_inc(s_top, 1)
                    v.wait_ge(s_top, n + 7)
            if layer == 1:
                v.tensor_tensor(score[:, :, :], score[:, :, :], top[:, :, 0].unsqueeze(2).broadcast_to([P, T, NE]),
                                ALU.subtract).then_inc(s_p, 1)
            v.tensor_tensor(prob[:, :, :], top[:, :, :], top[:, :, 0].unsqueeze(2).broadcast_to([P, T, TOPK]),
                            ALU.subtract).then_inc(s_p, 1)
            n = 1 + layer
            v.wait_ge(s_exp, n)
            if layer == 1:
                v.tensor_reduce(psum_p[:, :], score[:, :, :], AXX, ALU.add).then_inc(s_p, 1)
                v.wait_ge(s_p, n + 1)
                v.reciprocal(psum_p[:, :], psum_p[:, :]).then_inc(s_p, 1)
                v.wait_ge(s_p, n + 2)
                v.tensor_tensor(prob[:, :, :], prob[:, :, :], psum_p[:, :].unsqueeze(2).broadcast_to([P, T, TOPK]),
                                ALU.mult).then_inc(s_p, 1)
                n += 3
                v.wait_ge(s_p, n)
            v.tensor_tensor(psum_p[:, :], prob[:, :, 0], prob[:, :, 1], ALU.add).then_inc(s_p, 1)
            v.wait_ge(s_p, n + 1)
            if layer == 1:
                v.tensor_scalar(psum_p[:, :], psum_p[:, :], 1e-9, None, ALU.add).then_inc(s_p, 1)
                n += 1
                v.wait_ge(s_p, n + 1)
            v.reciprocal(psum_p[:, :], psum_p[:, :]).then_inc(s_p, 1)
            v.wait_ge(s_p, n + 2)
            v.tensor_tensor(prob[:, :, :], prob[:, :, :], psum_p[:, :].unsqueeze(2).broadcast_to([P, T, TOPK]),
                            ALU.mult).then_inc(s_p, 1)
            bins_vector(v, k, expert[:, :, :].rearrange("p t k -> p (t k)"), g["bin_no"], g["ones"], NE, T * TOPK,
                        bank[0], None, tile_map[:, :], FT, g["tile_at"], narrow[:, :], wide[:, :, :], s_ready)
            v.tensor_copy(slot[:, :, :].rearrange("p t k -> p (t k)"), k["posf"][:, :]).then_inc(s_p, 1)
            v.wait_ge(s_p, n + 4)

            def rows(t, b, r):
                v.wait_ge(s_sent[b], r * (16 * TOPK))
                v.tensor_copy(ids[:, b, :], tile_of(slot, t))
                v.tensor_scalar(xr[:, b, :], tile_of(x, t), tile_of(g["mv"], t)[:, 0:1], g["rstd"][:, bass.ds(t, 1)],
                                ALU.subtract, ALU.mult).then_inc(s_row, 1)
            with v.Fori(0, T // 4) as r:
                for b in range(4):
                    rows(r * 4 + b, b, r)
            rows(T - 1, 0, T // 4)

        @block.tensor
        def _(pe):
            pe.wait_ge(s_w, 32 - 16 * layer)

            def score_tile(t, b):
                pe.wait_ge(s_xT, t)
                pe.wait_ge(s_xn, t + 1)
                for c in range(KC):
                    mm = pe.transpose(bank[4 + b][:, c * 128:c * 128 + P], xn[:, b, c * 128:(c + 1) * 128], g["ident"][0:P, 0:P])
                mm.then_inc(s_tr, 1)
                pe.wait_ge(s_sb, t)
                pe.wait_ge(s_xT, t + 1)
                for c in range(KC):
                    mm = pe.matmul(bank[2 + b][0:P, 0:NE], xT[:, b, c, :], wg[:, c, :], start=c == 0,
                                   stop=c == 1 and layer == 1)
                if layer == 0:
                    mm = pe.matmul(bank[2 + b][0:P, 0:NE], g["ones"][0:1, 0:P], bg[:, :], start=False, stop=True)
                mm.then_inc(s_sc, 1)
            over_tiles(pe, score_tile)
            bins_tensor(pe, k, g["before"], g["ones"], NE, bank[0])

        @block.scalar
        def _(act):
            act.wait_ge(s_var, 1)
            act.activation(g["rstd"][:, :], g["rstd"][:, :], ACT.Sqrt).then_inc(s_rstd, 1)

            def score_tile(t, b):
                act.wait_ge(s_tr, t + 1)
                act.copy(xT[:, b, :, :], bank[4 + b][:, 0:256].rearrange("p (c q) -> p c q", c=2)[:, :, 0:P]).then_inc(s_xT, 1)
            over_tiles(act, score_tile)
            act.wait_ge(s_p, 1 + layer)
            if layer == 1:
                act.activation(score[:, :, :], score[:, :, :], ACT.Exp).then_inc(s_exp, 1)
            act.activation(prob[:, :, :], prob[:, :, :], ACT.Exp).then_inc(s_exp, 1)


def experts(nc, a, g, layer, w_in, w_out, tile_map):
    bank = g["bank"]
    HB = [bank[0], bank[1]] if layer == 0 else [bank[0], bank[1], bank[2], bank[3]]
    HC = H0 // 128 if layer == 0 else H1C
    tb, yb = ([bank[4], bank[5]], bank[6])
    xb = bank[7]
    xs = g["xs"].rearrange("(t p) f -> t p f", p=SLOT)
    ys = g["ys"].rearrange("(t p) f -> t p f", p=SLOT)
    HW = H0 if layer == 0 else H1
    chunks = [(c * 128, min(128, HW - c * 128)) for c in range(HC)]
    with Stage(nc, f"E{layer}") as st:
        xt = st.sb("xt", [SLOT, 2, D])
        xT = st.sb("xT", [128, 2, KC, SLOT])
        h = st.sb("h", [SLOT, HW])
        hT = st.sb("hT", [128, 2, HC, SLOT])
        y = st.sb("y", [SLOT, 2, D])
        if layer == 0:
            b1 = st.sb("b1", [128, NE, HC])
            b2 = st.sb("b2", [SLOT, NE, D])
        s_w = st.sem("weights")
        s_x, s_st = st.sems("x"), st.sems("stored")
        s_tr, s_xT, s_h, s_hs, s_hd, s_hTp, s_hT, s_y, s_ys = (st.sem(n) for n in (
            "x_transposed", "xT", "h", "h_gate", "h_sb", "h_transposed", "hT", "y", "y_sb"))
        block = st.block()

        @block.sync
        def _(sp):
            for e in range(NE):
                if layer == 0:
                    sp.dma_start(w_in[:, e, :, :], a["L0_ffn_W1_T"][e].rearrange("(k p) f -> p k f", p=128)).then_inc(s_w, 16)
                    sp.dma_start(w_out[:, e, :, :], a["L0_ffn_W2_T"][e].rearrange("(k p) f -> p k f", p=128)).then_inc(s_w, 16)
                else:
                    sp.dma_start(w_in[:, e, :, 0:H1], a["L1_ffn_w1_T"][e].rearrange("(k p) f -> p k f", p=128)).then_inc(s_w, 16)
                    sp.dma_start(w_in[:, e, :, H1:2 * H1], a["L1_ffn_w3_T"][e].rearrange("(k p) f -> p k f", p=128)).then_inc(s_w, 16)
                    sp.dma_start(w_out[:, e, 0:HC - 1, :], a["L1_ffn_w2_T"][e, 0:(HC - 1) * 128].rearrange(
                        "(k p) f -> p k f", p=128)).then_inc(s_w, 16)
                    sp.dma_start(w_out[0:H1 - (HC - 1) * 128, e, HC - 1, :], a["L1_ffn_w2_T"][e, (HC - 1) * 128:H1]).then_inc(s_w, 16)
            if layer == 0:
                sp.dma_start(b1[:, :, :].rearrange("p e c -> p (e c)"), a["L0_ffn_b1_cols"]).then_inc(s_w, 16)
                sp.dma_start(b2[:, :, :], a["L0_ffn_b2"].unsqueeze(0).broadcast_to([SLOT, NE, D])).then_inc(s_w, 16)

            def load(t, b):
                sp.wait_ge(s_tr, t)
                sp.dma_start(xt[:, b, :], xs[bass.ds(t, 1), :, :].rearrange("o p f -> (o p) f")).then_inc(s_x[b], 16)
            sp.dma_start(xt[:, 0, :], xs[0]).then_inc(s_x[0], 16)
            with sp.Fori(0, FT // 2 - 1) as j:
                load(j * 2 + 1, 1)
                load(j * 2 + 2, 0)
            load(FT - 1, 1)

        @block.tensor
        def _(pe):
            pe.wait_ge(s_w, 16 * (NE * 2 + 2 if layer == 0 else NE * 4))

            def turn(j, b):
                pe.wait_ge(s_x[b], j * 16 + 16)
                for c in range(KC):
                    mm = pe.transpose(xb[:, c * 128:(c + 1) * 128], xt[:, b, c * 128:(c + 1) * 128], g["ident"][:, :])
                mm.then_inc(s_tr, 1)

            def tile(t, j, b, last):
                e = pe.value_load(tile_map[0:1, bass.ds(t, 1)], min_val=0, max_val=NE - 1)
                pe.wait_ge(s_xT, t + 1)
                pe.wait_ge(s_hd, t)
                for n, hb in enumerate(HB):
                    if layer == 0:
                        c0, w = n * 512, 512
                    else:
                        c0, w = n // 2 * H1 + n % 2 * (H1 // 2), H1 // 2
                    for c in range(KC):
                        mm = pe.matmul(hb[:, 0:w], xT[:, b, c, :], w_in[:, bass.ds(e, 1), c, c0:c0 + w].rearrange("p o f -> p (o f)"),
                                       start=c == 0, stop=c == 1)
                mm.then_inc(s_h, 1)
                if not last:
                    turn(j + b, 1 - b)
                pe.wait_ge(s_hd, t + 1)
                pe.wait_ge(s_hT, t)
                for n, (c0, w) in enumerate(chunks):
                    mm = pe.transpose(tb[n // 4][0:w, n % 4 * 128:n % 4 * 128 + SLOT], h[:, c0:c0 + w], g["ident"][:, :])
                mm.then_inc(s_hTp, 1)
                pe.wait_ge(s_ys, t)
                pe.wait_ge(s_hT, t + 1)
                for n, (c0, w) in enumerate(chunks):
                    mm = pe.matmul(yb[:, 0:D], hT[0:w, b, n, :], w_out[0:w, bass.ds(e, 1), n, :].rearrange("p o f -> p (o f)"),
                                   start=n == 0, stop=n == HC - 1)
                mm.then_inc(s_y, 1)
            turn(0, 0)
            with pe.Fori(0, FT // 2 - 1) as j:
                tile(j * 2, j, 0, False)
                tile(j * 2 + 1, j, 1, False)
            tile(FT - 2, FT // 2 - 1, 0, False)
            tile(FT - 1, FT // 2 - 1, 1, True)

        @block.vector
        def _(v):
            def tile(t, j, b):
                if layer == 0:
                    e = v.value_load(tile_map[0:1, bass.ds(t, 1)], min_val=0, max_val=NE - 1)
                v.wait_ge(s_hTp, t)
                if layer == 0:
                    v.wait_ge(s_h, t + 1)
                    for n, hb in enumerate(HB):
                        o = v.tensor_copy(h[:, n * 512:(n + 1) * 512], hb[:, :])
                else:
                    v.wait_ge(s_hs, t + 1)
                    for n in range(2):
                        o = v.tensor_tensor(h[:, n * (H1 // 2):(n + 1) * (H1 // 2)], h[:, n * (H1 // 2):(n + 1) * (H1 // 2)],
                                            HB[2 + n][:, 0:H1 // 2], ALU.mult)
                o.then_inc(s_hd, 1)
                v.wait_ge(s_st[b], j * 16)
                v.wait_ge(s_y, t + 1)
                if layer == 0:
                    v.tensor_tensor(y[:, b, :], yb[:, 0:D], tile_of(b2, e), ALU.add).then_inc(s_ys, 1)
                else:
                    v.tensor_copy(y[:, b, :], yb[:, 0:D]).then_inc(s_ys, 1)
            with v.Fori(0, FT // 2) as j:
                tile(j * 2, j, 0)
                tile(j * 2 + 1, j, 1)

        @block.scalar
        def _(act):
            def tile(t, b):
                act.wait_ge(s_tr, t + 1)
                act.copy(xT[:, b, :, :], xb[:, 0:D].rearrange("p (c q) -> p c q", c=2)).then_inc(s_xT, 1)
                if layer == 1:
                    act.wait_ge(s_hTp, t)
                    act.wait_ge(s_h, t + 1)
                    for n in range(2):
                        o = act.activation(h[:, n * (H1 // 2):(n + 1) * (H1 // 2)], HB[n][:, 0:H1 // 2], ACT.Silu)
                    o.then_inc(s_hs, 1)
                if layer == 0:
                    e = act.value_load(tile_map[0:1, bass.ds(t, 1)], min_val=0, max_val=NE - 1)
                act.wait_ge(s_hTp, t + 1)
                if layer == 0:
                    for n in range(HC):
                        o = act.activation(hT[:, b, n, :], tb[n // 4][:, n % 4 * 128:(n % 4 + 1) * 128], ACT.Relu,
                                           bias=tile_of(b1, e)[:, n:n + 1])
                else:
                    w = H1 - (HC - 1) * 128
                    act.copy(hT[:, b, 0:4, :], tb[0][:, :].rearrange("p (c q) -> p c q", c=4))
                    act.copy(hT[:, b, 4, :], tb[1][:, 0:128])
                    o = act.copy(hT[0:w, b, 5, :], tb[1][0:w, 128:256])
                o.then_inc(s_hT, 1)
            def store(t, b):
                act.wait_ge(s_ys, t + 1)
                act.dma_start(ys[bass.ds(t, 1), :, :].rearrange("o p f -> (o p) f"), y[:, b, :]).then_inc(s_st[b], 16)
            with act.Fori(0, FT // 2) as j:
                tile(j * 2, 0)
                store(j * 2, 0)
                tile(j * 2 + 1, 1)
                store(j * 2 + 1, 1)
            act.wait_ge(s_st[0], FT // 2 * 16)
            act.wait_ge(s_st[1], FT // 2 * 16)


def combine(nc, g, slot, prob, out):
    x = g["x"]
    R = 4
    with Stage(nc, "C" + ("o" if out is not None else "x")) as st:
        yg = st.sb("yg", [P, R, TOPK, D])
        ids = st.sb("ids", [P, R, TOPK], I32)
        s_y = st.sems("y", R)
        s_x0, s_x, s_ids, s_go, s_out = st.sem("x0"), st.sem("x"), st.sem("ids"), st.sem("go"), st.sem("out")
        block = st.block()

        @block.gpsimd
        def _(gp):
            def fetch(t, b):
                gp.wait_ge(s_x, t)
                gp.tensor_copy(ids[:, b, :], tile_of(slot, t)).then_inc(s_ids, 1)
                gp.wait_ge(s_ids, t + 1)
                gp.sem_inc(s_go, 1)
                for c in range(TOPK):
                    gp.indirect_dma_start(yg[:, b, c, :], None, g["ys"],
                                          bass.IndirectOffsetOnAxis(ap=ids[:, b, c:c + 1], axis=0)).then_inc(s_y[b], 16)
            with gp.Fori(0, T // R) as r:
                for b in range(R):
                    fetch(r * R + b, b)
            fetch(T - 1, 0)

        @block.vector
        def _(v):
            v.sem_inc(s_x, R - 1)

            def add(t, r, b):
                v.wait_ge(s_y[b], r * (16 * TOPK) + 16 * TOPK)
                v.scalar_tensor_tensor(out=tile_of(x, t), in0=yg[:, b, 0, :], scalar=tile_of(prob, t)[:, 0:1],
                                       in1=tile_of(x, t), op0=ALU.mult, op1=ALU.add).then_inc(s_x0, 1)
                v.wait_ge(s_x0, t + 1)
                v.scalar_tensor_tensor(out=tile_of(x, t), in0=yg[:, b, 1, :], scalar=tile_of(prob, t)[:, 1:2],
                                       in1=tile_of(x, t), op0=ALU.mult, op1=ALU.add).then_inc(s_x, 1)
            with v.Fori(0, T // R) as r:
                for b in range(R):
                    add(r * R + b, r, b)
            add(T - 1, T // R, 0)

        if out is not None:
            rows = out.rearrange("(t p) f -> t p f", p=P)

            @block.sync
            def _(sp):
                with sp.Fori(0, T) as t:
                    sp.wait_ge(s_x, t + R)
                    sp.dma_start(rows[bass.ds(t, 1), :, :].rearrange("o p f -> (o p) f"), tile_of(x, t)).then_inc(s_out, 16)
                sp.wait_ge(s_out, T * 16)


L1H = 8
KV = L1H * HD


def l1_keys_values(nc, a, g):
    bank, x = g["bank"], g["x"]
    with Stage(nc, "K") as st:
        wkv = st.sb("wkv", [128, KC, 2 * KV])
        mean = st.sb("mean", [128, KC, 2 * L1H])
        wq = st.sb("wq", [128, KV // 128, D])
        wo = st.sb("wo", [128, KV // 128, D])
        xn = st.sb("xn", [P, 2, D])
        xT = st.sb("xT", [128, 2, KC, P])
        sq = st.sb("sq", [P, 2 * KV])
        var = st.sb("var", [P, 2, 2 * L1H])
        kvn = st.sb("kvn", [P, 2, 2 * KV])
        stats = st.sb("stats", [P, T, 6])
        dots = st.sb("dots", [128, KV // 128, 128])
        gm = st.sb("gm", [128, KV // 128, D])
        s_w, s_cw, s_zero = st.sem("weights"), st.sem("centred"), st.sem("zero")
        s_ln, s_var, s_rstd, s_xn, s_tr, s_xT, s_kv, s_sq, s_v1, s_root, s_r1, s_kvn, s_dot, s_dsb, s_g, s_gsb, s_c = (
            st.sem(n) for n in ("ln", "var", "rstd", "xn", "transposed", "xT", "kv", "squares", "kv_var", "kv_root",
                                "kv_rstd", "kv_normed", "dots", "dots_sb", "gm_psum", "gm", "c1"))
        block = st.block()

        @block.sync
        def _(sp):
            sp.dma_start(wkv[:, :, :], a["L1_mix_w_kv_T"].rearrange("(k p) f -> p k f", p=128)).then_inc(s_w, 16)
            sp.dma_start(wq[:, :, :], a["L1_mix_w_qkv"][0:KV].rearrange("(k p) f -> p k f", p=128)).then_inc(s_w, 16)
            sp.dma_start(wo[:, :, :], a["L1_mix_w_out_T"].rearrange("(k p) f -> p k f", p=128)).then_inc(s_w, 16)

        @block.gpsimd
        def _(gp):
            gp.memset(dots[:, :, :], 0.0).then_inc(s_zero, 1)

        @block.vector
        def _(v):
            layer_stats(v, x, stats, g["mv"], g["rstd"], s_ln, s_var)
            v.wait_ge(s_w, 48)
            heads = wkv[:, :, :].rearrange("p k (h f) -> p (k h) f", f=HD)
            m = mean[:, :, :].rearrange("p k h -> p (k h)")
            v.tensor_reduce(m, heads, AXX, ALU.add).then_inc(s_cw, 1)
            v.wait_ge(s_cw, 1)
            v.tensor_scalar(m, m, 1.0 / HD, None, ALU.mult).then_inc(s_cw, 1)
            v.wait_ge(s_cw, 2)
            v.tensor_tensor(heads, heads, m.unsqueeze(2).broadcast_to([128, KC * 2 * L1H, HD]), ALU.subtract).then_inc(s_cw, 1)
            v.wait_ge(s_rstd, 1)

            def normalise(t, b):
                v.wait_ge(s_tr, t)
                v.tensor_scalar(xn[:, b, :], tile_of(x, t), tile_of(g["mv"], t)[:, 0:1], g["rstd"][:, bass.ds(t, 1)],
                                ALU.subtract, ALU.mult).then_inc(s_xn, 1)

            def tile(t, b, first, last):
                if not last:
                    normalise(t + 1, 1 - b)
                v.wait_ge(s_sq, t + 1)
                v.tensor_reduce(var[:, b, :], sq[:, :].rearrange("p (h f) -> p h f", f=HD), AXX, ALU.add).then_inc(s_v1, 1)
                v.wait_ge(s_v1, t * 2 + 1)
                v.tensor_scalar(var[:, b, :], var[:, b, :], 1.0 / HD, EPS, ALU.mult, ALU.add).then_inc(s_v1, 1)
                v.wait_ge(s_v1, t * 2 + 2)
                v.reciprocal(var[:, b, :], var[:, b, :]).then_inc(s_root, 1)
                v.wait_ge(s_r1, t + 1)
                if not first:
                    v.wait_ge(s_dot, t - 1)
                for n in range(2):
                    o = v.tensor_tensor(kvn[:, b, n * KV:(n + 1) * KV].rearrange("p (h f) -> p h f", f=HD),
                                        bank[2 * n + b][0:P, :].rearrange("p (h f) -> p h f", f=HD),
                                        var[:, b, n * L1H:(n + 1) * L1H].unsqueeze(2).broadcast_to([P, L1H, HD]), ALU.mult)
                o.then_inc(s_kvn, 1)
            normalise(0, 0)
            over_tiles_summed(v, tile)
            v.wait_ge(s_dot, T)
            v.wait_ge(s_zero, 1)
            for h in range(L1H):
                r = slice(h % 2 * HD, h % 2 * HD + HD)
                o = v.tensor_copy(dots[r, h // 2, r], bank[5][r, h // 2 * 128 + h % 2 * HD:h // 2 * 128 + h % 2 * HD + HD])
            o.then_inc(s_dsb, 1)

        @block.tensor
        def _(pe):
            pe.wait_ge(s_cw, 3)

            def turn(t, b):
                pe.wait_ge(s_xT, t)
                pe.wait_ge(s_xn, t + 1)
                for c in range(KC):
                    mm = pe.transpose(bank[4][:, c * 128:c * 128 + P], xn[:, b, c * 128:(c + 1) * 128], g["ident"][0:P, 0:P])
                mm.then_inc(s_tr, 1)

            def keys(t, b, old):
                pe.wait_ge(s_xT, t + 1)
                if old:
                    pe.wait_ge(s_kvn, t - 1)
                for n in range(2):
                    for c in range(KC):
                        mm = pe.matmul(bank[2 * n + b][0:P, :], xT[:, b, c, :], wkv[:, c, n * KV:(n + 1) * KV],
                                       start=c == 0, stop=c == 1)
                mm.then_inc(s_kv, 1)

            def tile(t, b, first, last):
                if not last:
                    turn(t + 1, 1 - b)
                    keys(t + 1, 1 - b, not first)
                pe.wait_ge(s_kvn, t + 1)
                for j in range(KV // 128):
                    mm = pe.matmul(bank[5][:, j * 128:(j + 1) * 128], kvn[:, b, KV + j * 128:KV + (j + 1) * 128],
                                   kvn[:, b, j * 128:(j + 1) * 128], start=first and j == 0, stop=last, skip_group_check=True)
                mm.then_inc(s_dot, 1)
            turn(0, 0)
            keys(0, 0, False)
            over_tiles_summed(pe, tile)
            pe.wait_ge(s_dsb, 1)
            for j in range(KV // 128):
                mm = pe.matmul(bank[6 + j // 2][:, j % 2 * D:(j % 2 + 1) * D], dots[:, j, :], wo[:, j, :], start=True, stop=True)
            mm.then_inc(s_g, 1)
            pe.wait_ge(s_gsb, 1)
            for m in range(KC):
                for j in range(KV // 128):
                    mm = pe.matmul(bank[m][:, 0:D], wq[:, j, m * 128:(m + 1) * 128], gm[:, j, :], start=j == 0, stop=j == 3)
            mm.then_inc(s_c, 1)

        @block.scalar
        def _(act):
            act.wait_ge(s_var, 1)
            act.activation(g["rstd"][:, :], g["rstd"][:, :], ACT.Sqrt).then_inc(s_rstd, 1)

            def turned(t, b):
                act.wait_ge(s_tr, t + 1)
                act.copy(xT[:, b, :, :], bank[4][:, 0:256].rearrange("p (c q) -> p c q", c=2)[:, :, 0:P]).then_inc(s_xT, 1)

            def tile(t, b, first, last):
                act.wait_ge(s_kv, t + 1)
                act.wait_ge(s_v1, t * 2)
                for n in range(2):
                    o = act.activation(sq[:, n * KV:(n + 1) * KV], bank[2 * n + b][0:P, :], ACT.Square)
                o.then_inc(s_sq, 1)
                if not last:
                    turned(t + 1, 1 - b)
                act.wait_ge(s_root, t + 1)
                act.activation(var[:, b, :], var[:, b, :], ACT.Sqrt).then_inc(s_r1, 1)
            turned(0, 0)
            over_tiles_summed(act, tile)
            act.wait_ge(s_g, 1)
            for j in range(2):
                o = act.copy(gm[:, 2 * j:2 * j + 2, :], bank[6 + j][:, :].rearrange("p (k f) -> p k f", k=2))
            o.then_inc(s_gsb, 1)
            act.wait_ge(s_c, 1)
            for m in range(KC):
                act.activation(g["c1"][:, m, :], bank[m][:, 0:D], ACT.Copy, scale=1.0 / N)


def l1_update(nc, a, g):
    bank, x = g["bank"], g["x"]
    with Stage(nc, "U") as st:
        wd = st.sb("wd", [128, KC, HD])
        wf = st.sb("wf", [2 * HD, HD])
        wu = st.sb("wu", [HD, D])
        bd = st.sb("bd", [HD, 1])
        bf = st.sb("bf", [HD, 1])
        bo = st.sb("bo", [2, D])
        xn = st.sb("xn", [P, 2, D])
        xT = st.sb("xT", [128, 2, KC, P])
        tm = st.sb("tm", [P, 2, HD])
        rc = st.sb("rc", [P, T])
        nf = st.sb("nf", [2 * HD, 2, P])
        fu = st.sb("fu", [HD, 2, P])
        s_w = st.sem("weights")
        s_rc, s_xn, s_tr, s_xT, s_nf_ps, s_nf, s_fu_ps, s_fu, s_o, s_x0, s_x = (st.sem(n) for n in (
            "rcount", "xn", "transposed", "xT", "nf_psum", "nf", "fused_psum", "fused", "out", "x0", "x"))
        block = st.block()

        @block.sync
        def _(sp):
            for dst, src in ((wd[:, :, :], a["L1_gnn_W_down_T"].rearrange("(k p) f -> p k f", p=128)),
                             (wf[:, :], a["L1_gnn_W_fusion_T"]),
                             (wu[:, :], a["L1_gnn_W_up_T"]), (bd[:, :], a["L1_gnn_b_down_col"]),
                             (bf[:, :], a["L1_gnn_b_fusion_col"]), (bo[0:1, :], a["L1_gnn_b_up"].unsqueeze(0)),
                             (bo[1:2, :], a["L1_mix_b_out"].unsqueeze(0))):
                sp.dma_start(dst, src).then_inc(s_w, 16)

        @block.vector
        def _(v):
            v.tensor_scalar(rc[:, :], g["time"][:, :, HD], 1.0, None, ALU.max).then_inc(s_rc, 1)
            v.wait_ge(s_rc, 1)
            v.reciprocal(rc[:, :], rc[:, :]).then_inc(s_rc, 1)
            v.wait_ge(s_rc, 2)

            def prepare(t, b):
                v.wait_ge(s_tr, t)
                v.tensor_scalar(xn[:, b, :], tile_of(x, t), tile_of(g["mv"], t)[:, 0:1], g["rstd"][:, bass.ds(t, 1)],
                                ALU.subtract, ALU.mult)
                v.tensor_scalar(tm[:, b, :], tile_of(g["time"], t)[:, 0:HD], rc[:, bass.ds(t, 1)], None, ALU.mult).then_inc(s_xn, 1)

            def tile(t, b, first, last):
                v.wait_ge(s_xn, t + 1)
                v.tensor_tensor(tile_of(x, t), tile_of(x, t), xn[:, b, :], ALU.add).then_inc(s_x0, 1)
                if not last:
                    prepare(t + 1, 1 - b)
                v.wait_ge(s_x0, t + 1)
                v.wait_ge(s_o, t + 1)
                v.tensor_tensor(tile_of(x, t), tile_of(x, t), bank[6 + b][0:P, 0:D], ALU.add).then_inc(s_x, 1)
            prepare(0, 0)
            over_tiles_summed(v, tile)

        @block.tensor
        def _(pe):
            pe.wait_ge(s_w, 112)

            def tile(t, b):
                pe.wait_ge(s_xn, t + 1)
                for c in range(KC):
                    pe.transpose(bank[b][:, c * 128:c * 128 + P], xn[:, b, c * 128:(c + 1) * 128], g["ident"][0:P, 0:P])
                pe.transpose(bank[b][0:HD, 256:256 + P], tm[:, b, :], g["ident"][0:P, 0:P]).then_inc(s_tr, 1)
                pe.wait_ge(s_xT, t + 1)
                for c in range(KC):
                    mm = pe.matmul(bank[2 + b][0:HD, 0:P], wd[:, c, :], xT[:, b, c, :], start=c == 0, stop=c == 1)
                mm.then_inc(s_nf_ps, 1)
                for c in range(KC):
                    pe.matmul(bank[6 + b][0:P, 0:D], xT[:, b, c, :], g["c1"][:, c, :], start=c == 0, stop=False)
                pe.matmul(bank[6 + b][0:P, 0:D], g["ones"][0:2, 0:P], bo[:, :], start=False, stop=False)
                pe.wait_ge(s_nf, t + 1)
                pe.matmul(bank[4 + b][0:HD, 0:P], wf[:, :], nf[:, b, :], start=True, stop=True).then_inc(s_fu_ps, 1)
                pe.wait_ge(s_fu, t + 1)
                pe.matmul(bank[6 + b][0:P, 0:D], fu[:, b, :], wu[:, :], start=False, stop=True).then_inc(s_o, 1)
            over_tiles(pe, tile)

        @block.scalar
        def _(act):
            act.wait_ge(s_w, 112)

            def tile(t, b):
                act.wait_ge(s_tr, t + 1)
                act.copy(xT[:, b, :, :], bank[b][:, 0:256].rearrange("p (c q) -> p c q", c=2)[:, :, 0:P]).then_inc(s_xT, 1)
                act.copy(nf[HD:2 * HD, b, :], bank[b][0:HD, 256:256 + P])
                act.wait_ge(s_nf_ps, t + 1)
                act.activation(nf[0:HD, b, :], bank[2 + b][0:HD, 0:P], ACT.Relu, bias=bd[:, :]).then_inc(s_nf, 1)
                act.wait_ge(s_fu_ps, t + 1)
                act.activation(fu[:, b, :], bank[4 + b][0:HD, 0:P], ACT.Relu, bias=bf[:, :]).then_inc(s_fu, 1)
            over_tiles(act, tile)


_INS = ['x', 'src', 'dst', 'edge_attr_32', 'L0_gnn_W', 'L0_gnn_Wl', 'L0_gnn_Wr', 'L0_gnn_b', 'L0_mix_w_qkv',
        'L0_mix_b_qkv', 'L0_mix_norm_g', 'L0_mix_norm_b', 'L0_mix_w_fc1', 'L0_mix_b_fc1', 'L0_mix_w_fc2',
        'L0_mix_b_fc2', 'L0_ffn_Wg', 'L0_ffn_bg', 'L0_ffn_W1', 'L0_ffn_b1', 'L0_ffn_W2', 'L0_ffn_b2',
        'L1_gnn_W_down', 'L1_gnn_b_down', 'L1_gnn_W_time', 'L1_gnn_b_time', 'L1_gnn_W_fusion',
        'L1_gnn_b_fusion', 'L1_gnn_W_up', 'L1_gnn_b_up', 'L1_mix_w_qkv', 'L1_mix_w_out', 'L1_mix_b_out',
        'L1_ffn_router_w', 'L1_ffn_w1', 'L1_ffn_w2', 'L1_ffn_w3']


def layouts(x):
    import numpy as np

    def cols(b):
        return np.ascontiguousarray(b.reshape(-1, 128).T)

    def T(w):
        return np.ascontiguousarray(np.swapaxes(w, -1, -2))

    keep = ['x', 'src', 'dst', 'edge_attr_32', 'L0_gnn_W', 'L0_gnn_b', 'L0_mix_w_qkv', 'L0_mix_b_qkv',
            'L0_mix_w_fc1', 'L0_mix_w_fc2', 'L0_mix_b_fc2', 'L0_ffn_bg', 'L0_ffn_b2', 'L1_gnn_b_time',
            'L1_gnn_b_up', 'L1_mix_w_qkv', 'L1_mix_b_out', 'L0_ffn_b1']
    a = {n: np.ascontiguousarray(x[n]) for n in keep}
    a['L0_gnn_W_T'] = T(x['L0_gnn_W'])
    a['L0_gnn_Wl_T'] = T(x['L0_gnn_Wl'])
    a['L0_gnn_Wr_T'] = T(x['L0_gnn_Wr'])
    a['L0_mix_w_q_T'] = T(x['L0_mix_w_qkv'][:, :D])
    a['L0_mix_b_q_cols'] = cols(x['L0_mix_b_qkv'][:D])
    for n in ('L0_mix_norm_g', 'L0_mix_norm_b', 'L0_mix_b_fc1'):
        a[n + '_cols'] = cols(x[n])
    a['L0_ffn_b1_cols'] = np.ascontiguousarray(x['L0_ffn_b1'].reshape(-1, 128).T)
    for n in ('L0_ffn_Wg', 'L0_ffn_W1', 'L0_ffn_W2', 'L1_gnn_W_down', 'L1_gnn_W_time', 'L1_gnn_W_fusion',
              'L1_gnn_W_up', 'L1_mix_w_out', 'L1_ffn_router_w', 'L1_ffn_w1', 'L1_ffn_w2', 'L1_ffn_w3'):
        a[n + '_T'] = T(x[n])
    a['L1_mix_w_kv_T'] = T(x['L1_mix_w_qkv'][512:])
    for n in ('L1_gnn_b_down', 'L1_gnn_b_fusion'):
        a[n + '_col'] = np.ascontiguousarray(x[n].reshape(64, 1))
    return a


def kernel(**inputs):
    import numpy as _np
    import concourse.bacc as _bacc
    from concourse import mybir as _mybir
    from concourse.bass_utils import run_bass_kernel_spmd as _run

    nc = _bacc.Bacc("TRN2", target_bir_lowering=False, num_devices=1)
    laid = layouts({n: _np.asarray(inputs[n]) for n in _INS})
    arrays, aps = {}, {}
    for name, v in laid.items():
        arrays[f"in_{name}"] = v
        aps[name] = nc.dram_tensor(f"in_{name}", v.shape, _mybir.dt.from_np(v.dtype), kind="ExternalInput").ap()
    out = nc.dram_tensor("out_dram", (N, D), F32, kind="ExternalOutput").ap()
    build(nc, aps, out)
    r = _run(nc, [arrays], core_ids=[0])
    return r.results[0]["out_dram"]
```

```python
from contextlib import ExitStack

import concourse.bass as bass
from concourse import mybir

F32 = mybir.dt.float32
I32 = mybir.dt.int32
U32 = mybir.dt.uint32
ALU = mybir.AluOpType
ACT = mybir.ActivationFunctionType
AXX = mybir.AxisListType.X

N = 3125
D = 256
P = 125
T = N // P
KC = D // 128
E = 53125
EC = E // P
EU = 25
SLOT = 128
ET = 448
PAY = 34
AT = 32
HD = 64
NH = 4
TAB = HD + NH
VW = NH * HD + NH + HD + 1
O_W, O_T, O_C = NH * HD, NH * HD + NH, NH * HD + NH + HD
MLP = 768
NE = 8
TOPK = 2
FT = 56
H0 = 1024
H1 = 682
H1C = 6
EPS = 1e-5
assert T * P == N and EC * P == E and EC % (2 * EU) == EU and ET % 32 == 0
assert (E + T * (SLOT - 1)) // SLOT <= ET and (N * TOPK + NE * (SLOT - 1)) // SLOT == FT


def wait_count(eng, sem, n):
    if not isinstance(n, int) or n > 0:
        eng.wait_ge(sem, n)


def over_tiles(eng, body, count=T, written_out=2):
    body(0, 0)
    body(1, 1)
    pairs = (count - written_out + 1) // 2
    with eng.Fori(1, pairs) as j:
        body(j * 2, 0)
        body(j * 2 + 1, 1)
    for t in range(pairs * 2, count):
        body(t, t % 2)


def inside(t, count):
    return not isinstance(t, int) or 0 <= t < count


def at_first(t):
    return isinstance(t, int) and t == 0


def at_last(t, count=T):
    return isinstance(t, int) and t == count - 1


def over_rounds(eng, body, rounds, width, rest=0):
    for b in range(width):
        body(b, 0, b)
    with eng.Fori(1, rounds) as r:
        for b in range(width):
            body(r * width + b, r, b)
    for b in range(rest):
        body(rounds * width + b, rounds, b)


class Stage:

    def __init__(self, nc, name):
        self.nc, self.name = nc, name

    def __enter__(self):
        self.ctx, self.used = ExitStack(), []
        return self

    def __exit__(self, *a):
        self.ctx.close()
        if self.used:
            self.nc.clear_and_free_semaphores(self.used)
            self.nc.all_engine_barrier(sem_only=True)

    def sb(self, name, shape, dt=F32):
        return self.ctx.enter_context(self.nc.sbuf_tensor(f"{self.name}_{name}", shape, dt))

    def sem(self, name):
        self.used.append(self.nc.alloc_semaphore(f"{self.name}_{name}"))
        return self.used[-1]

    def sems(self, name, n=2):
        return [self.sem(f"{name}{k}") for k in range(n)]

    def block(self):
        return self.ctx.enter_context(self.nc.Block())


def layer_stats(v, x, stats, mv, rstd, done, ready):
    for t in range(T):
        v.bn_stats(stats[:, t, :], x[:, t, :]).then_inc(done, 1)
    v.wait_ge(done, T)
    v.tensor_tensor(mv[:, :, 0], stats[:, :, 1], stats[:, :, 4], ALU.add).then_inc(done, 1)
    v.tensor_tensor(mv[:, :, 1], stats[:, :, 1], stats[:, :, 4], ALU.subtract).then_inc(done, 1)
    v.tensor_tensor(rstd[:, :], stats[:, :, 2], stats[:, :, 5], ALU.add).then_inc(done, 1)
    v.wait_ge(done, T + 3)
    v.tensor_scalar(mv[:, :, 0], mv[:, :, 0], 0.5, None, ALU.mult).then_inc(done, 1)
    v.tensor_tensor(mv[:, :, 1], mv[:, :, 1], mv[:, :, 1], ALU.mult).then_inc(done, 1)
    v.tensor_scalar(rstd[:, :], rstd[:, :], 1.0 / D, EPS, ALU.mult, ALU.add).then_inc(done, 1)
    v.wait_ge(done, T + 6)
    v.scalar_tensor_tensor(out=rstd[:, :], in0=mv[:, :, 1], scalar=0.25, in1=rstd[:, :],
                           op0=ALU.mult, op1=ALU.add).then_inc(done, 1)
    v.wait_ge(done, T + 7)
    v.reciprocal(rstd[:, :], rstd[:, :]).then_inc(ready, 1)


def bins_buffers(st, B, C, room=0):
    onehot = st.sb("onehot", [P, max(B * C, room)])
    return dict(
        onehot_flat=onehot, onehot=onehot[:, 0:B * C].rearrange("p (b c) -> p b c", b=B), cum=st.sb("cum", [P, B, C]), cnt=st.sb("cnt", [P, B + 1]),
        part=st.sb("part", [P, B]), tot=st.sb("tot", [P, B]), toti=st.sb("toti", [P, B], I32),
        pad=st.sb("pad", [P, B]), start=st.sb("start", [P, B + 1]), posf=st.sb("posf", [P, C]),
        done=st.sem("bin_done"), counted=st.sem("bin_counted"), summed=st.sem("bin_summed"))


def bins_vector(v, k, bin_of, number, one, B, C, psum, parts, rows, map_out, map_n, tile_at, two, wide, ready):
    oh, cum, cnt, done = k["onehot"], k["cum"], k["cnt"], k["done"]
    v.tensor_tensor(oh[:, :, :], bin_of.unsqueeze(1).broadcast_to([P, B, C]),
                    number[0:P, 0:B].unsqueeze(2).broadcast_to([P, B, C]), ALU.is_equal).then_inc(done, 1)
    v.wait_ge(done, 1)
    v.tensor_tensor_scan(cum[:, :, :].rearrange("p b c -> p (b c)"), one[0:P, 0:1].broadcast_to([P, B * C]),
                         oh[:, :, :].rearrange("p b c -> p (b c)"), 0.0, ALU.mult, ALU.add).then_inc(done, 1)
    v.memset(cnt[:, 0:1], 0.0).then_inc(done, 1)
    v.wait_ge(done, 3)
    v.tensor_copy(cnt[:, 1:B + 1], cum[:, :, C - 1]).then_inc(done, 1)
    v.wait_ge(done, 4)
    v.tensor_tensor(k["part"][:, :], cnt[:, 1:B + 1], cnt[:, 0:B], ALU.subtract).then_inc(k["counted"], 1)
    v.wait_ge(k["summed"], 1)
    v.tensor_scalar(k["toti"][:, :], psum[0:P, B:2 * B], float(SLOT - 1), None, ALU.add).then_inc(done, 1)
    v.wait_ge(done, 5)
    v.tensor_scalar(k["toti"][:, :], k["toti"][:, :], 7, 7, ALU.logical_shift_right,
                    ALU.logical_shift_left).then_inc(done, 1)
    v.wait_ge(done, 6)
    v.tensor_copy(k["pad"][:, :], k["toti"][:, :]).then_inc(done, 1)
    v.memset(k["start"][:, 0:1], 0.0).then_inc(done, 1)
    v.wait_ge(done, 8)
    v.tensor_tensor_scan(k["start"][:, 1:B + 1], one[0:P, 0:1].broadcast_to([P, B]), k["pad"][:, :], 0.0,
                         ALU.mult, ALU.add).then_inc(done, 1)
    v.wait_ge(done, 9)
    v.tensor_tensor(k["tot"][:, :], psum[0:P, 0:B], k["start"][:, 0:B], ALU.add).then_inc(done, 1)
    v.wait_ge(done, 10)
    v.scalar_tensor_tensor(out=k["tot"][:, :], in0=k["tot"][:, :], scalar=-1.0, in1=cnt[:, 0:B],
                           op0=ALU.add, op1=ALU.subtract).then_inc(done, 1)
    v.wait_ge(done, 11)
    n = 11
    for first, end in parts:
        cols = slice(first, end)
        for b in range(B):
            o = v.scalar_tensor_tensor(out=cum[:, b, cols], in0=cum[:, b, cols], scalar=k["tot"][:, b:b + 1],
                                       in1=oh[:, b, cols], op0=ALU.add, op1=ALU.mult)
        o.then_inc(done, 1)
        v.wait_ge(done, n + 1)
        v.tensor_reduce(k["posf"][:, cols], cum[:, :, cols].rearrange("p b c -> p c b"), AXX, ALU.add).then_inc(done, 1)
        v.wait_ge(done, n + 2)
        n += 2
        if rows is not None:
            pi, lane, tile, row = rows
            v.tensor_copy(pi[:, cols], k["posf"][:, cols]).then_inc(done, 1)
            v.wait_ge(done, n + 1)
            v.tensor_scalar(lane[:, cols], pi[:, cols], SLOT - 1, None, ALU.bitwise_and).then_inc(done, 1)
            v.tensor_scalar(tile[:, cols], pi[:, cols], 7, None, ALU.logical_shift_right).then_inc(done, 1)
            v.wait_ge(done, n + 3)
            v.scalar_tensor_tensor(out=row[:, cols], in0=lane[:, cols], scalar=float(ET), in1=tile[:, cols],
                                   op0=ALU.mult, op1=ALU.add).then_inc(done, 1)
            v.wait_ge(done, n + 4)
            n += 4
        v.sem_inc(ready, 1)
    v.tensor_tensor(wide, tile_at[0:1, 0:map_n].unsqueeze(2).broadcast_to([1, map_n, B - 1]),
                    k["start"][0:1, 1:B].unsqueeze(1).broadcast_to([1, map_n, B - 1]), ALU.is_ge).then_inc(done, 1)
    v.wait_ge(done, n + 1)
    v.tensor_reduce(two, wide, AXX, ALU.add).then_inc(done, 1)
    v.wait_ge(done, n + 2)
    v.tensor_copy(map_out, two).then_inc(done, 1)
    v.wait_ge(done, n + 3)


def bins_tensor(pe, k, before, ones, B, psum):
    pe.wait_ge(k["counted"], 1)
    pe.matmul(psum[0:P, 0:B], before[0:P, 0:P], k["part"][:, :], start=True, stop=True)
    pe.matmul(psum[0:P, B:2 * B], ones[0:P, 0:P], k["part"][:, :], start=True, stop=True).then_inc(k["summed"], 1)


def tile_of(x, t):
    return x[:, bass.ds(t, 1), :].rearrange("p o f -> p (o f)")


def build(nc, a, out):
    with ExitStack() as ctx:
        def sb(name, shape, dt=F32):
            return ctx.enter_context(nc.sbuf_tensor(name, shape, dt))

        g = {
            "table": nc.dram_tensor("table", (N, TAB), F32).ap(),
            "slots": nc.dram_tensor("slots", (SLOT * ET, PAY), F32).ap(),
            "xs": nc.dram_tensor("xs", (FT * SLOT, D), F32).ap(),
            "ys": nc.dram_tensor("ys", (FT * SLOT, D), F32).ap(),
        }
        g["x"] = sb("x_nodes", [P, T, D])
        g["mv"] = sb("mv", [P, T, 2])
        g["rstd"] = sb("rstd", [P, T])
        g["ident"] = sb("ident", [128, 128])
        g["ones"] = sb("ones", [128, 128])
        g["before"] = sb("before", [128, 128])
        g["bin_no"] = sb("bin_no", [128, T + 1])
        g["tile_at"] = sb("tile_at", [1, ET])
        g["time"] = sb("time", [P, T, HD + 1])
        g["el"] = sb("el", [P, T, NH])
        g["edge_map"] = sb("edge_map", [1, ET], I32)
        g["bank"] = [ctx.enter_context(nc.psum_tensor(f"bank{k}", [128, 512], F32)) for k in range(8)]
        front(nc, a, g)
        with Stage(nc, "W0") as weights:
            w = input_weights(weights, 0)
            with Stage(nc, "G") as agg:
                g["agg"] = agg.sb("agg", [P, T, VW])
                edge_aggregation(nc, a, g, w)
                gat_finish(nc, a, g)
            moe(nc, a, g, 0, w)
        with Stage(nc, "W1") as weights:
            w = input_weights(weights, 1)
            with Stage(nc, "L") as l1:
                g["c1"] = l1.sb("c1", [128, KC, D])
                l1_keys_values(nc, a, g, w)
                l1_update(nc, a, g)
            moe(nc, a, g, 1, w, out)


def front(nc, a, g):
    bank = g["bank"]
    table_rows = g["table"].rearrange("(t p) f -> t p f", p=P)
    attr = a["edge_attr_32"].rearrange("(p c) f -> p c f", c=EC)
    slots_pf = g["slots"].rearrange("(p t) f -> p (t f)", p=SLOT)
    FILLS = 8
    ROUNDS = EC // EU
    MC = MLP // 128
    with Stage(nc, "A") as st:
        src_i = st.sb("src_i", [P, EC], I32)
        dst_i = st.sb("dst_i", [P, EC], I32)
        src_f = st.sb("src_f", [P, EC])
        own = st.sb("own_tile", [P, EC])
        ends = st.sb("ends", [P, EC, 2], I32)
        k = bins_buffers(st, T, EC, ET * (T - 1))
        pos_i = st.sb("pos_i", [P, EC], I32)
        lane_i = st.sb("lane_i", [P, EC], I32)
        tile_i = st.sb("tile_i", [P, EC], I32)
        row_i = st.sb("row_i", [P, EC], I32)
        narrow = st.sb("narrow", [1, ET])
        fill = st.sb("fill", [128, ET // FILLS, PAY])
        pay = st.sb("pay", [P, 2, EU, PAY])
        ids = st.sb("ids", [P, 2, EU], I32)
        w72 = st.sb("w72", [128, KC, TAB + NH])
        wT = st.sb("wT", [HD, D])
        wlrT = st.sb("wlrT", [HD, 2 * NH])
        stats = st.sb("stats", [P, T, 6])
        xn = st.sb("xn", [P, 2, D + 1])
        xT = st.sb("xT", [128, 2, KC, P])
        tab = st.sb("tab", [P, 2, TAB + NH])
        wkv = st.sb("wkv", [128, KC, 2 * D])
        bkv = st.sb("bkv", [1, 2 * D])
        wqT = st.sb("wqT", [128, KC, D])
        bq = st.sb("bq", [128, KC])
        nn = st.sb("nn", [1, 1])
        gram = st.sb("gram", [128, KC, D + 1])
        grow = st.sb("grow", [1, D])
        gwv = st.sb("gwv", [128, KC, D])
        gwv_row = st.sb("gwv_row", [1, D])
        logit = st.sb("logit", [128, KC, HD])
        lmax = st.sb("lmax", [128, KC])
        lsum = st.sb("lsum", [128, KC])
        diag = st.sb("diag", [128, KC, 128])
        attnT = st.sb("attnT", [128, KC, 128])
        c0 = st.sb("c0", [128, KC, D])
        c0_row = st.sb("c0_row", [1, D])
        x1 = k["cum"][:, :, :].rearrange("p b c -> p (b c)")[:, 0:T * D].rearrange("p (t f) -> p t f", f=D)
        mv1 = st.sb("mv1", [P, T, 2])
        rstd1 = st.sb("rstd1", [P, T])
        lnT = st.sb("lnT", [128, 2, KC])
        fc1 = st.sb("fc1", [128, KC, MLP])
        fb1 = st.sb("fb1", [128, MC])
        fc2 = st.sb("fc2", [128, MC, D])
        fb2 = st.sb("fb2", [1, D])
        gT = st.sb("gT", [128, 2, MC, P])
        s_edges, s_w, s_x, s_wm = st.sem("edges"), st.sem("weights"), st.sem("x_loaded"), st.sem("mix_weights")
        s_const, s_ones = st.sem("const"), st.sem("ones")
        s_fill, s_filled = st.sem("fill"), st.sem("filled")
        s_rows, s_ends = st.sem("rows_ready"), st.sem("round_ends")
        s_go, s_own = st.sem("round_go"), st.sem("own_row")
        s_attr, s_scat = st.sems("attr_loaded"), st.sems("scattered")
        s_ln = st.sem("ln")
        s_rstd, s_var = st.sem("rstd"), st.sem("var")
        s_xn, s_tr, s_xT, s_h, s_tab, s_wa, s_waT = (st.sem(n) for n in (
            "xn_ready", "transposed", "xT_ready", "h_ready", "tab_ready", "wa", "wa_ready"))
        s_st = st.sems("table_stored")
        ps_bin, ps_g = bank[0], [bank[1], bank[2]]
        ps_t, ps_h = [bank[3], bank[4]], [bank[5], bank[6]]
        s_gram, s_fold_pe, s_fold = st.sem("gram"), st.sem("fold_pe"), st.sem("fold")
        s_b_xn, s_b_tr, s_b_xT, s_b_mm, s_b_x1, s_b_st = (st.sem("b_" + n) for n in (
            "xn", "tr", "xT", "mm", "x1", "stat"))
        s_m_xn, s_m_tr, s_m_xT, s_m_h, s_m_g, s_m_y, s_m_out, s_m_var, s_m_rstd = (st.sem("m_" + n) for n in (
            "xn", "tr", "xT", "h", "g", "y", "out", "var", "rstd"))
        block = st.block()

        @block.sync
        def _(sp):
            sp.dma_start(src_i[:, :], a["src"].rearrange("(p c) -> p c", c=EC)).then_inc(s_edges, 16)
            sp.dma_start(dst_i[:, :], a["dst"].rearrange("(p c) -> p c", c=EC)).then_inc(s_edges, 16)
            sp.wait_ge(s_fill, 3)
            w = ET // FILLS * PAY
            for q in range(FILLS):
                sp.dma_start(slots_pf[:, q * w:(q + 1) * w],
                             fill[:, :, :].rearrange("p t f -> p (t f)")).then_inc(s_filled, 16)
            sp.dma_start(g["x"][:, :, :], a["x"].rearrange("(t p) f -> p t f", p=P)).then_inc(s_x, 16)
            sp.dma_start(w72[:, :, 0:HD], a["L0_gnn_W"].rearrange("(k p) f -> p k f", p=128)).then_inc(s_w, 16)
            sp.dma_start(wT[:, :], a["L0_gnn_W_T"]).then_inc(s_w, 16)
            sp.dma_start(wlrT[:, 0:NH], a["L0_gnn_Wr_T"]).then_inc(s_w, 16)
            sp.dma_start(wlrT[:, NH:2 * NH], a["L0_gnn_Wl_T"]).then_inc(s_w, 16)
            mix = [(wkv[:, :, :], a["L0_mix_w_qkv"].rearrange("(k p) f -> p k f", p=128)[:, :, D:3 * D]),
                   (bkv[:, :], a["L0_mix_b_qkv"][D:3 * D].unsqueeze(0)),
                   (wqT[:, :, :], a["L0_mix_w_q_T"].rearrange("(k p) f -> p k f", p=128)),
                   (bq[:, :], a["L0_mix_b_q_cols"]),
                   (lnT[:, 0, :], a["L0_mix_norm_g_cols"]), (lnT[:, 1, :], a["L0_mix_norm_b_cols"]),
                   (fc1[:, :, :], a["L0_mix_w_fc1"].rearrange("(k p) f -> p k f", p=128)),
                   (fb1[:, :], a["L0_mix_b_fc1_cols"]),
                   (fc2[:, :, :], a["L0_mix_w_fc2"].rearrange("(k p) f -> p k f", p=128)),
                   (fb2[:, :], a["L0_mix_b_fc2"].unsqueeze(0))]
            for dst, src in mix:
                sp.dma_start(dst, src).then_inc(s_wm, 16)
            def load(n, r, b):
                wait_count(sp, s_scat[b], r * (16 * EU))
                sp.dma_start(pay[:, b, :, 0:AT], attr[:, bass.ds(n * EU, EU), :]).then_inc(s_attr[b], 16)
            over_rounds(sp, load, ROUNDS // 2, 2, ROUNDS % 2)

        @block.gpsimd
        def _(gp):
            gp.memset(fill[:, :, 0:AT], 0.0).then_inc(s_fill, 1)
            gp.memset(fill[:, :, AT:AT + 1], -1.0).then_inc(s_fill, 1)
            gp.memset(fill[:, :, AT + 1:PAY], 0.0).then_inc(s_fill, 1)
            gp.iota(g["bin_no"][:, :], [[1, T + 1]], base=0, channel_multiplier=0,
                    allow_small_or_imprecise_dtypes=True).then_inc(s_const, 1)
            gp.iota(g["tile_at"][:, :], [[SLOT, ET]], base=0, channel_multiplier=0,
                    allow_small_or_imprecise_dtypes=True).then_inc(s_const, 1)
            gp.memset(g["ones"][:, :], 1.0).then_inc(s_ones, 1)
            gp.wait_ge(s_ones, 1)
            gp.affine_select(out=g["ident"][:, :], in_=g["ones"][:, :], compare_op=ALU.is_equal, fill=0.0, base=0,
                             pattern=[[1, 128]], channel_multiplier=-1).then_inc(s_const, 1)
            gp.affine_select(out=g["before"][:, :], in_=g["ones"][:, :], compare_op=ALU.is_gt, fill=0.0, base=0,
                             pattern=[[1, 128]], channel_multiplier=-1).then_inc(s_const, 1)
            gp.memset(xn[:, :, D:D + 1], 1.0).then_inc(s_const, 1)
            gp.memset(nn[:, :], float(N)).then_inc(s_const, 1)
            gp.memset(diag[:, :, :], 0.0).then_inc(s_const, 1)
            gp.wait_ge(s_rows, 1)
            gp.wait_ge(s_filled, 16 * FILLS)

            def scatter(n, r, b):
                if not isinstance(r, int):
                    gp.wait_ge(s_rows, 2)
                wait_count(gp, s_scat[b], r * (16 * EU))
                gp.tensor_copy(pay[:, b, :, AT:PAY].bitcast(I32), ends[:, bass.ds(n * EU, EU), :]).then_inc(s_ends, 1)
                gp.tensor_copy(ids[:, b, :], row_i[:, bass.ds(n * EU, EU)]).then_inc(s_ends, 1)
                gp.wait_ge(s_ends, n * 2 + 2)
                gp.wait_ge(s_attr[b], r * 16 + 16)
                gp.sem_inc(s_go, 1)
                for u in range(EU):
                    gp.indirect_dma_start(g["slots"], bass.IndirectOffsetOnAxis(ap=ids[:, b, u:u + 1], axis=0),
                                          pay[:, b, u, :], None).then_inc(s_scat[b], 16)
            over_rounds(gp, scatter, ROUNDS // 2, 2, ROUNDS % 2)
            gp.wait_ge(s_scat[0], (ROUNDS // 2 + 1) * 16 * EU)
            gp.wait_ge(s_scat[1], ROUNDS // 2 * 16 * EU)

        @block.vector
        def _(v):
            v.wait_ge(s_edges, 32)
            v.tensor_copy(src_f[:, :], src_i[:, :]).then_inc(s_own, 1)
            v.tensor_copy(ends[:, :, 1], dst_i[:, :])
            v.wait_ge(s_own, 1)
            v.tensor_scalar(own[:, :], src_f[:, :], 0.5, 1.0 / P, ALU.add, ALU.mult).then_inc(s_own, 1)
            v.wait_ge(s_own, 2)
            v.tensor_scalar(own[:, :], own[:, :], -0.5, 1.5 * 2 ** 23, ALU.add, ALU.add).then_inc(s_own, 1)
            v.wait_ge(s_own, 3)
            v.tensor_scalar(own[:, :], own[:, :], -1.5 * 2 ** 23, None, ALU.add).then_inc(s_own, 1)
            v.wait_ge(s_own, 4)
            v.scalar_tensor_tensor(out=ends[:, :, 0].bitcast(F32), in0=own[:, :], scalar=-float(P), in1=src_f[:, :],
                                   op0=ALU.mult, op1=ALU.add).then_inc(s_own, 1)
            v.wait_ge(s_const, 7)
            v.wait_ge(s_own, 5)
            wide = k["onehot_flat"][0:1, 0:ET * (T - 1)].rearrange("o (t b) -> o t b", b=T - 1)
            bins_vector(v, k, own[:, :], g["bin_no"], g["ones"], T, EC, ps_bin, ((0, 2 * EU), (2 * EU, EC)),
                        (pos_i, lane_i, tile_i, row_i), g["edge_map"][:, :], ET, g["tile_at"],
                        narrow[:, :], wide, s_rows)
            v.wait_ge(s_x, 16)
            layer_stats(v, g["x"], stats, g["mv"], g["rstd"], s_ln, s_var)
            v.wait_ge(s_wa, 1)
            v.tensor_copy(w72[:, :, HD:TAB + NH],
                          bank[7][:, 0:4 * NH].rearrange("p (k f) -> p k f", k=2)).then_inc(s_waT, 1)
            v.wait_ge(s_rstd, 1)

            def normalise(t, b):
                wait_count(v, s_tr, t)
                v.tensor_scalar(xn[:, b, 0:D], tile_of(g["x"], t), tile_of(g["mv"], t)[:, 0:1],
                                g["rstd"][:, bass.ds(t, 1)], ALU.subtract, ALU.mult).then_inc(s_xn, 1)
            over_tiles(v, normalise)

            for c in range(KC):
                v.wait_ge(s_fold_pe, 4)
                for h in range(2):
                    r = slice(h * HD, h * HD + HD)
                    v.tensor_copy(logit[r, c, :], bank[5][r, c * 128 + h * HD:c * 128 + h * HD + HD]).then_inc(s_fold, 1)
            v.wait_ge(s_fold, 4)
            v.tensor_reduce(lmax[:, :], logit[:, :, :], AXX, ALU.max).then_inc(s_fold, 1)
            v.wait_ge(s_fold, 5)
            v.tensor_tensor(logit[:, :, :], logit[:, :, :], lmax[:, :].unsqueeze(2).broadcast_to([128, KC, HD]),
                            ALU.subtract).then_inc(s_fold, 1)
            v.wait_ge(s_fold, 7)
            v.tensor_reduce(lsum[:, :], logit[:, :, :], AXX, ALU.add).then_inc(s_fold, 1)
            v.wait_ge(s_fold, 8)
            v.reciprocal(lsum[:, :], lsum[:, :]).then_inc(s_fold, 1)
            v.wait_ge(s_fold, 9)
            for c in range(KC):
                for h in range(2):
                    r = slice(h * HD, h * HD + HD)
                    v.tensor_scalar(diag[r, c, h * HD:h * HD + HD], logit[r, c, :], lsum[r, c:c + 1], None,
                                    ALU.mult).then_inc(s_fold, 1)

            def attend_in(t, b):
                wait_count(v, s_b_tr, t - 1)
                wait_count(v, s_b_x1, t - 1)
                v.tensor_scalar(xn[:, b, 0:D], tile_of(g["x"], t), tile_of(g["mv"], t)[:, 0:1],
                                g["rstd"][:, bass.ds(t, 1)], ALU.subtract, ALU.mult).then_inc(s_b_xn, 1)

            def attend(t, b):
                if not at_last(t):
                    attend_in(t + 1, 1 - b)
                v.wait_ge(s_b_mm, t + 1)
                v.wait_ge(s_b_xn, t + 1)
                v.tensor_tensor(tile_of(x1, t), ps_h[b][0:P, 0:D], xn[:, b, 0:D], ALU.add).then_inc(s_b_x1, 1)
            attend_in(0, 0)
            over_tiles(v, attend)
            v.wait_ge(s_b_x1, T)
            layer_stats(v, x1, stats, mv1, rstd1, s_b_st, s_m_var)
            v.wait_ge(s_m_rstd, 1)

            def mlp_in(t, b):
                wait_count(v, s_m_tr, t - 1)
                v.tensor_scalar(xn[:, b, 0:D], tile_of(x1, t), tile_of(mv1, t)[:, 0:1],
                                rstd1[:, bass.ds(t, 1)], ALU.subtract, ALU.mult).then_inc(s_m_xn, 1)

            def mlp_out(t, b):
                v.tensor_tensor(tile_of(g["x"], t), tile_of(g["x"], t), tile_of(x1, t), ALU.add).then_inc(s_m_out, 1)
                if inside(t + 2, T):
                    mlp_in(t + 2, b)
                v.wait_ge(s_m_out, t * 2 + 1)
                v.wait_ge(s_m_y, t + 1)
                v.tensor_tensor(tile_of(g["x"], t), tile_of(g["x"], t), ps_h[b][0:P, 0:D], ALU.add).then_inc(s_m_out, 1)
            mlp_in(0, 0)
            mlp_in(1, 1)
            over_tiles(v, mlp_out, T, 4)

        @block.tensor
        def _(pe):
            pe.wait_ge(s_const, 7)
            bins_tensor(pe, k, g["before"], g["ones"], T, ps_bin)
            pe.wait_ge(s_w, 64)
            pe.matmul(bank[7][:, 0:2 * NH], wT[:, 0:128], wlrT[:, :], start=True, stop=True)
            pe.matmul(bank[7][:, 2 * NH:4 * NH], wT[:, 128:256], wlrT[:, :], start=True, stop=True).then_inc(s_wa, 1)
            pe.wait_ge(s_waT, 1)

            def body(t, b):
                pe.wait_ge(s_xn, t + 1)
                wait_count(pe, s_xT, t)
                for c in range(KC):
                    pe.transpose(ps_t[b][:, c * 128:c * 128 + P], xn[:, b, c * 128:(c + 1) * 128], g["ident"][0:P, 0:P])
                for c in range(KC):
                    mm = pe.matmul(ps_g[c][:, 0:D + 1], xn[:, b, c * 128:(c + 1) * 128], xn[:, b, :], start=at_first(t), stop=at_last(t))
                mm.then_inc(s_tr, 1)
                pe.wait_ge(s_xT, t + 1)
                wait_count(pe, s_tab, t)
                for c in range(KC):
                    mm = pe.matmul(ps_h[b][0:P, 0:TAB + NH], xT[:, b, c, :], w72[:, c, :], start=c == 0, stop=c == 1)
                mm.then_inc(s_h, 1)
            over_tiles(pe, body)

            pe.wait_ge(s_gram, 1)
            pe.wait_ge(s_wm, 160)
            for c in range(KC):
                mm = pe.transpose(bank[0][0:1, c * 128:(c + 1) * 128], gram[:, c, D:D + 1], g["ident"][:, :])
            mm.then_inc(s_fold_pe, 1)
            pe.wait_ge(s_gram, 2)
            for m in range(KC):
                for c in range(KC):
                    pe.matmul(bank[1 + m][:, 0:D], gram[:, c, m * 128:(m + 1) * 128], wkv[:, c, D:2 * D], start=c == 0, stop=False)
                mm = pe.matmul(bank[1 + m][:, 0:D], grow[:, m * 128:(m + 1) * 128], bkv[:, D:2 * D], start=False, stop=True)
            mm.then_inc(s_fold_pe, 1)
            for c in range(KC):
                pe.matmul(bank[7][0:1, 0:D], gram[:, c, D:D + 1], wkv[:, c, D:2 * D], start=c == 0, stop=False)
            pe.matmul(bank[7][0:1, 0:D], nn[:, :], bkv[:, D:2 * D], start=False, stop=True).then_inc(s_fold_pe, 1)
            pe.wait_ge(s_gram, 4)
            for m in range(KC):
                cols = slice(m * 128, (m + 1) * 128)
                for c in range(KC):
                    pe.matmul(bank[5][:, cols], wkv[:, c, cols], gwv[:, c, cols], start=c == 0, stop=False)
                mm = pe.matmul(bank[5][:, cols], bkv[:, cols], gwv_row[:, cols], start=False, stop=True)
            mm.then_inc(s_fold_pe, 1)
            pe.wait_ge(s_fold, 13)
            for c in range(KC):
                mm = pe.transpose(bank[0][:, c * 128:(c + 1) * 128], diag[:, c, :], g["ident"][:, :])
            mm.then_inc(s_fold_pe, 1)
            pe.wait_ge(s_gram, 5)
            for m in range(KC):
                for j in range(KC):
                    pe.matmul(bank[1 + m][:, j * 128:(j + 1) * 128], wqT[:, j, m * 128:(m + 1) * 128], attnT[:, j, :],
                              start=True, stop=True)
            for j in range(KC):
                mm = pe.matmul(bank[7][0:1, j * 128:(j + 1) * 128], bq[:, j:j + 1], attnT[:, j, :], start=True, stop=True)
            mm.then_inc(s_fold_pe, 1)
            pe.wait_ge(s_gram, 6)

            def turn(t, b):
                pe.wait_ge(s_b_xn, t + 1)
                for c in range(KC):
                    mm = pe.transpose(ps_t[b][:, c * 128:c * 128 + P], xn[:, b, c * 128:(c + 1) * 128], g["ident"][0:P, 0:P])
                mm.then_inc(s_b_tr, 1)

            def attend(t, b):
                if not at_last(t):
                    turn(t + 1, 1 - b)
                pe.wait_ge(s_b_xT, t + 1)
                for c in range(KC):
                    pe.matmul(ps_h[b][0:P, 0:D], xT[:, b, c, :], c0[:, c, :], start=c == 0, stop=False)
                pe.matmul(ps_h[b][0:P, 0:D], g["ones"][0:1, 0:P], c0_row[:, :], start=False, stop=True).then_inc(s_b_mm, 1)
            turn(0, 0)
            over_tiles(pe, attend)

            def mlp_hidden(t, b):
                pe.wait_ge(s_m_xn, t + 1)
                for c in range(KC):
                    mm = pe.transpose(ps_t[b][:, c * 128:c * 128 + P], xn[:, b, c * 128:(c + 1) * 128], g["ident"][0:P, 0:P])
                mm.then_inc(s_m_tr, 1)
                pe.wait_ge(s_m_xT, t + 1)
                for m in range(MC):
                    hb = [bank[1], bank[2], bank[0], bank[7]][2 * b + m // 3]
                    for c in range(KC):
                        mm = pe.matmul(hb[:, m % 3 * P:m % 3 * P + P], fc1[:, c, m * 128:(m + 1) * 128], xT[:, b, c, :],
                                       start=c == 0, stop=c == 1)
                mm.then_inc(s_m_h, 1)

            def mlp(t, b):
                if not at_last(t):
                    mlp_hidden(t + 1, 1 - b)
                wait_count(pe, s_m_out, 2 * t - 2)
                pe.wait_ge(s_m_g, t + 1)
                for m in range(MC):
                    pe.matmul(ps_h[b][0:P, 0:D], gT[:, b, m, :], fc2[:, m, :], start=m == 0, stop=False)
                pe.matmul(ps_h[b][0:P, 0:D], g["ones"][0:1, 0:P], fb2[:, :], start=False, stop=True).then_inc(s_m_y, 1)
            mlp_hidden(0, 0)
            over_tiles(pe, mlp)

        @block.scalar
        def _(act):
            act.wait_ge(s_var, 1)
            act.activation(g["rstd"][:, :], g["rstd"][:, :], ACT.Sqrt).then_inc(s_rstd, 1)

            def body(t, b):
                act.wait_ge(s_tr, t + 1)
                act.copy(xT[:, b, :, :], ps_t[b][:, 0:256].rearrange("p (c q) -> p c q", c=2)[:, :, 0:P]).then_inc(s_xT, 1)
                wait_count(act, s_st[b], (t - b) * 8)
                act.wait_ge(s_h, t + 1)
                act.copy(tab[:, b, :], ps_h[b][0:P, 0:TAB + NH])
                act.copy(tile_of(g["el"], t), ps_h[b][0:P, TAB:TAB + NH]).then_inc(s_tab, 1)
                act.wait_ge(s_tab, t + 1)
                act.dma_start(table_rows[bass.ds(t, 1), :, :].rearrange("o p f -> (o p) f"), tab[:, b, 0:TAB]).then_inc(s_st[b], 16)
            over_tiles(act, body)
            act.wait_ge(s_tr, T)
            for c in range(KC):
                cp = act.copy(gram[:, c, :], ps_g[c][:, 0:D + 1])
            cp.then_inc(s_gram, 1)
            act.wait_ge(s_fold_pe, 1)
            act.copy(grow[:, :], bank[0][0:1, 0:D]).then_inc(s_gram, 1)
            act.wait_ge(s_fold_pe, 2)
            for m in range(KC):
                cp = act.copy(gwv[:, m, :], bank[1 + m][:, 0:D])
            cp.then_inc(s_gram, 1)
            act.wait_ge(s_fold_pe, 3)
            act.copy(gwv_row[:, :], bank[7][0:1, 0:D]).then_inc(s_gram, 1)
            act.wait_ge(s_fold, 6)
            act.activation(logit[:, :, :], logit[:, :, :], ACT.Exp, scale=HD ** -0.5).then_inc(s_fold, 1)
            act.wait_ge(s_fold_pe, 5)
            act.copy(attnT[:, :, :], bank[0][:, 0:D].rearrange("p (c q) -> p c q", c=2)).then_inc(s_gram, 1)
            act.wait_ge(s_fold_pe, 6)
            for m in range(KC):
                act.copy(c0[:, m, :], bank[1 + m][:, 0:D])
            act.copy(c0_row[:, :], bank[7][0:1, 0:D]).then_inc(s_gram, 1)

            def attend(t, b):
                act.wait_ge(s_b_tr, t + 1)
                act.copy(xT[:, b, :, :], ps_t[b][:, 0:256].rearrange("p (c q) -> p c q", c=2)[:, :, 0:P]).then_inc(s_b_xT, 1)
            over_tiles(act, attend)
            act.wait_ge(s_m_var, 1)
            act.activation(rstd1[:, :], rstd1[:, :], ACT.Sqrt).then_inc(s_m_rstd, 1)

            def mlp(t, b):
                act.wait_ge(s_m_tr, t + 1)
                for c in range(KC):
                    cp = act.activation(xT[:, b, c, :], ps_t[b][:, c * 128:c * 128 + P], ACT.Identity,
                                        bias=lnT[:, 1, c:c + 1], scale=lnT[:, 0, c:c + 1])
                cp.then_inc(s_m_xT, 1)
                act.wait_ge(s_m_h, t + 1)
                for m in range(MC):
                    hb = [bank[1], bank[2], bank[0], bank[7]][2 * b + m // 3]
                    cp = act.activation(gT[:, b, m, :], hb[:, m % 3 * P:m % 3 * P + P], ACT.Gelu, bias=fb1[:, m:m + 1])
                cp.then_inc(s_m_g, 1)
            over_tiles(act, mlp)
            act.wait_ge(s_st[0], (T + 1) // 2 * 16)
            act.wait_ge(s_st[1], T // 2 * 16)


def node_tiles(nc, g, engine, q):
    _, tiles = nc.values_load_multi_w_load_instructions(
        g["edge_map"][0:1, bass.ds(q * 4, 8)], engines=(engine,), min_val=0, max_val=T - 1,
        skip_runtime_bounds_check_because="the map counts the bins that start before a slot: 0 to T - 1")
    return tiles


def edge_aggregation(nc, a, g, w_in):
    bank = g["bank"]
    G = 4
    RING = 8
    VR = 4
    NG = ET // G
    AHEAD = NE * KC - NG // RING
    agg = g["agg"]
    slots = g["slots"].rearrange("(p t) f -> p t f", p=SLOT)
    with Stage(nc, "D") as st:
        row_no = st.sb("row_no", [128, P])
        pay = st.sb("pay", [128, RING, G, PAY])
        hg = st.sb("hg", [128, RING, G, TAB])
        hot = st.sb("hot", [128, VR, G, P])
        hotT = st.sb("hotT", [P, 2, G, 128])
        attr = st.sb("attr", [128, 2, G * AT])
        attrT = st.sb("attrT", [128, 2, 128])
        wt = st.sb("wt", [128, G, HD])
        bt = st.sb("bt", [1, G, HD])
        z = st.sb("z", [128, 2, G, NH])
        val = st.sb("val", [128, VR, G, VW])
        blank = st.sb("blank", [128, FT * D // 8])
        s_blank, s_blanked = st.sem("blank"), st.sem("blanked")
        s_w, s_zero, s_start = st.sem("weights"), st.sem("zero"), st.sem("start")
        s_pay = st.sems("pay", RING)
        s_hg = st.sems("hg", RING)
        s_go, s_attr = st.sem("go"), st.sem("attr")
        s_hot, s_hotT_ps, s_hotT, s_at_ps, s_at, s_time, s_relu, s_el, s_z0, s_z, s_w_exp, s_val, s_main, s_agg = (
            st.sem(n) for n in ("hot", "hotT_psum", "hotT", "attrT_psum", "attrT", "time", "relu", "el",
                                "z_sum", "z", "w_exp", "val", "summed", "agg"))
        block = st.block()

        @block.sync
        def _(sp):
            sp.wait_ge(s_zero, 1)
            for j in range(G):
                sp.dma_start(wt[AT * j:AT * j + AT, j, :], a["L1_gnn_W_time_T"]).then_inc(s_w, 16)
                sp.dma_start(bt[:, j, :], a["L1_gnn_b_time"].unsqueeze(0)).then_inc(s_w, 16)
            sp.wait_ge(s_blank, 1)
            for c in range(8):
                sp.dma_start(g["xs"].rearrange("(p t) f -> p (t f)", p=SLOT)[:, c * (FT * D // 8):(c + 1) * (FT * D // 8)],
                             blank[:, :]).then_inc(s_blanked, 16)

            def load(q, r, b):
                wait_count(sp, s_val, q - RING + 1)
                sp.dma_start(pay[:, b, :, :], slots[:, bass.ds(q * G, G), :]).then_inc(s_pay[b], 16)
                if b == RING - 1:
                    if at_first(r):
                        for n in range(AHEAD + 1):
                            load_input_weights(sp, a, w_in, 0, n)
                    else:
                        load_input_weights(sp, a, w_in, 0, r + AHEAD)
            over_rounds(sp, load, NG // RING, RING)
            sp.wait_ge(s_blanked, 16 * 8)

        @block.gpsimd
        def _(gp):
            gp.memset(wt[:, :, :], 0.0).then_inc(s_zero, 1)
            gp.memset(blank[:, :], 0.0).then_inc(s_blank, 1)
            gp.iota(row_no[:, :], [[1, P]], base=0, channel_multiplier=0,
                    allow_small_or_imprecise_dtypes=True).then_inc(s_start, 1)
            gp.memset(agg[:, :, :], 0.0).then_inc(s_start, 1)
            gp.memset(val[:, :, :, O_C:O_C + 1], 1.0).then_inc(s_start, 1)

            def fetch(q, r, b):
                wait_count(gp, s_val, q - RING + 1)
                gp.wait_ge(s_pay[b], r * 16 + 16)
                gp.sem_inc(s_go, 1)
                for j in range(G):
                    gp.indirect_dma_start(hg[:, b, j, :], None, g["table"],
                                          bass.IndirectOffsetOnAxis(ap=pay[:, b, j, AT + 1:PAY].bitcast(I32), axis=0)
                                          ).then_inc(s_hg[b], 16)
            over_rounds(gp, fetch, NG // RING, RING)


        @block.vector
        def _(v):
            v.wait_ge(s_start, 3)

            def logits(q, r, b):
                v.wait_ge(s_hg[b], r * (16 * G) + 16 * G)
                v.wait_ge(s_el, q + 1)
                v.tensor_tensor(z[:, b % 2, :, :], bank[3][:, 0:G * NH].rearrange("p (j h) -> p j h", j=G),
                                hg[:, b, :, HD:TAB], ALU.add).then_inc(s_z0, 1)

            def leaky_relu(q, b):
                v.wait_ge(s_z0, q + 1)
                v.scalar_tensor_tensor(out=z[:, b % 2, :, :], in0=z[:, b % 2, :, :], scalar=0.2, in1=z[:, b % 2, :, :],
                                       op0=ALU.mult, op1=ALU.max).then_inc(s_z, 1)

            def make_hot(q, r, b):
                v.wait_ge(s_pay[b], r * 16 + 16)
                v.tensor_tensor(hot[:, b % VR, :, :], row_no[:, :].unsqueeze(1).broadcast_to([128, G, P]),
                                pay[:, b, :, AT:AT + 1].broadcast_to([128, G, P]), ALU.is_equal).then_inc(s_hot, 1)

            def values(q, b):
                p = b % VR
                v.wait_ge(s_w_exp, q + 1)
                v.tensor_tensor(val[:, p, :, 0:O_W].rearrange("p j (h f) -> p j h f", h=NH),
                                hg[:, b, :, 0:HD].unsqueeze(2).broadcast_to([128, G, NH, HD]),
                                val[:, p, :, O_W:O_T].unsqueeze(3).broadcast_to([128, G, NH, HD]),
                                ALU.mult).then_inc(s_val, 1)

            def add(q, window, j):
                v.wait_ge(s_main, q * G + j + 1)
                wait_count(v, s_agg, q * G + j)
                v.tensor_tensor(tile_of(agg, window[j]), tile_of(agg, window[j]), bank[4 + j][0:P, 0:VW],
                                ALU.add).then_inc(s_agg, 1)

            windows = [None]

            def step(s, r, b):
                last, sums = inside(s - 1, NG), inside(s - 2, NG)
                last_b = (b - 1) % RING
                if sums and b % 2 == 0:
                    windows[0] = node_tiles(nc, g, mybir.EngineType.DVE, s - 2)
                window = windows[0] and windows[0][b % 2 * G:]
                if last:
                    logits(s - 1, r if b else r - 1, last_b)
                if inside(s, NG):
                    make_hot(s, r, b)
                if sums:
                    add(s - 2, window, 0)
                if last:
                    leaky_relu(s - 1, last_b)
                if sums:
                    add(s - 2, window, 1)
                if last:
                    values(s - 1, last_b)
                if sums:
                    add(s - 2, window, 2)
                    add(s - 2, window, 3)
            over_rounds(v, step, NG // RING, RING, 2)

        @block.tensor
        def _(pe):
            pe.wait_ge(s_w, 32 * G)

            def sum_slots(q, b, tiles):
                if tiles[0] == 0:
                    pe.wait_ge(s_val, q + 1)
                    pe.wait_ge(s_relu, q + 1)
                for j in tiles:
                    wait_count(pe, s_agg, (q - 1) * G + j + 1)
                    pe.matmul(bank[4 + j][0:P, 0:VW], hot[:, b % VR, j, :], val[:, b % VR, j, :], start=True, stop=True
                              ).then_inc(s_main, 1)

            def transposes(q, b):
                p = b % 2
                wait_count(pe, s_at, q)
                pe.wait_ge(s_attr, q + 1)
                pe.transpose(bank[1][:, 0:128], attr[:, p, :], g["ident"][:, :]).then_inc(s_at_ps, 1)
                wait_count(pe, s_hotT, q)
                pe.wait_ge(s_hot, q + 1)
                for j in range(G):
                    mm = pe.transpose(bank[0][0:P, j * 128:(j + 1) * 128], hot[:, b % VR, j, :], g["ident"][:, :])
                mm.then_inc(s_hotT_ps, 1)

            def el_of_slots(q, b, window):
                wait_count(pe, s_z0, q)
                pe.wait_ge(s_hotT, q + 1)
                for j in range(G):
                    mm = pe.matmul(bank[3][:, j * NH:(j + 1) * NH], hotT[:, b % 2, j, :], tile_of(g["el"], window[j]),
                                   start=True, stop=True)
                mm.then_inc(s_el, 1)

            def features(q, b):
                wait_count(pe, s_relu, q)
                pe.wait_ge(s_at, q + 1)
                pe.matmul(bank[2][:, 0:G * HD], g["ones"][0:1, :], bt[:, :, :].rearrange("p j f -> p (j f)"), start=True, stop=False)
                pe.matmul(bank[2][:, 0:G * HD], attrT[:, b % 2, :], wt[:, :, :].rearrange("p j f -> p (j f)"),
                          start=False, stop=True).then_inc(s_time, 1)

            windows = [None]

            def step(s, r, b):
                if inside(s, NG) and b % 2 == 0:
                    windows[0] = node_tiles(nc, g, mybir.EngineType.PE, s)
                if inside(s - 2, NG):
                    sum_slots(s - 2, b - 2, (0, 1))
                if inside(s, NG):
                    transposes(s, b)
                if inside(s - 2, NG):
                    sum_slots(s - 2, b - 2, (2, 3))
                if inside(s, NG):
                    el_of_slots(s, b, windows[0][b % 2 * G:])
                    features(s, b)
            over_rounds(pe, step, NG // RING, RING, 2)

        @block.scalar
        def _(act):
            act.wait_ge(s_start, 3)

            def step(s, r, b):
                p = b % 2
                if inside(s, NG):
                    act.wait_ge(s_pay[b], r * 16 + 16)
                    act.copy(attr[:, p, :].rearrange("p (j f) -> p j f", j=G), pay[:, b, :, 0:AT]).then_inc(s_attr, 1)
                if inside(s - 1, NG):
                    act.wait_ge(s_z, s)
                    act.activation(val[:, (b - 1) % VR, :, O_W:O_T], z[:, 1 - p, :, :], ACT.Exp).then_inc(s_w_exp, 1)
                if inside(s, NG):
                    act.wait_ge(s_hotT_ps, s + 1)
                    act.copy(hotT[:, p, :, :], bank[0][0:P, :].rearrange("p (j s) -> p j s", j=G)).then_inc(s_hotT, 1)
                    act.wait_ge(s_at_ps, s + 1)
                    act.copy(attrT[:, p, :], bank[1][:, 0:128]).then_inc(s_at, 1)
                    act.wait_ge(s_time, s + 1)
                    act.activation(val[:, b % VR, :, O_T:O_C], bank[2][:, 0:G * HD].rearrange("p (j f) -> p j f", j=G),
                                   ACT.Relu).then_inc(s_relu, 1)
            over_rounds(act, step, NG // RING, RING, 1)


def gat_finish(nc, a, g):
    CH = 5
    agg, x = g["agg"], g["x"]
    with Stage(nc, "F") as st:
        den = st.sb("den", [P, T, NH])
        bias = st.sb("bias", [P, HD])
        low = st.sb("low", [P, T, NH * HD])
        s_b, s_den, s_o, s_low, s_exp, s_x = (st.sem(n) for n in ("bias", "den", "o", "low", "exp", "x"))
        block = st.block()

        @block.sync
        def _(sp):
            sp.dma_start(bias[:, :], a["L0_gnn_b"].unsqueeze(0).broadcast_to([P, HD])).then_inc(s_b, 16)

        @block.vector
        def _(v):
            v.tensor_copy(g["time"][:, :, :], agg[:, :, O_T:VW])
            v.tensor_scalar(den[:, :, :], agg[:, :, O_W:O_T], 1e-12, None, ALU.max).then_inc(s_den, 1)
            v.wait_ge(s_den, 1)
            v.reciprocal(den[:, :, :], den[:, :, :]).then_inc(s_den, 1)
            v.wait_ge(s_den, 2)
            v.wait_ge(s_b, 16)
            for c in range(T // CH):
                t = slice(c * CH, (c + 1) * CH)
                o = agg[:, t, 0:O_W].rearrange("p t (h f) -> p t h f", h=NH)
                v.tensor_tensor(o, o, den[:, t, :].unsqueeze(3).broadcast_to([P, CH, NH, HD]), ALU.mult).then_inc(s_o, 1)
                v.wait_ge(s_o, c * 2 + 1)
                v.tensor_tensor(o, o, bias[:, :].unsqueeze(1).unsqueeze(1).broadcast_to([P, CH, NH, HD]), ALU.add).then_inc(s_o, 1)
                v.wait_ge(s_o, c * 2 + 2)
                v.tensor_scalar(low[:, t, :], agg[:, t, 0:O_W], 0.0, None, ALU.min).then_inc(s_low, 1)
            for c in range(T // CH):
                t = slice(c * CH, (c + 1) * CH)
                v.wait_ge(s_exp, c + 1)
                v.scalar_tensor_tensor(out=low[:, t, :], in0=agg[:, t, 0:O_W], scalar=0.0, in1=low[:, t, :],
                                       op0=ALU.max, op1=ALU.add).then_inc(s_x, 1)
                v.wait_ge(s_x, c * 2 + 1)
                v.scalar_tensor_tensor(out=x[:, t, :], in0=low[:, t, :], scalar=-1.0, in1=x[:, t, :],
                                       op0=ALU.add, op1=ALU.add).then_inc(s_x, 1)

        @block.scalar
        def _(act):
            for c in range(T // CH):
                t = slice(c * CH, (c + 1) * CH)
                act.wait_ge(s_low, c + 1)
                act.activation(low[:, t, :], low[:, t, :], ACT.Exp).then_inc(s_exp, 1)


def input_weights(st, layer):
    width = H0 if layer == 0 else 2 * H1
    t = st.sb("w_in", [128, NE * KC, width])
    return dict(t=t, sem=st.sem("w_in"), loads=NE * KC if layer == 0 else 2 * NE * KC)


def load_input_weights(eng, a, w, layer, n):
    for name, c, width in ((("L0_ffn_W1_T", 0, H0),) if layer == 0 else (("L1_ffn_w1_T", 0, H1), ("L1_ffn_w3_T", H1, H1))):
        rows = a[name].rearrange("e (k p) f -> p (e k) f", p=128)
        eng.dma_start(w["t"][:, bass.ds(n, 1), c:c + width], rows[:, bass.ds(n, 1), :]).then_inc(w["sem"], 16)


def moe(nc, a, g, layer, w_in, out=None):
    with Stage(nc, f"M{layer}") as keep:
        w_out = dict(t=keep.sb("w_out", [128, NE, H0 // 128 if layer == 0 else H1C, D]), sem=keep.sem("w_out"),
                     loads=NE * 1 + 2 if layer == 0 else NE * 2)
        if layer == 0:
            w_out["b1"] = keep.sb("b1", [128, NE, H0 // 128])
            w_out["b2"] = keep.sb("b2", [SLOT, NE, D])
        slot = keep.sb("slot", [P, T, TOPK], I32)
        prob = keep.sb("prob", [P, T, TOPK])
        tile_map = keep.sb("tile_map", [1, FT], I32)
        route(nc, a, g, layer, slot, prob, tile_map, w_out)
        experts(nc, a, g, layer, w_in, w_out, tile_map)
        combine(nc, g, slot, prob, out)


def load_output_weights(eng, a, w, layer):
    if layer == 0:
        eng.dma_start(w["b1"][:, :, :].rearrange("p e c -> p (e c)"), a["L0_ffn_b1_cols"]).then_inc(w["sem"], 16)
        eng.dma_start(w["b2"][:, :, :], a["L0_ffn_b2"].unsqueeze(0).broadcast_to([SLOT, NE, D])).then_inc(w["sem"], 16)
    for e in range(NE):
        if layer == 0:
            eng.dma_start(w["t"][:, e, :, :], a["L0_ffn_W2_T"][e].rearrange("(k p) f -> p k f", p=128)).then_inc(w["sem"], 16)
        else:
            full = (H1C - 1) * 128
            eng.dma_start(w["t"][:, e, 0:H1C - 1, :], a["L1_ffn_w2_T"][e, 0:full].rearrange("(k p) f -> p k f", p=128)
                          ).then_inc(w["sem"], 16)
            eng.dma_start(w["t"][0:H1 - full, e, H1C - 1, :], a["L1_ffn_w2_T"][e, full:H1]).then_inc(w["sem"], 16)


def route(nc, a, g, layer, slot, prob, tile_map, w_out):
    bank, x = g["bank"], g["x"]
    with Stage(nc, f"R{layer}") as st:
        stats = st.sb("stats", [P, T, 6])
        xn = st.sb("xn", [P, 2, D])
        xT = st.sb("xT", [128, 2, KC, P])
        wg = st.sb("wg", [128, KC, NE])
        bg = st.sb("bg", [1, NE])
        score = st.sb("score", [P, T, NE])
        best = st.sb("best", [P, T, NE])
        rest = st.sb("rest", [P, T, NE])
        top = st.sb("top", [P, T, TOPK])
        expert = st.sb("expert", [P, T, TOPK])
        psum_p = st.sb("psum_p", [P, T])
        k = bins_buffers(st, NE, T * TOPK)
        narrow = st.sb("narrow", [1, FT])
        wide = st.sb("wide", [1, FT, NE - 1])
        xr = st.sb("xr", [P, 4, D])
        ids = st.sb("ids", [P, 4, TOPK], I32)
        s_w = st.sem("weights")
        s_ln, s_var, s_rstd, s_xn, s_tr, s_xT, s_sc, s_sb, s_top, s_p, s_exp, s_ready, s_row, s_go = (
            st.sem(n) for n in ("ln", "var", "rstd", "xn", "transposed", "xT", "scored", "score_sb", "top", "prob",
                                "exp", "ready", "row", "go"))
        s_sent = st.sems("sent", 4)
        block = st.block()

        @block.sync
        def _(sp):
            if layer == 0:
                sp.dma_start(wg[:, :, :], a["L0_ffn_Wg_T"].rearrange("(k p) f -> p k f", p=128)).then_inc(s_w, 16)
                sp.dma_start(bg[:, :], a["L0_ffn_bg"].unsqueeze(0)).then_inc(s_w, 16)
            else:
                sp.dma_start(wg[:, :, :], a["L1_ffn_router_w_T"].rearrange("(k p) f -> p k f", p=128)).then_inc(s_w, 16)
            load_output_weights(sp, a, w_out, layer)

        @block.gpsimd
        def _(gp):
            def send(t, r, b):
                gp.wait_ge(s_row, t + 1)
                gp.sem_inc(s_go, 1)
                for c in range(TOPK):
                    gp.indirect_dma_start(g["xs"], bass.IndirectOffsetOnAxis(ap=ids[:, b, c:c + 1], axis=0),
                                          xr[:, b, :], None).then_inc(s_sent[b], 16)
            over_rounds(gp, send, T // 4, 4, T % 4)
            for b in range(4):
                gp.wait_ge(s_sent[b], (T // 4 + (b == 0)) * 16 * TOPK)

        @block.vector
        def _(v):
            layer_stats(v, x, stats, g["mv"], g["rstd"], s_ln, s_var)
            v.wait_ge(s_rstd, 1)

            def normalise(t, b):
                wait_count(v, s_tr, t - 1)
                v.tensor_scalar(xn[:, b, :], tile_of(x, t), tile_of(g["mv"], t)[:, 0:1], g["rstd"][:, bass.ds(t, 1)],
                                ALU.subtract, ALU.mult).then_inc(s_xn, 1)

            def score_tile(t, b):
                if inside(t + 2, T):
                    normalise(t + 2, b)
                v.wait_ge(s_sc, t + 1)
                v.tensor_copy(tile_of(score, t), bank[2 + b][0:P, 0:NE]).then_inc(s_sb, 1)
            normalise(0, 0)
            normalise(1, 1)
            over_tiles(v, score_tile, T, 4)

            v.wait_ge(s_sb, T)
            number = g["bin_no"][0:P, 0:NE].unsqueeze(1).broadcast_to([P, T, NE])
            for c in range(TOPK):
                from_ = score if c == 0 else rest
                n = c * 7
                v.tensor_reduce(top[:, :, c], from_[:, :, :], AXX, ALU.max).then_inc(s_top, 1)
                v.wait_ge(s_top, n + 1)
                v.tensor_tensor(best[:, :, :], from_[:, :, :], top[:, :, c].unsqueeze(2).broadcast_to([P, T, NE]),
                                ALU.is_equal).then_inc(s_top, 1)
                v.wait_ge(s_top, n + 2)
                v.scalar_tensor_tensor(out=best[:, :, :], in0=best[:, :, :], scalar=-float(2 * NE), in1=number,
                                       op0=ALU.mult, op1=ALU.add).then_inc(s_top, 1)
                v.wait_ge(s_top, n + 3)
                v.tensor_reduce(expert[:, :, c], best[:, :, :], AXX, ALU.min).then_inc(s_top, 1)
                v.wait_ge(s_top, n + 4)
                v.tensor_scalar(expert[:, :, c], expert[:, :, c], float(2 * NE), None, ALU.add).then_inc(s_top, 1)
                v.wait_ge(s_top, n + 5)
                if c == 0:
                    v.tensor_tensor(best[:, :, :], number, expert[:, :, c].unsqueeze(2).broadcast_to([P, T, NE]),
                                    ALU.is_equal).then_inc(s_top, 1)
                    v.wait_ge(s_top, n + 6)
                    v.scalar_tensor_tensor(out=rest[:, :, :], in0=best[:, :, :], scalar=-3e38, in1=score[:, :, :],
                                           op0=ALU.mult, op1=ALU.add).then_inc(s_top, 1)
                    v.wait_ge(s_top, n + 7)
            if layer == 1:
                v.tensor_tensor(score[:, :, :], score[:, :, :], top[:, :, 0].unsqueeze(2).broadcast_to([P, T, NE]),
                                ALU.subtract).then_inc(s_p, 1)
            v.tensor_tensor(prob[:, :, :], top[:, :, :], top[:, :, 0].unsqueeze(2).broadcast_to([P, T, TOPK]),
                            ALU.subtract).then_inc(s_p, 1)
            n = 1 + layer
            v.wait_ge(s_exp, n)
            if layer == 1:
                v.tensor_reduce(psum_p[:, :], score[:, :, :], AXX, ALU.add).then_inc(s_p, 1)
                v.wait_ge(s_p, n + 1)
                v.reciprocal(psum_p[:, :], psum_p[:, :]).then_inc(s_p, 1)
                v.wait_ge(s_p, n + 2)
                v.tensor_tensor(prob[:, :, :], prob[:, :, :], psum_p[:, :].unsqueeze(2).broadcast_to([P, T, TOPK]),
                                ALU.mult).then_inc(s_p, 1)
                n += 3
                v.wait_ge(s_p, n)
            v.tensor_tensor(psum_p[:, :], prob[:, :, 0], prob[:, :, 1], ALU.add).then_inc(s_p, 1)
            v.wait_ge(s_p, n + 1)
            if layer == 1:
                v.tensor_scalar(psum_p[:, :], psum_p[:, :], 1e-9, None, ALU.add).then_inc(s_p, 1)
                n += 1
                v.wait_ge(s_p, n + 1)
            v.reciprocal(psum_p[:, :], psum_p[:, :]).then_inc(s_p, 1)
            v.wait_ge(s_p, n + 2)
            v.tensor_tensor(prob[:, :, :], prob[:, :, :], psum_p[:, :].unsqueeze(2).broadcast_to([P, T, TOPK]),
                            ALU.mult).then_inc(s_p, 1)
            bins_vector(v, k, expert[:, :, :].rearrange("p t k -> p (t k)"), g["bin_no"], g["ones"], NE, T * TOPK,
                        bank[0], ((0, T * TOPK),), None, tile_map[:, :], FT, g["tile_at"], narrow[:, :], wide[:, :, :], s_ready)
            v.tensor_copy(slot[:, :, :].rearrange("p t k -> p (t k)"), k["posf"][:, :]).then_inc(s_p, 1)
            v.wait_ge(s_p, n + 4)

            def rows(t, r, b):
                wait_count(v, s_sent[b], r * (16 * TOPK))
                v.tensor_copy(ids[:, b, :], tile_of(slot, t))
                v.tensor_scalar(xr[:, b, :], tile_of(x, t), tile_of(g["mv"], t)[:, 0:1], g["rstd"][:, bass.ds(t, 1)],
                                ALU.subtract, ALU.mult).then_inc(s_row, 1)
            over_rounds(v, rows, T // 4, 4, T % 4)

        @block.tensor
        def _(pe):
            pe.wait_ge(s_w, 32 - 16 * layer)

            def turn(t, b):
                wait_count(pe, s_xT, t - 1)
                pe.wait_ge(s_xn, t + 1)
                for c in range(KC):
                    mm = pe.transpose(bank[4 + b][:, c * 128:c * 128 + P], xn[:, b, c * 128:(c + 1) * 128], g["ident"][0:P, 0:P])
                mm.then_inc(s_tr, 1)

            def score_tile(t, b):
                if not at_last(t):
                    turn(t + 1, 1 - b)
                wait_count(pe, s_sb, t - 1)
                pe.wait_ge(s_xT, t + 1)
                for c in range(KC):
                    mm = pe.matmul(bank[2 + b][0:P, 0:NE], xT[:, b, c, :], wg[:, c, :], start=c == 0,
                                   stop=c == 1 and layer == 1)
                if layer == 0:
                    mm = pe.matmul(bank[2 + b][0:P, 0:NE], g["ones"][0:1, 0:P], bg[:, :], start=False, stop=True)
                mm.then_inc(s_sc, 1)
            turn(0, 0)
            over_tiles(pe, score_tile)
            bins_tensor(pe, k, g["before"], g["ones"], NE, bank[0])

        @block.scalar
        def _(act):
            act.wait_ge(s_var, 1)
            act.activation(g["rstd"][:, :], g["rstd"][:, :], ACT.Sqrt).then_inc(s_rstd, 1)

            def score_tile(t, b):
                act.wait_ge(s_tr, t + 1)
                act.copy(xT[:, b, :, :], bank[4 + b][:, 0:256].rearrange("p (c q) -> p c q", c=2)[:, :, 0:P]).then_inc(s_xT, 1)
            over_tiles(act, score_tile)
            act.wait_ge(s_p, 1 + layer)
            if layer == 1:
                act.activation(score[:, :, :], score[:, :, :], ACT.Exp).then_inc(s_exp, 1)
            act.activation(prob[:, :, :], prob[:, :, :], ACT.Exp).then_inc(s_exp, 1)


def experts(nc, a, g, layer, w_in, w_out, tile_map):
    bank = g["bank"]
    HB = [bank[0], bank[1]] if layer == 0 else [bank[0], bank[1], bank[2], bank[3]]
    HC = H0 // 128 if layer == 0 else H1C
    tb, yb = ([bank[4], bank[5]], bank[6])
    xb = bank[7]
    xs = g["xs"].rearrange("(t p) f -> t p f", p=SLOT)
    ys = g["ys"].rearrange("(t p) f -> t p f", p=SLOT)
    HW = H0 if layer == 0 else H1
    chunks = [(c * 128, min(128, HW - c * 128)) for c in range(HC)]
    with Stage(nc, f"E{layer}") as st:
        xt = st.sb("xt", [SLOT, 2, D])
        xT = st.sb("xT", [128, 2, KC, SLOT])
        h = st.sb("h", [SLOT, HW])
        hT = st.sb("hT", [128, 2, HC, SLOT])
        y = st.sb("y", [SLOT, 2, D])
        s_x, s_st = st.sems("x"), st.sems("stored")
        s_tr, s_xT, s_h, s_hs, s_hd, s_hTp, s_hT, s_y, s_ys = (st.sem(n) for n in (
            "x_transposed", "xT", "h", "h_gate", "h_sb", "h_transposed", "hT", "y", "y_sb"))
        block = st.block()

        @block.sync
        def _(sp):
            def load(t, b):
                wait_count(sp, s_tr, t - 1)
                sp.dma_start(xt[:, b, :], xs[bass.ds(t, 1), :, :].rearrange("o p f -> (o p) f")).then_inc(s_x[b], 16)

            def tile(t, b):
                if inside(t + 3, FT):
                    load(t + 3, 1 - b)
                sp.wait_ge(s_ys, t + 1)
                sp.dma_start(ys[bass.ds(t, 1), :, :].rearrange("o p f -> (o p) f"), y[:, b, :]).then_inc(s_st[b], 16)
            for t in range(3):
                load(t, t % 2)
            over_tiles(sp, tile, FT, 4)
            sp.wait_ge(s_st[0], FT // 2 * 16)
            sp.wait_ge(s_st[1], FT // 2 * 16)


        @block.tensor
        def _(pe):
            def turn(t, b):
                pe.wait_ge(s_x[b], (t - b) * 8 + 16)
                wait_count(pe, s_xT, t)
                for c in range(KC):
                    mm = pe.transpose(xb[:, c * 128:(c + 1) * 128], xt[:, b, c * 128:(c + 1) * 128], g["ident"][:, :])
                mm.then_inc(s_tr, 1)

            def hidden(t, b):
                e = pe.value_load(tile_map[0:1, bass.ds(t, 1)], min_val=0, max_val=NE - 1)
                pe.wait_ge(s_xT, t + 1)
                for n, hb in enumerate(HB):
                    if layer == 0:
                        c0, w = n * 512, 512
                    else:
                        c0, w = n // 2 * H1 + n % 2 * (H1 // 2), H1 // 2
                    for c in range(KC):
                        mm = pe.matmul(hb[:, 0:w], xT[:, b, c, :], w_in["t"][:, bass.ds(e * KC + c, 1), c0:c0 + w].rearrange("p o f -> p (o f)"),
                                       start=c == 0, stop=c == 1)
                mm.then_inc(s_h, 1)

            def tile(t, b):
                pe.wait_ge(s_hd, t + 1)
                wait_count(pe, s_hT, t)
                for n, (c0, w) in enumerate(chunks):
                    mm = pe.transpose(tb[n // 4][0:w, n % 4 * 128:n % 4 * 128 + SLOT], h[:, c0:c0 + w], g["ident"][:, :])
                mm.then_inc(s_hTp, 1)
                if inside(t + 2, FT):
                    turn(t + 2, b)
                if inside(t + 1, FT):
                    hidden(t + 1, 1 - b)
                e = pe.value_load(tile_map[0:1, bass.ds(t, 1)], min_val=0, max_val=NE - 1)
                wait_count(pe, s_ys, t)
                pe.wait_ge(s_hT, t + 1)
                for n, (c0, w) in enumerate(chunks):
                    mm = pe.matmul(yb[:, 0:D], hT[0:w, b, n, :], w_out["t"][0:w, bass.ds(e, 1), n, :].rearrange("p o f -> p (o f)"),
                                   start=n == 0, stop=n == HC - 1)
                mm.then_inc(s_y, 1)
            turn(0, 0)
            turn(1, 1)
            pe.wait_ge(w_in["sem"], 16 * w_in["loads"])
            hidden(0, 0)
            pe.wait_ge(w_out["sem"], 16 * w_out["loads"])
            over_tiles(pe, tile, FT, 4)

        @block.vector
        def _(v):
            def gate(t):
                wait_count(v, s_hTp, t)
                if layer == 0:
                    v.wait_ge(s_h, t + 1)
                    for n, hb in enumerate(HB):
                        o = v.tensor_copy(h[:, n * 512:(n + 1) * 512], hb[:, :])
                else:
                    v.wait_ge(s_hs, t + 1)
                    for n in range(2):
                        half = slice(n * (H1 // 2), (n + 1) * (H1 // 2))
                        o = v.tensor_tensor(h[:, half], h[:, half], HB[2 + n][:, 0:H1 // 2], ALU.mult)
                o.then_inc(s_hd, 1)

            def tile(t, b):
                if inside(t + 1, FT):
                    gate(t + 1)
                if layer == 0:
                    e = v.value_load(tile_map[0:1, bass.ds(t, 1)], min_val=0, max_val=NE - 1)
                wait_count(v, s_st[b], (t - b) * 8)
                v.wait_ge(s_y, t + 1)
                if layer == 0:
                    v.tensor_tensor(y[:, b, :], yb[:, 0:D], tile_of(w_out["b2"], e), ALU.add).then_inc(s_ys, 1)
                else:
                    v.tensor_copy(y[:, b, :], yb[:, 0:D]).then_inc(s_ys, 1)
            gate(0)
            v.wait_ge(w_out["sem"], 16 * w_out["loads"])
            over_tiles(v, tile, FT, 4)

        @block.scalar
        def _(act):
            act.wait_ge(w_out["sem"], 16 * w_out["loads"])

            def turned(t, b):
                act.wait_ge(s_tr, t + 1)
                act.copy(xT[:, b, :, :], xb[:, 0:D].rearrange("p (c q) -> p c q", c=2)).then_inc(s_xT, 1)

            def silu(t):
                wait_count(act, s_hTp, t)
                act.wait_ge(s_h, t + 1)
                for n in range(2):
                    o = act.activation(h[:, n * (H1 // 2):(n + 1) * (H1 // 2)], HB[n][:, 0:H1 // 2], ACT.Silu)
                o.then_inc(s_hs, 1)

            def tile(t, b):
                if layer == 0:
                    e = act.value_load(tile_map[0:1, bass.ds(t, 1)], min_val=0, max_val=NE - 1)
                act.wait_ge(s_hTp, t + 1)
                if layer == 0:
                    for n in range(HC):
                        o = act.activation(hT[:, b, n, :], tb[n // 4][:, n % 4 * 128:(n % 4 + 1) * 128], ACT.Relu,
                                           bias=tile_of(w_out["b1"], e)[:, n:n + 1])
                else:
                    w = H1 - (HC - 1) * 128
                    act.copy(hT[:, b, 0:4, :], tb[0][:, :].rearrange("p (c q) -> p c q", c=4))
                    act.copy(hT[:, b, 4, :], tb[1][:, 0:128])
                    o = act.copy(hT[0:w, b, 5, :], tb[1][0:w, 128:256])
                o.then_inc(s_hT, 1)
                if inside(t + 2, FT):
                    turned(t + 2, b)
                if layer == 1 and inside(t + 1, FT):
                    silu(t + 1)
            turned(0, 0)
            turned(1, 1)
            if layer == 1:
                silu(0)
            over_tiles(act, tile, FT, 4)


def combine(nc, g, slot, prob, out):
    x = g["x"]
    R = 4
    with Stage(nc, "C" + ("o" if out is not None else "x")) as st:
        yg = st.sb("yg", [P, R, TOPK, D])
        ids = st.sb("ids", [P, R, TOPK], I32)
        s_y = st.sems("y", R)
        s_x0, s_x, s_ids, s_go, s_out = st.sem("x0"), st.sem("x"), st.sem("ids"), st.sem("go"), st.sem("out")
        block = st.block()

        @block.gpsimd
        def _(gp):
            def fetch(t, r, b):
                wait_count(gp, s_x, t - R + 1)
                gp.tensor_copy(ids[:, b, :], tile_of(slot, t)).then_inc(s_ids, 1)
                gp.wait_ge(s_ids, t + 1)
                gp.sem_inc(s_go, 1)
                for c in range(TOPK):
                    gp.indirect_dma_start(yg[:, b, c, :], None, g["ys"],
                                          bass.IndirectOffsetOnAxis(ap=ids[:, b, c:c + 1], axis=0)).then_inc(s_y[b], 16)
            over_rounds(gp, fetch, T // R, R, T % R)

        @block.vector
        def _(v):
            def add(t, r, b):
                v.wait_ge(s_y[b], r * (16 * TOPK) + 16 * TOPK)
                v.scalar_tensor_tensor(out=tile_of(x, t), in0=yg[:, b, 0, :], scalar=tile_of(prob, t)[:, 0:1],
                                       in1=tile_of(x, t), op0=ALU.mult, op1=ALU.add).then_inc(s_x0, 1)
                v.wait_ge(s_x0, t + 1)
                v.scalar_tensor_tensor(out=tile_of(x, t), in0=yg[:, b, 1, :], scalar=tile_of(prob, t)[:, 1:2],
                                       in1=tile_of(x, t), op0=ALU.mult, op1=ALU.add).then_inc(s_x, 1)
            over_rounds(v, add, T // R, R, T % R)

        if out is not None:
            rows = out.rearrange("(t p) f -> t p f", p=P)

            @block.sync
            def _(sp):
                with sp.Fori(0, T) as t:
                    sp.wait_ge(s_x, t + 1)
                    sp.dma_start(rows[bass.ds(t, 1), :, :].rearrange("o p f -> (o p) f"), tile_of(x, t)).then_inc(s_out, 16)
                sp.wait_ge(s_out, T * 16)


L1H = 8
KV = L1H * HD


def l1_keys_values(nc, a, g, w_in):
    bank, x = g["bank"], g["x"]
    with Stage(nc, "K") as st:
        wkv = st.sb("wkv", [128, KC, 2 * KV])
        mean = st.sb("mean", [128, KC, 2 * L1H])
        wq = st.sb("wq", [128, KV // 128, D])
        wo = st.sb("wo", [128, KV // 128, D])
        xn = st.sb("xn", [P, 2, D])
        xT = st.sb("xT", [128, 2, KC, P])
        sq = st.sb("sq", [P, 2 * KV])
        var = st.sb("var", [P, 2, 2 * L1H])
        kvn = st.sb("kvn", [P, 2, 2 * KV])
        stats = st.sb("stats", [P, T, 6])
        dots = st.sb("dots", [128, KV // 128, 128])
        gm = st.sb("gm", [128, KV // 128, D])
        s_w, s_cw, s_zero = st.sem("weights"), st.sem("centred"), st.sem("zero")
        s_ln, s_var, s_rstd, s_xn, s_tr, s_xT, s_kv, s_sq, s_v1, s_root, s_r1, s_kvn, s_dot, s_dsb, s_g, s_gsb, s_c = (
            st.sem(n) for n in ("ln", "var", "rstd", "xn", "transposed", "xT", "kv", "squares", "kv_var", "kv_root",
                                "kv_rstd", "kv_normed", "dots", "dots_sb", "gm_psum", "gm", "c1"))
        block = st.block()

        @block.sync
        def _(sp):
            sp.dma_start(wkv[:, :, :], a["L1_mix_w_kv_T"].rearrange("(k p) f -> p k f", p=128)).then_inc(s_w, 16)
            sp.dma_start(wq[:, :, :], a["L1_mix_w_qkv"][0:KV].rearrange("(k p) f -> p k f", p=128)).then_inc(s_w, 16)
            sp.dma_start(wo[:, :, :], a["L1_mix_w_out_T"].rearrange("(k p) f -> p k f", p=128)).then_inc(s_w, 16)
            for n in range(NE * KC):
                load_input_weights(sp, a, w_in, 1, n)

        @block.gpsimd
        def _(gp):
            gp.memset(dots[:, :, :], 0.0).then_inc(s_zero, 1)

        @block.vector
        def _(v):
            layer_stats(v, x, stats, g["mv"], g["rstd"], s_ln, s_var)
            v.wait_ge(s_w, 48)
            heads = wkv[:, :, :].rearrange("p k (h f) -> p (k h) f", f=HD)
            m = mean[:, :, :].rearrange("p k h -> p (k h)")
            v.tensor_reduce(m, heads, AXX, ALU.add).then_inc(s_cw, 1)
            v.wait_ge(s_cw, 1)
            v.tensor_scalar(m, m, 1.0 / HD, None, ALU.mult).then_inc(s_cw, 1)
            v.wait_ge(s_cw, 2)
            v.tensor_tensor(heads, heads, m.unsqueeze(2).broadcast_to([128, KC * 2 * L1H, HD]), ALU.subtract).then_inc(s_cw, 1)
            v.wait_ge(s_rstd, 1)

            def normalise(t, b):
                wait_count(v, s_tr, t)
                v.tensor_scalar(xn[:, b, :], tile_of(x, t), tile_of(g["mv"], t)[:, 0:1], g["rstd"][:, bass.ds(t, 1)],
                                ALU.subtract, ALU.mult).then_inc(s_xn, 1)

            def tile(t, b):
                if not at_last(t):
                    normalise(t + 1, 1 - b)
                v.wait_ge(s_sq, t + 1)
                v.tensor_reduce(var[:, b, :], sq[:, :].rearrange("p (h f) -> p h f", f=HD), AXX, ALU.add).then_inc(s_v1, 1)
                v.wait_ge(s_v1, t * 2 + 1)
                v.tensor_scalar(var[:, b, :], var[:, b, :], 1.0 / HD, EPS, ALU.mult, ALU.add).then_inc(s_v1, 1)
                v.wait_ge(s_v1, t * 2 + 2)
                v.reciprocal(var[:, b, :], var[:, b, :]).then_inc(s_root, 1)
                v.wait_ge(s_r1, t + 1)
                wait_count(v, s_dot, t - 1)
                for n in range(2):
                    o = v.tensor_tensor(kvn[:, b, n * KV:(n + 1) * KV].rearrange("p (h f) -> p h f", f=HD),
                                        bank[2 * n + b][0:P, :].rearrange("p (h f) -> p h f", f=HD),
                                        var[:, b, n * L1H:(n + 1) * L1H].unsqueeze(2).broadcast_to([P, L1H, HD]), ALU.mult)
                o.then_inc(s_kvn, 1)
            normalise(0, 0)
            over_tiles(v, tile)
            v.wait_ge(s_dot, T)
            v.wait_ge(s_zero, 1)
            for h in range(L1H):
                r = slice(h % 2 * HD, h % 2 * HD + HD)
                o = v.tensor_copy(dots[r, h // 2, r], bank[5][r, h // 2 * 128 + h % 2 * HD:h // 2 * 128 + h % 2 * HD + HD])
            o.then_inc(s_dsb, 1)

        @block.tensor
        def _(pe):
            pe.wait_ge(s_cw, 3)

            def turn(t, b):
                wait_count(pe, s_xT, t)
                pe.wait_ge(s_xn, t + 1)
                for c in range(KC):
                    mm = pe.transpose(bank[4][:, c * 128:c * 128 + P], xn[:, b, c * 128:(c + 1) * 128], g["ident"][0:P, 0:P])
                mm.then_inc(s_tr, 1)

            def keys(t, b):
                pe.wait_ge(s_xT, t + 1)
                wait_count(pe, s_kvn, t - 1)
                for n in range(2):
                    for c in range(KC):
                        mm = pe.matmul(bank[2 * n + b][0:P, :], xT[:, b, c, :], wkv[:, c, n * KV:(n + 1) * KV],
                                       start=c == 0, stop=c == 1)
                mm.then_inc(s_kv, 1)

            def tile(t, b):
                if not at_last(t):
                    turn(t + 1, 1 - b)
                    keys(t + 1, 1 - b)
                pe.wait_ge(s_kvn, t + 1)
                for j in range(KV // 128):
                    mm = pe.matmul(bank[5][:, j * 128:(j + 1) * 128], kvn[:, b, KV + j * 128:KV + (j + 1) * 128],
                                   kvn[:, b, j * 128:(j + 1) * 128], start=at_first(t) and j == 0, stop=at_last(t), skip_group_check=True)
                mm.then_inc(s_dot, 1)
            turn(0, 0)
            keys(0, 0)
            over_tiles(pe, tile)
            pe.wait_ge(s_dsb, 1)
            for j in range(KV // 128):
                mm = pe.matmul(bank[6 + j // 2][:, j % 2 * D:(j % 2 + 1) * D], dots[:, j, :], wo[:, j, :], start=True, stop=True)
            mm.then_inc(s_g, 1)
            pe.wait_ge(s_gsb, 1)
            for m in range(KC):
                for j in range(KV // 128):
                    mm = pe.matmul(bank[m][:, 0:D], wq[:, j, m * 128:(m + 1) * 128], gm[:, j, :], start=j == 0, stop=j == 3)
            mm.then_inc(s_c, 1)

        @block.scalar
        def _(act):
            act.wait_ge(s_var, 1)
            act.activation(g["rstd"][:, :], g["rstd"][:, :], ACT.Sqrt).then_inc(s_rstd, 1)

            def turned(t, b):
                act.wait_ge(s_tr, t + 1)
                act.copy(xT[:, b, :, :], bank[4][:, 0:256].rearrange("p (c q) -> p c q", c=2)[:, :, 0:P]).then_inc(s_xT, 1)

            def tile(t, b):
                act.wait_ge(s_kv, t + 1)
                wait_count(act, s_v1, t * 2)
                for n in range(2):
                    o = act.activation(sq[:, n * KV:(n + 1) * KV], bank[2 * n + b][0:P, :], ACT.Square)
                o.then_inc(s_sq, 1)
                if not at_last(t):
                    turned(t + 1, 1 - b)
                act.wait_ge(s_root, t + 1)
                act.activation(var[:, b, :], var[:, b, :], ACT.Sqrt).then_inc(s_r1, 1)
            turned(0, 0)
            over_tiles(act, tile)
            act.wait_ge(s_g, 1)
            for j in range(2):
                o = act.copy(gm[:, 2 * j:2 * j + 2, :], bank[6 + j][:, :].rearrange("p (k f) -> p k f", k=2))
            o.then_inc(s_gsb, 1)
            act.wait_ge(s_c, 1)
            for m in range(KC):
                act.activation(g["c1"][:, m, :], bank[m][:, 0:D], ACT.Copy, scale=1.0 / N)


def l1_update(nc, a, g):
    bank, x = g["bank"], g["x"]
    with Stage(nc, "U") as st:
        wd = st.sb("wd", [128, KC, HD])
        wf = st.sb("wf", [2 * HD, HD])
        wu = st.sb("wu", [HD, D])
        bd = st.sb("bd", [HD, 1])
        bf = st.sb("bf", [HD, 1])
        bo = st.sb("bo", [2, D])
        xn = st.sb("xn", [P, 2, D])
        xT = st.sb("xT", [128, 2, KC, P])
        tm = st.sb("tm", [P, 2, HD])
        rc = st.sb("rc", [P, T])
        nf = st.sb("nf", [2 * HD, 2, P])
        fu = st.sb("fu", [HD, 2, P])
        s_w = st.sem("weights")
        s_rc, s_xn, s_tr, s_xT, s_nf_ps, s_nf, s_fu_ps, s_fu, s_o, s_x0, s_x = (st.sem(n) for n in (
            "rcount", "xn", "transposed", "xT", "nf_psum", "nf", "fused_psum", "fused", "out", "x0", "x"))
        block = st.block()

        @block.sync
        def _(sp):
            for dst, src in ((wd[:, :, :], a["L1_gnn_W_down_T"].rearrange("(k p) f -> p k f", p=128)),
                             (wf[:, :], a["L1_gnn_W_fusion_T"]),
                             (wu[:, :], a["L1_gnn_W_up_T"]), (bd[:, :], a["L1_gnn_b_down_col"]),
                             (bf[:, :], a["L1_gnn_b_fusion_col"]), (bo[0:1, :], a["L1_gnn_b_up"].unsqueeze(0)),
                             (bo[1:2, :], a["L1_mix_b_out"].unsqueeze(0))):
                sp.dma_start(dst, src).then_inc(s_w, 16)

        @block.vector
        def _(v):
            v.tensor_scalar(rc[:, :], g["time"][:, :, HD], 1.0, None, ALU.max).then_inc(s_rc, 1)
            v.wait_ge(s_rc, 1)
            v.reciprocal(rc[:, :], rc[:, :]).then_inc(s_rc, 1)
            v.wait_ge(s_rc, 2)

            def prepare(t, b):
                wait_count(v, s_tr, t)
                v.tensor_scalar(xn[:, b, :], tile_of(x, t), tile_of(g["mv"], t)[:, 0:1], g["rstd"][:, bass.ds(t, 1)],
                                ALU.subtract, ALU.mult)
                v.tensor_scalar(tm[:, b, :], tile_of(g["time"], t)[:, 0:HD], rc[:, bass.ds(t, 1)], None, ALU.mult).then_inc(s_xn, 1)

            def tile(t, b):
                v.wait_ge(s_xn, t + 1)
                v.tensor_tensor(tile_of(x, t), tile_of(x, t), xn[:, b, :], ALU.add).then_inc(s_x0, 1)
                if not at_last(t):
                    prepare(t + 1, 1 - b)
                v.wait_ge(s_x0, t + 1)
                v.wait_ge(s_o, t + 1)
                v.tensor_tensor(tile_of(x, t), tile_of(x, t), bank[6 + b][0:P, 0:D], ALU.add).then_inc(s_x, 1)
            prepare(0, 0)
            over_tiles(v, tile)

        @block.tensor
        def _(pe):
            pe.wait_ge(s_w, 112)

            def tile(t, b):
                pe.wait_ge(s_xn, t + 1)
                for c in range(KC):
                    pe.transpose(bank[b][:, c * 128:c * 128 + P], xn[:, b, c * 128:(c + 1) * 128], g["ident"][0:P, 0:P])
                pe.transpose(bank[b][0:HD, 256:256 + P], tm[:, b, :], g["ident"][0:P, 0:P]).then_inc(s_tr, 1)
                pe.wait_ge(s_xT, t + 1)
                for c in range(KC):
                    mm = pe.matmul(bank[2 + b][0:HD, 0:P], wd[:, c, :], xT[:, b, c, :], start=c == 0, stop=c == 1)
                mm.then_inc(s_nf_ps, 1)
                for c in range(KC):
                    pe.matmul(bank[6 + b][0:P, 0:D], xT[:, b, c, :], g["c1"][:, c, :], start=c == 0, stop=False)
                pe.matmul(bank[6 + b][0:P, 0:D], g["ones"][0:2, 0:P], bo[:, :], start=False, stop=False)
                pe.wait_ge(s_nf, t + 1)
                pe.matmul(bank[4 + b][0:HD, 0:P], wf[:, :], nf[:, b, :], start=True, stop=True).then_inc(s_fu_ps, 1)
                pe.wait_ge(s_fu, t + 1)
                pe.matmul(bank[6 + b][0:P, 0:D], fu[:, b, :], wu[:, :], start=False, stop=True).then_inc(s_o, 1)
            over_tiles(pe, tile)

        @block.scalar
        def _(act):
            act.wait_ge(s_w, 112)

            def tile(t, b):
                act.wait_ge(s_tr, t + 1)
                act.copy(xT[:, b, :, :], bank[b][:, 0:256].rearrange("p (c q) -> p c q", c=2)[:, :, 0:P]).then_inc(s_xT, 1)
                act.copy(nf[HD:2 * HD, b, :], bank[b][0:HD, 256:256 + P])
                act.wait_ge(s_nf_ps, t + 1)
                act.activation(nf[0:HD, b, :], bank[2 + b][0:HD, 0:P], ACT.Relu, bias=bd[:, :]).then_inc(s_nf, 1)
                act.wait_ge(s_fu_ps, t + 1)
                act.activation(fu[:, b, :], bank[4 + b][0:HD, 0:P], ACT.Relu, bias=bf[:, :]).then_inc(s_fu, 1)
            over_tiles(act, tile)


_INS = ['x', 'src', 'dst', 'edge_attr_32', 'L0_gnn_W', 'L0_gnn_Wl', 'L0_gnn_Wr', 'L0_gnn_b', 'L0_mix_w_qkv',
        'L0_mix_b_qkv', 'L0_mix_norm_g', 'L0_mix_norm_b', 'L0_mix_w_fc1', 'L0_mix_b_fc1', 'L0_mix_w_fc2',
        'L0_mix_b_fc2', 'L0_ffn_Wg', 'L0_ffn_bg', 'L0_ffn_W1', 'L0_ffn_b1', 'L0_ffn_W2', 'L0_ffn_b2',
        'L1_gnn_W_down', 'L1_gnn_b_down', 'L1_gnn_W_time', 'L1_gnn_b_time', 'L1_gnn_W_fusion',
        'L1_gnn_b_fusion', 'L1_gnn_W_up', 'L1_gnn_b_up', 'L1_mix_w_qkv', 'L1_mix_w_out', 'L1_mix_b_out',
        'L1_ffn_router_w', 'L1_ffn_w1', 'L1_ffn_w2', 'L1_ffn_w3']


def layouts(x):
    import numpy as np

    def cols(b):
        return np.ascontiguousarray(b.reshape(-1, 128).T)

    def T(w):
        return np.ascontiguousarray(np.swapaxes(w, -1, -2))

    keep = ['x', 'src', 'dst', 'edge_attr_32', 'L0_gnn_W', 'L0_gnn_b', 'L0_mix_w_qkv', 'L0_mix_b_qkv',
            'L0_mix_w_fc1', 'L0_mix_w_fc2', 'L0_mix_b_fc2', 'L0_ffn_bg', 'L0_ffn_b2', 'L1_gnn_b_time',
            'L1_gnn_b_up', 'L1_mix_w_qkv', 'L1_mix_b_out', 'L0_ffn_b1']
    a = {n: np.ascontiguousarray(x[n]) for n in keep}
    a['L0_gnn_W_T'] = T(x['L0_gnn_W'])
    a['L0_gnn_Wl_T'] = T(x['L0_gnn_Wl'])
    a['L0_gnn_Wr_T'] = T(x['L0_gnn_Wr'])
    a['L0_mix_w_q_T'] = T(x['L0_mix_w_qkv'][:, :D])
    a['L0_mix_b_q_cols'] = cols(x['L0_mix_b_qkv'][:D])
    for n in ('L0_mix_norm_g', 'L0_mix_norm_b', 'L0_mix_b_fc1'):
        a[n + '_cols'] = cols(x[n])
    a['L0_ffn_b1_cols'] = np.ascontiguousarray(x['L0_ffn_b1'].reshape(-1, 128).T)
    for n in ('L0_ffn_Wg', 'L0_ffn_W1', 'L0_ffn_W2', 'L1_gnn_W_down', 'L1_gnn_W_time', 'L1_gnn_W_fusion',
              'L1_gnn_W_up', 'L1_mix_w_out', 'L1_ffn_router_w', 'L1_ffn_w1', 'L1_ffn_w2', 'L1_ffn_w3'):
        a[n + '_T'] = T(x[n])
    a['L1_mix_w_kv_T'] = T(x['L1_mix_w_qkv'][512:])
    for n in ('L1_gnn_b_down', 'L1_gnn_b_fusion'):
        a[n + '_col'] = np.ascontiguousarray(x[n].reshape(64, 1))
    return a


def kernel(**inputs):
    import numpy as _np
    import concourse.bacc as _bacc
    from concourse import mybir as _mybir
    from concourse.bass_utils import run_bass_kernel_spmd as _run

    nc = _bacc.Bacc("TRN2", target_bir_lowering=False, num_devices=1)
    laid = layouts({n: _np.asarray(inputs[n]) for n in _INS})
    arrays, aps = {}, {}
    for name, v in laid.items():
        arrays[f"in_{name}"] = v
        aps[name] = nc.dram_tensor(f"in_{name}", v.shape, _mybir.dt.from_np(v.dtype), kind="ExternalInput").ap()
    out = nc.dram_tensor("out_dram", (N, D), F32, kind="ExternalOutput").ap()
    build(nc, aps, out)
    r = _run(nc, [arrays], core_ids=[0])
    return r.results[0]["out_dram"]
```

```python
from contextlib import ExitStack

import concourse.bass as bass
from concourse import mybir

F32 = mybir.dt.float32
I32 = mybir.dt.int32
U32 = mybir.dt.uint32
ALU = mybir.AluOpType
ACT = mybir.ActivationFunctionType
AXX = mybir.AxisListType.X

N = 3125
D = 256
P = 125
T = N // P
KC = D // 128
E = 53125
EC = E // P
EU = 25
SLOT = 128
ET = 440
PAY = 34
AT = 32
HD = 64
NH = 4
TAB = HD + NH
VW = NH * HD + NH + HD + 1
O_W, O_T, O_C = NH * HD, NH * HD + NH, NH * HD + NH + HD
MLP = 768
NE = 8
TOPK = 2
FT = 56
REG = 26 * SLOT
XS = NE * REG + FT * SLOT
H0 = 1024
H1 = 682
H1C = 6
EPS = 1e-5
assert T * P == N and EC * P == E and EC % (2 * EU) == EU and ET % 4 == 0
assert (E + T * (SLOT - 1)) // SLOT <= ET and (N * TOPK + NE * (SLOT - 1)) // SLOT == FT
assert N + SLOT <= REG


def wait_count(eng, sem, n):
    if not isinstance(n, int) or n > 0:
        eng.wait_ge(sem, n)


def over_tiles(eng, body, count=T, written_out=2):
    body(0, 0)
    body(1, 1)
    pairs = (count - written_out + 1) // 2
    with eng.Fori(1, pairs) as j:
        body(j * 2, 0)
        body(j * 2 + 1, 1)
    for t in range(pairs * 2, count):
        body(t, t % 2)


def inside(t, count):
    return not isinstance(t, int) or 0 <= t < count


def at_first(t):
    return isinstance(t, int) and t == 0


def at_last(t, count=T):
    return isinstance(t, int) and t == count - 1


def over_rounds(eng, body, rounds, width, rest=0):
    for b in range(width):
        body(b, 0, b)
    with eng.Fori(1, rounds) as r:
        for b in range(width):
            body(r * width + b, r, b)
    for b in range(rest):
        body(rounds * width + b, rounds + b // width, b % width)


class Stage:

    def __init__(self, nc, name):
        self.nc, self.name = nc, name

    def __enter__(self):
        self.ctx, self.used = ExitStack(), []
        return self

    def __exit__(self, *a):
        self.ctx.close()
        if self.used:
            self.nc.clear_and_free_semaphores(self.used)
            self.nc.all_engine_barrier(sem_only=True)

    def sb(self, name, shape, dt=F32):
        return self.ctx.enter_context(self.nc.sbuf_tensor(f"{self.name}_{name}", shape, dt))

    def sem(self, name):
        self.used.append(self.nc.alloc_semaphore(f"{self.name}_{name}"))
        return self.used[-1]

    def sems(self, name, n=2):
        return [self.sem(f"{name}{k}") for k in range(n)]

    def block(self):
        return self.ctx.enter_context(self.nc.Block())


def layer_stats(v, x, stats, mv, rstd, done, ready):
    for t in range(T):
        v.bn_stats(stats[:, t, :], x[:, t, :]).then_inc(done, 1)
    v.wait_ge(done, T)
    close_stats(v, stats, mv, rstd, done, T, ready)


def close_stats(v, stats, mv, rstd, done, n, ready):
    v.tensor_tensor(mv[:, :, 0], stats[:, :, 1], stats[:, :, 4], ALU.add).then_inc(done, 1)
    v.tensor_tensor(mv[:, :, 1], stats[:, :, 1], stats[:, :, 4], ALU.subtract).then_inc(done, 1)
    v.tensor_tensor(rstd[:, :], stats[:, :, 2], stats[:, :, 5], ALU.add).then_inc(done, 1)
    v.wait_ge(done, n + 3)
    v.tensor_scalar(mv[:, :, 0], mv[:, :, 0], 0.5, None, ALU.mult).then_inc(done, 1)
    v.tensor_tensor(mv[:, :, 1], mv[:, :, 1], mv[:, :, 1], ALU.mult).then_inc(done, 1)
    v.tensor_scalar(rstd[:, :], rstd[:, :], 1.0 / D, EPS, ALU.mult, ALU.add).then_inc(done, 1)
    v.wait_ge(done, n + 6)
    v.scalar_tensor_tensor(out=rstd[:, :], in0=mv[:, :, 1], scalar=0.25, in1=rstd[:, :],
                           op0=ALU.mult, op1=ALU.add).then_inc(done, 1)
    v.wait_ge(done, n + 7)
    v.reciprocal(rstd[:, :], rstd[:, :]).then_inc(ready, 1)


def bins_buffers(st, B, C, room=0):
    onehot = st.sb("onehot", [P, max(B * C, room)])
    return dict(
        onehot_flat=onehot, onehot=onehot[:, 0:B * C].rearrange("p (b c) -> p b c", b=B), cum=st.sb("cum", [P, B, C]), cnt=st.sb("cnt", [P, B + 1]),
        part=st.sb("part", [P, B]), tot=st.sb("tot", [P, B]), toti=st.sb("toti", [P, B], I32),
        pad=st.sb("pad", [P, B]), start=st.sb("start", [P, B + 1]), posf=st.sb("posf", [P, C]),
        done=st.sem("bin_done"), counted=st.sem("bin_counted"), summed=st.sem("bin_summed"))


def bins_vector(v, k, bin_of, number, one, B, C, psum, parts, rows, map_out, map_n, tile_at, two, wide, ready):
    oh, cum, cnt, done = k["onehot"], k["cum"], k["cnt"], k["done"]
    v.tensor_tensor(oh[:, :, :], bin_of.unsqueeze(1).broadcast_to([P, B, C]),
                    number[0:P, 0:B].unsqueeze(2).broadcast_to([P, B, C]), ALU.is_equal).then_inc(done, 1)
    v.wait_ge(done, 1)
    v.tensor_tensor_scan(cum[:, :, :].rearrange("p b c -> p (b c)"), one[0:P, 0:1].broadcast_to([P, B * C]),
                         oh[:, :, :].rearrange("p b c -> p (b c)"), 0.0, ALU.mult, ALU.add).then_inc(done, 1)
    v.memset(cnt[:, 0:1], 0.0).then_inc(done, 1)
    v.wait_ge(done, 3)
    v.tensor_copy(cnt[:, 1:B + 1], cum[:, :, C - 1]).then_inc(done, 1)
    v.wait_ge(done, 4)
    v.tensor_tensor(k["part"][:, :], cnt[:, 1:B + 1], cnt[:, 0:B], ALU.subtract).then_inc(k["counted"], 1)
    v.wait_ge(k["summed"], 1)
    v.tensor_scalar(k["toti"][:, :], psum[0:P, B:2 * B], float(SLOT - 1), None, ALU.add).then_inc(done, 1)
    v.wait_ge(done, 5)
    v.tensor_scalar(k["toti"][:, :], k["toti"][:, :], 7, 7, ALU.logical_shift_right,
                    ALU.logical_shift_left).then_inc(done, 1)
    v.wait_ge(done, 6)
    v.tensor_copy(k["pad"][:, :], k["toti"][:, :]).then_inc(done, 1)
    v.memset(k["start"][:, 0:1], 0.0).then_inc(done, 1)
    v.wait_ge(done, 8)
    v.tensor_tensor_scan(k["start"][:, 1:B + 1], one[0:P, 0:1].broadcast_to([P, B]), k["pad"][:, :], 0.0,
                         ALU.mult, ALU.add).then_inc(done, 1)
    v.wait_ge(done, 9)
    v.tensor_tensor(k["tot"][:, :], psum[0:P, 0:B], k["start"][:, 0:B], ALU.add).then_inc(done, 1)
    v.wait_ge(done, 10)
    v.scalar_tensor_tensor(out=k["tot"][:, :], in0=k["tot"][:, :], scalar=-1.0, in1=cnt[:, 0:B],
                           op0=ALU.add, op1=ALU.subtract).then_inc(done, 1)
    v.wait_ge(done, 11)
    n = 11
    for first, end in parts:
        cols = slice(first, end)
        for b in range(B):
            o = v.scalar_tensor_tensor(out=cum[:, b, cols], in0=cum[:, b, cols], scalar=k["tot"][:, b:b + 1],
                                       in1=oh[:, b, cols], op0=ALU.add, op1=ALU.mult)
        o.then_inc(done, 1)
        v.wait_ge(done, n + 1)
        v.tensor_reduce(k["posf"][:, cols], cum[:, :, cols].rearrange("p b c -> p c b"), AXX, ALU.add).then_inc(done, 1)
        v.wait_ge(done, n + 2)
        n += 2
        if rows is not None:
            pi, lane, tile, row = rows
            v.tensor_copy(pi[:, cols], k["posf"][:, cols]).then_inc(done, 1)
            v.wait_ge(done, n + 1)
            v.tensor_scalar(lane[:, cols], pi[:, cols], SLOT - 1, None, ALU.bitwise_and).then_inc(done, 1)
            v.tensor_scalar(tile[:, cols], pi[:, cols], 7, None, ALU.logical_shift_right).then_inc(done, 1)
            v.wait_ge(done, n + 3)
            v.scalar_tensor_tensor(out=row[:, cols], in0=lane[:, cols], scalar=float(ET), in1=tile[:, cols],
                                   op0=ALU.mult, op1=ALU.add).then_inc(done, 1)
            v.wait_ge(done, n + 4)
            n += 4
        v.sem_inc(ready, 1)
    v.tensor_tensor(wide, tile_at[0:1, 0:map_n].unsqueeze(2).broadcast_to([1, map_n, B - 1]),
                    k["start"][0:1, 1:B].unsqueeze(1).broadcast_to([1, map_n, B - 1]), ALU.is_ge).then_inc(done, 1)
    v.wait_ge(done, n + 1)
    v.tensor_reduce(two, wide, AXX, ALU.add).then_inc(done, 1)
    v.wait_ge(done, n + 2)
    v.tensor_copy(map_out, two).then_inc(done, 1)
    v.wait_ge(done, n + 3)


def bins_tensor(pe, k, before, ones, B, psum):
    pe.wait_ge(k["counted"], 1)
    pe.matmul(psum[0:P, 0:B], before[0:P, 0:P], k["part"][:, :], start=True, stop=True)
    pe.matmul(psum[0:P, B:2 * B], ones[0:P, 0:P], k["part"][:, :], start=True, stop=True).then_inc(k["summed"], 1)


def tile_of(x, t):
    return x[:, bass.ds(t, 1), :].rearrange("p o f -> p (o f)")


def build(nc, a, out):
    with ExitStack() as ctx:
        def sb(name, shape, dt=F32):
            return ctx.enter_context(nc.sbuf_tensor(name, shape, dt))

        g = {
            "table": nc.dram_tensor("table", (N, TAB), F32).ap(),
            "slots": nc.dram_tensor("slots", (SLOT * ET, PAY), F32).ap(),
            "xs": nc.dram_tensor("xs", (XS, D), F32).ap(),
            "ys": nc.dram_tensor("ys", (FT * SLOT, D), F32).ap(),
        }
        g["x"] = sb("x_nodes", [P, T, D])
        g["mv"] = sb("mv", [P, T, 2])
        g["rstd"] = sb("rstd", [P, T])
        g["stats"] = sb("stats", [P, T, 6])
        g["slot"] = sb("slot", [P, T, TOPK], I32)
        g["prob"] = sb("prob", [P, T, TOPK])
        g["ident"] = sb("ident", [128, 128])
        g["ones"] = sb("ones", [128, 128])
        g["before"] = sb("before", [128, 128])
        g["bin_no"] = sb("bin_no", [128, T + 1])
        g["tile_at"] = sb("tile_at", [1, ET])
        g["time"] = sb("time", [P, T, HD + 1])
        g["el"] = sb("el", [P, T, NH])
        g["edge_map"] = sb("edge_map", [1, ET], I32)
        g["bank"] = [ctx.enter_context(nc.psum_tensor(f"bank{k}", [128, 512], F32)) for k in range(8)]
        front(nc, a, g)
        with Stage(nc, "W0") as weights:
            w = input_weights(weights, 0)
            with Stage(nc, "G") as agg:
                g["agg"] = agg.sb("agg", [P, T, VW])
                edge_aggregation(nc, a, g, w)
                gat_finish(nc, a, g)
            moe(nc, a, g, 0, w)
        with Stage(nc, "W1") as weights:
            w = input_weights(weights, 1)
            with Stage(nc, "L") as l1:
                g["c1"] = l1.sb("c1", [128, KC, D])
                w_up = update_weights(l1)
                l1_keys_values(nc, a, g, w, w_up)
                l1_update(nc, a, g, w_up)
            moe(nc, a, g, 1, w)
            combine(nc, g, out)


def front(nc, a, g):
    bank = g["bank"]
    table_rows = g["table"].rearrange("(t p) f -> t p f", p=P)
    attr = a["edge_attr_32"].rearrange("(p c) f -> p c f", c=EC)
    slots_pf = g["slots"].rearrange("(p t) f -> p (t f)", p=SLOT)
    FILLS = 8
    ROUNDS = EC // EU
    MC = MLP // 128
    spare = g["xs"][NE * REG:XS, :].rearrange("(p t) f -> p (t f)", p=SLOT)
    BLANK = FT * D // (ROUNDS // 2 * 2)
    with Stage(nc, "A") as st:
        src_i = st.sb("src_i", [P, EC], I32)
        dst_i = st.sb("dst_i", [P, EC], I32)
        src_f = st.sb("src_f", [P, EC])
        own = st.sb("own_tile", [P, EC])
        ends = st.sb("ends", [P, EC, 2], I32)
        k = bins_buffers(st, T, EC, ET * (T - 1))
        pos_i = st.sb("pos_i", [P, EC], I32)
        lane_i = st.sb("lane_i", [P, EC], I32)
        tile_i = st.sb("tile_i", [P, EC], I32)
        row_i = st.sb("row_i", [P, EC], I32)
        narrow = st.sb("narrow", [1, ET])
        blank = st.sb("blank", [128, BLANK])
        s_blank, s_blanked = st.sem("blank"), st.sem("blanked")
        fill = st.sb("fill", [128, ET // FILLS, PAY])
        pay = st.sb("pay", [P, 2, EU, PAY])
        ids = st.sb("ids", [P, 2, EU], I32)
        w72 = st.sb("w72", [128, KC, TAB + NH])
        wT = st.sb("wT", [HD, D])
        wlrT = st.sb("wlrT", [HD, 2 * NH])
        stats = st.sb("stats", [P, T, 6])
        xn = st.sb("xn", [P, 2, D + 1])
        xT = st.sb("xT", [128, 2, KC, P])
        tab = st.sb("tab", [P, 2, TAB + NH])
        wkv = st.sb("wkv", [128, KC, 2 * D])
        bkv = st.sb("bkv", [1, 2 * D])
        wqT = st.sb("wqT", [128, KC, D])
        bq = st.sb("bq", [128, KC])
        nn = st.sb("nn", [1, 1])
        gram = st.sb("gram", [128, KC, D + 1])
        grow = st.sb("grow", [1, D])
        gwv = st.sb("gwv", [128, KC, D])
        gwv_row = st.sb("gwv_row", [1, D])
        logit = st.sb("logit", [128, KC, HD])
        lmax = st.sb("lmax", [128, KC])
        lsum = st.sb("lsum", [128, KC])
        diag = st.sb("diag", [128, KC, 128])
        attnT = st.sb("attnT", [128, KC, 128])
        c0 = st.sb("c0", [128, KC, D])
        c0_row = st.sb("c0_row", [1, D])
        x1 = k["cum"][:, :, :].rearrange("p b c -> p (b c)")[:, 0:T * D].rearrange("p (t f) -> p t f", f=D)
        mv1 = st.sb("mv1", [P, T, 2])
        rstd1 = st.sb("rstd1", [P, T])
        lnT = st.sb("lnT", [128, 2, KC])
        fc1 = st.sb("fc1", [128, KC, MLP])
        fb1 = st.sb("fb1", [128, MC])
        fc2 = st.sb("fc2", [128, MC, D])
        fb2 = st.sb("fb2", [1, D])
        gT = st.sb("gT", [128, 2, MC, P])
        s_edges, s_w, s_x, s_wm = st.sem("edges"), st.sem("weights"), st.sem("x_loaded"), st.sem("mix_weights")
        s_const, s_ones = st.sem("const"), st.sem("ones")
        s_fill, s_filled = st.sem("fill"), st.sem("filled")
        s_rows, s_ends = st.sem("rows_ready"), st.sem("round_ends")
        s_go, s_own = st.sem("round_go"), st.sem("own_row")
        s_attr, s_scat = st.sems("attr_loaded"), st.sems("scattered")
        s_ln = st.sem("ln")
        s_rstd, s_var = st.sem("rstd"), st.sem("var")
        s_xn, s_tr, s_xT, s_h, s_tab, s_wa, s_waT = (st.sem(n) for n in (
            "xn_ready", "transposed", "xT_ready", "h_ready", "tab_ready", "wa", "wa_ready"))
        s_st = st.sems("table_stored")
        ps_bin, ps_g = bank[0], [bank[1], bank[2]]
        ps_t, ps_h = [bank[3], bank[4]], [bank[5], bank[6]]
        s_gram, s_fold_pe, s_fold = st.sem("gram"), st.sem("fold_pe"), st.sem("fold")
        s_b_xn, s_b_tr, s_b_xT, s_b_mm, s_b_x1, s_b_st = (st.sem("b_" + n) for n in (
            "xn", "tr", "xT", "mm", "x1", "stat"))
        s_m_xn, s_m_tr, s_m_xT, s_m_h, s_m_g, s_m_y, s_m_out, s_m_var, s_m_rstd = (st.sem("m_" + n) for n in (
            "xn", "tr", "xT", "h", "g", "y", "out", "var", "rstd"))
        block = st.block()

        @block.sync
        def _(sp):
            sp.dma_start(src_i[:, :], a["src"].rearrange("(p c) -> p c", c=EC)).then_inc(s_edges, 16)
            sp.dma_start(dst_i[:, :], a["dst"].rearrange("(p c) -> p c", c=EC)).then_inc(s_edges, 16)
            sp.wait_ge(s_fill, 3)
            w = ET // FILLS * PAY
            for q in range(FILLS):
                sp.dma_start(slots_pf[:, q * w:(q + 1) * w],
                             fill[:, :, :].rearrange("p t f -> p (t f)")).then_inc(s_filled, 16)
            sp.dma_start(g["x"][:, :, :], a["x"].rearrange("(t p) f -> p t f", p=P)).then_inc(s_x, 16)
            sp.dma_start(w72[:, :, 0:HD], a["L0_gnn_W"].rearrange("(k p) f -> p k f", p=128)).then_inc(s_w, 16)
            sp.dma_start(wT[:, :], a["L0_gnn_W_T"]).then_inc(s_w, 16)
            sp.dma_start(wlrT[:, 0:NH], a["L0_gnn_Wr_T"]).then_inc(s_w, 16)
            sp.dma_start(wlrT[:, NH:2 * NH], a["L0_gnn_Wl_T"]).then_inc(s_w, 16)
            mix = [(wkv[:, :, :], a["L0_mix_w_qkv"].rearrange("(k p) f -> p k f", p=128)[:, :, D:3 * D]),
                   (bkv[:, :], a["L0_mix_b_qkv"][D:3 * D].unsqueeze(0)),
                   (wqT[:, :, :], a["L0_mix_w_q_T"].rearrange("(k p) f -> p k f", p=128)),
                   (bq[:, :], a["L0_mix_b_q_cols"]),
                   (lnT[:, 0, :], a["L0_mix_norm_g_cols"]), (lnT[:, 1, :], a["L0_mix_norm_b_cols"]),
                   (fc1[:, :, :], a["L0_mix_w_fc1"].rearrange("(k p) f -> p k f", p=128)),
                   (fb1[:, :], a["L0_mix_b_fc1_cols"]),
                   (fc2[:, :, :], a["L0_mix_w_fc2"].rearrange("(k p) f -> p k f", p=128)),
                   (fb2[:, :], a["L0_mix_b_fc2"].unsqueeze(0))]
            for dst, src in mix:
                sp.dma_start(dst, src).then_inc(s_wm, 16)
            def load(n, r, b):
                wait_count(sp, s_scat[b], r * (16 * EU))
                sp.dma_start(pay[:, b, :, 0:AT], attr[:, bass.ds(n * EU, EU), :]).then_inc(s_attr[b], 16)
                if b == 1:
                    if at_first(r):
                        sp.wait_ge(s_blank, 1)
                    for c in range(2):
                        sp.dma_start(spare[:, bass.ds(r * (2 * BLANK) + c * BLANK, BLANK)], blank[:, :]).then_inc(s_blanked, 16)
            over_rounds(sp, load, ROUNDS // 2, 2, ROUNDS % 2)
            sp.wait_ge(s_blanked, ROUNDS // 2 * 32)

        @block.gpsimd
        def _(gp):
            gp.memset(fill[:, :, 0:AT], 0.0).then_inc(s_fill, 1)
            gp.memset(fill[:, :, AT:AT + 1], -1.0).then_inc(s_fill, 1)
            gp.memset(fill[:, :, AT + 1:PAY], 0.0).then_inc(s_fill, 1)
            gp.iota(g["bin_no"][:, :], [[1, T + 1]], base=0, channel_multiplier=0,
                    allow_small_or_imprecise_dtypes=True).then_inc(s_const, 1)
            gp.iota(g["tile_at"][:, :], [[SLOT, ET]], base=0, channel_multiplier=0,
                    allow_small_or_imprecise_dtypes=True).then_inc(s_const, 1)
            gp.memset(g["ones"][:, :], 1.0).then_inc(s_ones, 1)
            gp.wait_ge(s_ones, 1)
            gp.affine_select(out=g["ident"][:, :], in_=g["ones"][:, :], compare_op=ALU.is_equal, fill=0.0, base=0,
                             pattern=[[1, 128]], channel_multiplier=-1).then_inc(s_const, 1)
            gp.affine_select(out=g["before"][:, :], in_=g["ones"][:, :], compare_op=ALU.is_gt, fill=0.0, base=0,
                             pattern=[[1, 128]], channel_multiplier=-1).then_inc(s_const, 1)
            gp.memset(xn[:, :, D:D + 1], 1.0).then_inc(s_const, 1)
            gp.memset(nn[:, :], float(N)).then_inc(s_const, 1)
            gp.memset(diag[:, :, :], 0.0).then_inc(s_const, 1)
            gp.memset(blank[:, :], 0.0).then_inc(s_blank, 1)
            gp.wait_ge(s_rows, 1)
            gp.wait_ge(s_filled, 16 * FILLS)

            def scatter(n, r, b):
                if not isinstance(r, int):
                    gp.wait_ge(s_rows, 2)
                wait_count(gp, s_scat[b], r * (16 * EU))
                gp.tensor_copy(pay[:, b, :, AT:PAY].bitcast(I32), ends[:, bass.ds(n * EU, EU), :]).then_inc(s_ends, 1)
                gp.tensor_copy(ids[:, b, :], row_i[:, bass.ds(n * EU, EU)]).then_inc(s_ends, 1)
                gp.wait_ge(s_ends, n * 2 + 2)
                gp.wait_ge(s_attr[b], r * 16 + 16)
                gp.sem_inc(s_go, 1)
                for u in range(EU):
                    gp.indirect_dma_start(g["slots"], bass.IndirectOffsetOnAxis(ap=ids[:, b, u:u + 1], axis=0),
                                          pay[:, b, u, :], None).then_inc(s_scat[b], 16)
            over_rounds(gp, scatter, ROUNDS // 2, 2, ROUNDS % 2)
            gp.wait_ge(s_scat[0], (ROUNDS // 2 + 1) * 16 * EU)
            gp.wait_ge(s_scat[1], ROUNDS // 2 * 16 * EU)

        @block.vector
        def _(v):
            v.wait_ge(s_edges, 32)
            v.tensor_copy(src_f[:, :], src_i[:, :]).then_inc(s_own, 1)
            v.tensor_copy(ends[:, :, 1], dst_i[:, :])
            v.wait_ge(s_own, 1)
            v.tensor_scalar(own[:, :], src_f[:, :], 0.5, 1.0 / P, ALU.add, ALU.mult).then_inc(s_own, 1)
            v.wait_ge(s_own, 2)
            v.tensor_scalar(own[:, :], own[:, :], -0.5, 1.5 * 2 ** 23, ALU.add, ALU.add).then_inc(s_own, 1)
            v.wait_ge(s_own, 3)
            v.tensor_scalar(own[:, :], own[:, :], -1.5 * 2 ** 23, None, ALU.add).then_inc(s_own, 1)
            v.wait_ge(s_own, 4)
            v.scalar_tensor_tensor(out=ends[:, :, 0].bitcast(F32), in0=own[:, :], scalar=-float(P), in1=src_f[:, :],
                                   op0=ALU.mult, op1=ALU.add).then_inc(s_own, 1)
            v.wait_ge(s_const, 7)
            v.wait_ge(s_own, 5)
            wide = k["onehot_flat"][0:1, 0:ET * (T - 1)].rearrange("o (t b) -> o t b", b=T - 1)
            bins_vector(v, k, own[:, :], g["bin_no"], g["ones"], T, EC, ps_bin, ((0, 2 * EU), (2 * EU, EC)),
                        (pos_i, lane_i, tile_i, row_i), g["edge_map"][:, :], ET, g["tile_at"],
                        narrow[:, :], wide, s_rows)
            v.wait_ge(s_x, 16)
            layer_stats(v, g["x"], stats, g["mv"], g["rstd"], s_ln, s_var)
            v.wait_ge(s_wa, 1)
            v.tensor_copy(w72[:, :, HD:TAB + NH],
                          bank[7][:, 0:4 * NH].rearrange("p (k f) -> p k f", k=2)).then_inc(s_waT, 1)
            v.wait_ge(s_rstd, 1)

            def normalise(t, b):
                wait_count(v, s_tr, t)
                v.tensor_scalar(xn[:, b, 0:D], tile_of(g["x"], t), tile_of(g["mv"], t)[:, 0:1],
                                g["rstd"][:, bass.ds(t, 1)], ALU.subtract, ALU.mult).then_inc(s_xn, 1)
            over_tiles(v, normalise)

            for c in range(KC):
                v.wait_ge(s_fold_pe, 4)
                for h in range(2):
                    r = slice(h * HD, h * HD + HD)
                    v.tensor_copy(logit[r, c, :], bank[5][r, c * 128 + h * HD:c * 128 + h * HD + HD]).then_inc(s_fold, 1)
            v.wait_ge(s_fold, 4)
            v.tensor_reduce(lmax[:, :], logit[:, :, :], AXX, ALU.max).then_inc(s_fold, 1)
            v.wait_ge(s_fold, 5)
            v.tensor_tensor(logit[:, :, :], logit[:, :, :], lmax[:, :].unsqueeze(2).broadcast_to([128, KC, HD]),
                            ALU.subtract).then_inc(s_fold, 1)
            v.wait_ge(s_fold, 7)
            v.tensor_reduce(lsum[:, :], logit[:, :, :], AXX, ALU.add).then_inc(s_fold, 1)
            v.wait_ge(s_fold, 8)
            v.reciprocal(lsum[:, :], lsum[:, :]).then_inc(s_fold, 1)
            v.wait_ge(s_fold, 9)
            for c in range(KC):
                for h in range(2):
                    r = slice(h * HD, h * HD + HD)
                    v.tensor_scalar(diag[r, c, h * HD:h * HD + HD], logit[r, c, :], lsum[r, c:c + 1], None,
                                    ALU.mult).then_inc(s_fold, 1)

            def attend_in(t, b):
                wait_count(v, s_b_tr, t - 1)
                wait_count(v, s_b_x1, t - 1)
                v.tensor_scalar(xn[:, b, 0:D], tile_of(g["x"], t), tile_of(g["mv"], t)[:, 0:1],
                                g["rstd"][:, bass.ds(t, 1)], ALU.subtract, ALU.mult).then_inc(s_b_xn, 1)

            def attend(t, b):
                if not at_last(t):
                    attend_in(t + 1, 1 - b)
                v.wait_ge(s_b_mm, t + 1)
                v.wait_ge(s_b_xn, t + 1)
                v.tensor_tensor(tile_of(x1, t), ps_h[b][0:P, 0:D], xn[:, b, 0:D], ALU.add).then_inc(s_b_x1, 1)
            attend_in(0, 0)
            over_tiles(v, attend)
            v.wait_ge(s_b_x1, T)
            layer_stats(v, x1, stats, mv1, rstd1, s_b_st, s_m_var)
            v.wait_ge(s_m_rstd, 1)

            def mlp_in(t, b):
                wait_count(v, s_m_tr, t - 1)
                v.tensor_scalar(xn[:, b, 0:D], tile_of(x1, t), tile_of(mv1, t)[:, 0:1],
                                rstd1[:, bass.ds(t, 1)], ALU.subtract, ALU.mult).then_inc(s_m_xn, 1)

            def mlp_out(t, b):
                v.tensor_tensor(tile_of(g["x"], t), tile_of(g["x"], t), tile_of(x1, t), ALU.add).then_inc(s_m_out, 1)
                if inside(t + 2, T):
                    mlp_in(t + 2, b)
                v.wait_ge(s_m_out, t * 2 + 1)
                v.wait_ge(s_m_y, t + 1)
                v.tensor_tensor(tile_of(g["x"], t), tile_of(g["x"], t), ps_h[b][0:P, 0:D], ALU.add).then_inc(s_m_out, 1)
            mlp_in(0, 0)
            mlp_in(1, 1)
            over_tiles(v, mlp_out, T, 4)

        @block.tensor
        def _(pe):
            pe.wait_ge(s_const, 7)
            bins_tensor(pe, k, g["before"], g["ones"], T, ps_bin)
            pe.wait_ge(s_w, 64)
            pe.matmul(bank[7][:, 0:2 * NH], wT[:, 0:128], wlrT[:, :], start=True, stop=True)
            pe.matmul(bank[7][:, 2 * NH:4 * NH], wT[:, 128:256], wlrT[:, :], start=True, stop=True).then_inc(s_wa, 1)
            pe.wait_ge(s_waT, 1)

            def body(t, b):
                pe.wait_ge(s_xn, t + 1)
                wait_count(pe, s_xT, t)
                for c in range(KC):
                    pe.transpose(ps_t[b][:, c * 128:c * 128 + P], xn[:, b, c * 128:(c + 1) * 128], g["ident"][0:P, 0:P])
                for c in range(KC):
                    mm = pe.matmul(ps_g[c][:, 0:D + 1], xn[:, b, c * 128:(c + 1) * 128], xn[:, b, :], start=at_first(t), stop=at_last(t))
                mm.then_inc(s_tr, 1)
                pe.wait_ge(s_xT, t + 1)
                wait_count(pe, s_tab, t)
                for c in range(KC):
                    mm = pe.matmul(ps_h[b][0:P, 0:TAB + NH], xT[:, b, c, :], w72[:, c, :], start=c == 0, stop=c == 1)
                mm.then_inc(s_h, 1)
            over_tiles(pe, body)

            pe.wait_ge(s_gram, 1)
            pe.wait_ge(s_wm, 160)
            for c in range(KC):
                mm = pe.transpose(bank[0][0:1, c * 128:(c + 1) * 128], gram[:, c, D:D + 1], g["ident"][:, :])
            mm.then_inc(s_fold_pe, 1)
            pe.wait_ge(s_gram, 2)
            for m in range(KC):
                for c in range(KC):
                    pe.matmul(bank[1 + m][:, 0:D], gram[:, c, m * 128:(m + 1) * 128], wkv[:, c, D:2 * D], start=c == 0, stop=False)
                mm = pe.matmul(bank[1 + m][:, 0:D], grow[:, m * 128:(m + 1) * 128], bkv[:, D:2 * D], start=False, stop=True)
            mm.then_inc(s_fold_pe, 1)
            for c in range(KC):
                pe.matmul(bank[7][0:1, 0:D], gram[:, c, D:D + 1], wkv[:, c, D:2 * D], start=c == 0, stop=False)
            pe.matmul(bank[7][0:1, 0:D], nn[:, :], bkv[:, D:2 * D], start=False, stop=True).then_inc(s_fold_pe, 1)
            pe.wait_ge(s_gram, 4)
            for m in range(KC):
                cols = slice(m * 128, (m + 1) * 128)
                for c in range(KC):
                    pe.matmul(bank[5][:, cols], wkv[:, c, cols], gwv[:, c, cols], start=c == 0, stop=False)
                mm = pe.matmul(bank[5][:, cols], bkv[:, cols], gwv_row[:, cols], start=False, stop=True)
            mm.then_inc(s_fold_pe, 1)
            pe.wait_ge(s_fold, 13)
            for c in range(KC):
                mm = pe.transpose(bank[0][:, c * 128:(c + 1) * 128], diag[:, c, :], g["ident"][:, :])
            mm.then_inc(s_fold_pe, 1)
            pe.wait_ge(s_gram, 5)
            for m in range(KC):
                for j in range(KC):
                    pe.matmul(bank[1 + m][:, j * 128:(j + 1) * 128], wqT[:, j, m * 128:(m + 1) * 128], attnT[:, j, :],
                              start=True, stop=True)
            for j in range(KC):
                mm = pe.matmul(bank[7][0:1, j * 128:(j + 1) * 128], bq[:, j:j + 1], attnT[:, j, :], start=True, stop=True)
            mm.then_inc(s_fold_pe, 1)
            pe.wait_ge(s_gram, 6)

            def turn(t, b):
                pe.wait_ge(s_b_xn, t + 1)
                for c in range(KC):
                    mm = pe.transpose(ps_t[b][:, c * 128:c * 128 + P], xn[:, b, c * 128:(c + 1) * 128], g["ident"][0:P, 0:P])
                mm.then_inc(s_b_tr, 1)

            def attend(t, b):
                if not at_last(t):
                    turn(t + 1, 1 - b)
                pe.wait_ge(s_b_xT, t + 1)
                for c in range(KC):
                    pe.matmul(ps_h[b][0:P, 0:D], xT[:, b, c, :], c0[:, c, :], start=c == 0, stop=False)
                pe.matmul(ps_h[b][0:P, 0:D], g["ones"][0:1, 0:P], c0_row[:, :], start=False, stop=True).then_inc(s_b_mm, 1)
            turn(0, 0)
            over_tiles(pe, attend)

            def mlp_hidden(t, b):
                pe.wait_ge(s_m_xn, t + 1)
                for c in range(KC):
                    mm = pe.transpose(ps_t[b][:, c * 128:c * 128 + P], xn[:, b, c * 128:(c + 1) * 128], g["ident"][0:P, 0:P])
                mm.then_inc(s_m_tr, 1)
                pe.wait_ge(s_m_xT, t + 1)
                for m in range(MC):
                    hb = [bank[1], bank[2], bank[0], bank[7]][2 * b + m // 3]
                    for c in range(KC):
                        mm = pe.matmul(hb[:, m % 3 * P:m % 3 * P + P], fc1[:, c, m * 128:(m + 1) * 128], xT[:, b, c, :],
                                       start=c == 0, stop=c == 1)
                mm.then_inc(s_m_h, 1)

            def mlp(t, b):
                if not at_last(t):
                    mlp_hidden(t + 1, 1 - b)
                wait_count(pe, s_m_out, 2 * t - 2)
                pe.wait_ge(s_m_g, t + 1)
                for m in range(MC):
                    pe.matmul(ps_h[b][0:P, 0:D], gT[:, b, m, :], fc2[:, m, :], start=m == 0, stop=False)
                pe.matmul(ps_h[b][0:P, 0:D], g["ones"][0:1, 0:P], fb2[:, :], start=False, stop=True).then_inc(s_m_y, 1)
            mlp_hidden(0, 0)
            over_tiles(pe, mlp)

        @block.scalar
        def _(act):
            act.wait_ge(s_var, 1)
            act.activation(g["rstd"][:, :], g["rstd"][:, :], ACT.Sqrt).then_inc(s_rstd, 1)

            def body(t, b):
                act.wait_ge(s_tr, t + 1)
                act.copy(xT[:, b, :, :], ps_t[b][:, 0:256].rearrange("p (c q) -> p c q", c=2)[:, :, 0:P]).then_inc(s_xT, 1)
                wait_count(act, s_st[b], (t - b) * 8)
                act.wait_ge(s_h, t + 1)
                act.copy(tab[:, b, :], ps_h[b][0:P, 0:TAB + NH])
                act.copy(tile_of(g["el"], t), ps_h[b][0:P, TAB:TAB + NH]).then_inc(s_tab, 1)
                act.wait_ge(s_tab, t + 1)
                act.dma_start(table_rows[bass.ds(t, 1), :, :].rearrange("o p f -> (o p) f"), tab[:, b, 0:TAB]).then_inc(s_st[b], 16)
            over_tiles(act, body)
            act.wait_ge(s_tr, T)
            for c in range(KC):
                cp = act.copy(gram[:, c, :], ps_g[c][:, 0:D + 1])
            cp.then_inc(s_gram, 1)
            act.wait_ge(s_fold_pe, 1)
            act.copy(grow[:, :], bank[0][0:1, 0:D]).then_inc(s_gram, 1)
            act.wait_ge(s_fold_pe, 2)
            for m in range(KC):
                cp = act.copy(gwv[:, m, :], bank[1 + m][:, 0:D])
            cp.then_inc(s_gram, 1)
            act.wait_ge(s_fold_pe, 3)
            act.copy(gwv_row[:, :], bank[7][0:1, 0:D]).then_inc(s_gram, 1)
            act.wait_ge(s_fold, 6)
            act.activation(logit[:, :, :], logit[:, :, :], ACT.Exp, scale=HD ** -0.5).then_inc(s_fold, 1)
            act.wait_ge(s_fold_pe, 5)
            act.copy(attnT[:, :, :], bank[0][:, 0:D].rearrange("p (c q) -> p c q", c=2)).then_inc(s_gram, 1)
            act.wait_ge(s_fold_pe, 6)
            for m in range(KC):
                act.copy(c0[:, m, :], bank[1 + m][:, 0:D])
            act.copy(c0_row[:, :], bank[7][0:1, 0:D]).then_inc(s_gram, 1)

            def attend(t, b):
                act.wait_ge(s_b_tr, t + 1)
                act.copy(xT[:, b, :, :], ps_t[b][:, 0:256].rearrange("p (c q) -> p c q", c=2)[:, :, 0:P]).then_inc(s_b_xT, 1)
            over_tiles(act, attend)
            act.wait_ge(s_m_var, 1)
            act.activation(rstd1[:, :], rstd1[:, :], ACT.Sqrt).then_inc(s_m_rstd, 1)

            def mlp(t, b):
                act.wait_ge(s_m_tr, t + 1)
                for c in range(KC):
                    cp = act.activation(xT[:, b, c, :], ps_t[b][:, c * 128:c * 128 + P], ACT.Identity,
                                        bias=lnT[:, 1, c:c + 1], scale=lnT[:, 0, c:c + 1])
                cp.then_inc(s_m_xT, 1)
                act.wait_ge(s_m_h, t + 1)
                for m in range(MC):
                    hb = [bank[1], bank[2], bank[0], bank[7]][2 * b + m // 3]
                    cp = act.activation(gT[:, b, m, :], hb[:, m % 3 * P:m % 3 * P + P], ACT.Gelu, bias=fb1[:, m:m + 1])
                cp.then_inc(s_m_g, 1)
            over_tiles(act, mlp)
            act.wait_ge(s_st[0], (T + 1) // 2 * 16)
            act.wait_ge(s_st[1], T // 2 * 16)


def node_tiles(nc, g, engine, q):
    _, tiles = nc.values_load_multi_w_load_instructions(
        g["edge_map"][0:1, bass.ds(q * 4, 8)], engines=(engine,), min_val=0, max_val=T - 1,
        skip_runtime_bounds_check_because="the map counts the bins that start before a slot: 0 to T - 1")
    return tiles


def edge_aggregation(nc, a, g, w_in):
    bank = g["bank"]
    G = 4
    RING = 8
    VR = 4
    NG = ET // G
    ROUNDS, REST = NG // RING, NG % RING
    AHEAD = NE * KC - ROUNDS
    agg = g["agg"]
    slots = g["slots"].rearrange("(p t) f -> p t f", p=SLOT)
    with Stage(nc, "D") as st:
        row_no = st.sb("row_no", [128, P])
        pay = st.sb("pay", [128, RING, G, PAY])
        hg = st.sb("hg", [128, RING, G, TAB])
        hot = st.sb("hot", [128, VR, G, P])
        hotT = st.sb("hotT", [P, 2, G, 128])
        attr = st.sb("attr", [128, 2, G * AT])
        attrT = st.sb("attrT", [128, 2, 128])
        wt = st.sb("wt", [128, G, HD])
        bt = st.sb("bt", [1, G, HD])
        z = st.sb("z", [128, 2, G, NH])
        val = st.sb("val", [128, VR, G, VW])
        s_w, s_zero, s_start = st.sem("weights"), st.sem("zero"), st.sem("start")
        s_pay = st.sems("pay", RING)
        s_hg = st.sems("hg", RING)
        s_go, s_attr = st.sem("go"), st.sem("attr")
        s_hot, s_hotT_ps, s_hotT, s_at_ps, s_at, s_time, s_relu, s_el, s_z0, s_z, s_w_exp, s_val, s_main, s_agg = (
            st.sem(n) for n in ("hot", "hotT_psum", "hotT", "attrT_psum", "attrT", "time", "relu", "el",
                                "z_sum", "z", "w_exp", "val", "summed", "agg"))
        block = st.block()

        @block.sync
        def _(sp):
            sp.wait_ge(s_zero, 1)
            for j in range(G):
                sp.dma_start(wt[AT * j:AT * j + AT, j, :], a["L1_gnn_W_time_T"]).then_inc(s_w, 16)
                sp.dma_start(bt[:, j, :], a["L1_gnn_b_time"].unsqueeze(0)).then_inc(s_w, 16)
            def load(q, r, b):
                wait_count(sp, s_val, q - RING + 1)
                sp.dma_start(pay[:, b, :, :], slots[:, bass.ds(q * G, G), :]).then_inc(s_pay[b], 16)
                if b == RING - 1:
                    if at_first(r):
                        for n in range(AHEAD + 1):
                            load_input_weights(sp, a, w_in, 0, n)
                    else:
                        load_input_weights(sp, a, w_in, 0, r + AHEAD)
            over_rounds(sp, load, ROUNDS, RING, REST)

        @block.gpsimd
        def _(gp):
            gp.iota(row_no[:, :], [[1, P]], base=0, channel_multiplier=0,
                    allow_small_or_imprecise_dtypes=True).then_inc(s_start, 1)

            def fetch(q, r, b):
                wait_count(gp, s_val, q - RING + 1)
                gp.wait_ge(s_pay[b], r * 16 + 16)
                gp.sem_inc(s_go, 1)
                for j in range(G):
                    gp.indirect_dma_start(hg[:, b, j, :], None, g["table"],
                                          bass.IndirectOffsetOnAxis(ap=pay[:, b, j, AT + 1:PAY].bitcast(I32), axis=0)
                                          ).then_inc(s_hg[b], 16)
            over_rounds(gp, fetch, ROUNDS, RING, REST)


        @block.vector
        def _(v):
            v.memset(wt[:, :, :], 0.0).then_inc(s_zero, 1)
            v.memset(val[:, :, :, O_C:O_C + 1], 1.0).then_inc(s_start, 1)
            v.memset(agg[:, :, :], 0.0).then_inc(s_start, 1)
            v.wait_ge(s_start, 3)

            def logits(q, r, b):
                v.wait_ge(s_hg[b], r * (16 * G) + 16 * G)
                v.wait_ge(s_el, q + 1)
                v.tensor_tensor(z[:, b % 2, :, :], bank[3][:, 0:G * NH].rearrange("p (j h) -> p j h", j=G),
                                hg[:, b, :, HD:TAB], ALU.add).then_inc(s_z0, 1)

            def leaky_relu(q, b):
                v.wait_ge(s_z0, q + 1)
                v.scalar_tensor_tensor(out=z[:, b % 2, :, :], in0=z[:, b % 2, :, :], scalar=0.2, in1=z[:, b % 2, :, :],
                                       op0=ALU.mult, op1=ALU.max).then_inc(s_z, 1)

            def make_hot(q, r, b):
                v.wait_ge(s_pay[b], r * 16 + 16)
                v.tensor_tensor(hot[:, b % VR, :, :], row_no[:, :].unsqueeze(1).broadcast_to([128, G, P]),
                                pay[:, b, :, AT:AT + 1].broadcast_to([128, G, P]), ALU.is_equal).then_inc(s_hot, 1)

            def values(q, b):
                p = b % VR
                v.wait_ge(s_w_exp, q + 1)
                v.tensor_tensor(val[:, p, :, 0:O_W].rearrange("p j (h f) -> p j h f", h=NH),
                                hg[:, b, :, 0:HD].unsqueeze(2).broadcast_to([128, G, NH, HD]),
                                val[:, p, :, O_W:O_T].unsqueeze(3).broadcast_to([128, G, NH, HD]),
                                ALU.mult).then_inc(s_val, 1)

            def add(q, window, j):
                v.wait_ge(s_main, q * G + j + 1)
                wait_count(v, s_agg, q * G + j)
                v.tensor_tensor(tile_of(agg, window[j]), tile_of(agg, window[j]), bank[4 + j][0:P, 0:VW],
                                ALU.add).then_inc(s_agg, 1)

            windows = [None]

            def step(s, r, b):
                last, sums = inside(s - 1, NG), inside(s - 2, NG)
                last_b = (b - 1) % RING
                if sums and b % 2 == 0:
                    windows[0] = node_tiles(nc, g, mybir.EngineType.DVE, s - 2)
                window = windows[0] and windows[0][b % 2 * G:]
                if last:
                    logits(s - 1, r if b else r - 1, last_b)
                if inside(s, NG):
                    make_hot(s, r, b)
                if sums:
                    add(s - 2, window, 0)
                if last:
                    leaky_relu(s - 1, last_b)
                if sums:
                    add(s - 2, window, 1)
                if last:
                    values(s - 1, last_b)
                if sums:
                    add(s - 2, window, 2)
                    add(s - 2, window, 3)
            over_rounds(v, step, ROUNDS, RING, REST + 2)

        @block.tensor
        def _(pe):
            pe.wait_ge(s_w, 32 * G)

            def sum_slots(q, b, tiles):
                if tiles[0] == 0:
                    pe.wait_ge(s_val, q + 1)
                    pe.wait_ge(s_relu, q + 1)
                for j in tiles:
                    wait_count(pe, s_agg, (q - 1) * G + j + 1)
                    pe.matmul(bank[4 + j][0:P, 0:VW], hot[:, b % VR, j, :], val[:, b % VR, j, :], start=True, stop=True
                              ).then_inc(s_main, 1)

            def transposes(q, b):
                p = b % 2
                wait_count(pe, s_at, q)
                pe.wait_ge(s_attr, q + 1)
                pe.transpose(bank[1][:, 0:128], attr[:, p, :], g["ident"][:, :]).then_inc(s_at_ps, 1)
                wait_count(pe, s_hotT, q)
                pe.wait_ge(s_hot, q + 1)
                for j in range(G):
                    mm = pe.transpose(bank[0][0:P, j * 128:(j + 1) * 128], hot[:, b % VR, j, :], g["ident"][:, :])
                mm.then_inc(s_hotT_ps, 1)

            def el_of_slots(q, b, window):
                wait_count(pe, s_z0, q)
                pe.wait_ge(s_hotT, q + 1)
                for j in range(G):
                    mm = pe.matmul(bank[3][:, j * NH:(j + 1) * NH], hotT[:, b % 2, j, :], tile_of(g["el"], window[j]),
                                   start=True, stop=True)
                mm.then_inc(s_el, 1)

            def features(q, b):
                wait_count(pe, s_relu, q)
                pe.wait_ge(s_at, q + 1)
                pe.matmul(bank[2][:, 0:G * HD], g["ones"][0:1, :], bt[:, :, :].rearrange("p j f -> p (j f)"), start=True, stop=False)
                pe.matmul(bank[2][:, 0:G * HD], attrT[:, b % 2, :], wt[:, :, :].rearrange("p j f -> p (j f)"),
                          start=False, stop=True).then_inc(s_time, 1)

            windows = [None]

            def step(s, r, b):
                if inside(s, NG) and b % 2 == 0:
                    windows[0] = node_tiles(nc, g, mybir.EngineType.PE, s)
                if inside(s - 2, NG):
                    sum_slots(s - 2, b - 2, (0, 1))
                if inside(s, NG):
                    transposes(s, b)
                if inside(s - 2, NG):
                    sum_slots(s - 2, b - 2, (2, 3))
                if inside(s, NG):
                    el_of_slots(s, b, windows[0][b % 2 * G:])
                    features(s, b)
            over_rounds(pe, step, ROUNDS, RING, REST + 2)

        @block.scalar
        def _(act):
            act.wait_ge(s_start, 3)

            def step(s, r, b):
                p = b % 2
                if inside(s, NG):
                    act.wait_ge(s_pay[b], r * 16 + 16)
                    act.copy(attr[:, p, :].rearrange("p (j f) -> p j f", j=G), pay[:, b, :, 0:AT]).then_inc(s_attr, 1)
                if inside(s - 1, NG):
                    act.wait_ge(s_z, s)
                    act.activation(val[:, (b - 1) % VR, :, O_W:O_T], z[:, 1 - p, :, :], ACT.Exp).then_inc(s_w_exp, 1)
                if inside(s, NG):
                    act.wait_ge(s_hotT_ps, s + 1)
                    act.copy(hotT[:, p, :, :], bank[0][0:P, :].rearrange("p (j s) -> p j s", j=G)).then_inc(s_hotT, 1)
                    act.wait_ge(s_at_ps, s + 1)
                    act.copy(attrT[:, p, :], bank[1][:, 0:128]).then_inc(s_at, 1)
                    act.wait_ge(s_time, s + 1)
                    act.activation(val[:, b % VR, :, O_T:O_C], bank[2][:, 0:G * HD].rearrange("p (j f) -> p j f", j=G),
                                   ACT.Relu).then_inc(s_relu, 1)
            over_rounds(act, step, ROUNDS, RING, REST + 1)


def gat_finish(nc, a, g):
    CH = 5
    agg, x = g["agg"], g["x"]
    with Stage(nc, "F") as st:
        den = st.sb("den", [P, T, NH])
        bias = st.sb("bias", [P, HD])
        low = st.sb("low", [P, T, NH * HD])
        one_less = st.sb("one_less", [P, 1])
        s_b, s_den, s_o, s_ob, s_exp, s_less, s_x, s_const = (st.sem(n) for n in (
            "bias", "den", "o", "o_bias", "exp", "x_less_1", "x", "const"))
        block = st.block()

        def heads(t):
            return agg[:, t, 0:O_W].rearrange("p t (h f) -> p t h f", h=NH)

        @block.sync
        def _(sp):
            sp.dma_start(bias[:, :], a["L0_gnn_b"].unsqueeze(0).broadcast_to([P, HD])).then_inc(s_b, 16)

        @block.vector
        def _(v):
            v.tensor_scalar(den[:, :, :], agg[:, :, O_W:O_T], 1e-12, None, ALU.max).then_inc(s_den, 1)
            v.wait_ge(s_den, 1)
            v.reciprocal(den[:, :, :], den[:, :, :]).then_inc(s_den, 1)
            v.wait_ge(s_den, 2)

            def divide(c):
                t = slice(c * CH, (c + 1) * CH)
                v.tensor_tensor(heads(t), heads(t), den[:, t, :].unsqueeze(3).broadcast_to([P, CH, NH, HD]),
                                ALU.mult).then_inc(s_o, 1)

            def add(c):
                t = slice(c * CH, (c + 1) * CH)
                v.wait_ge(s_less, c + 1)
                v.wait_ge(s_exp, c + 1)
                v.scalar_tensor_tensor(out=x[:, t, :], in0=agg[:, t, 0:O_W], scalar=0.0, in1=x[:, t, :],
                                       op0=ALU.max, op1=ALU.add).then_inc(s_x, 1)
                v.wait_ge(s_x, c * 2 + 1)
                v.scalar_tensor_tensor(out=x[:, t, :], in0=low[:, t, :], scalar=1.0, in1=x[:, t, :],
                                       op0=ALU.min, op1=ALU.add).then_inc(s_x, 1)

            def statistics(c):
                v.wait_ge(s_x, c * 2 + 2)
                for t in range(c * CH, (c + 1) * CH):
                    v.bn_stats(g["stats"][:, t, :], x[:, t, :])
            for c in range(T // CH):
                divide(c)
            for c in range(T // CH):
                add(c)
                if c:
                    statistics(c - 1)
            statistics(T // CH - 1)

        @block.gpsimd
        def _(gp):
            gp.memset(one_less[:, :], -1.0).then_inc(s_const, 1)
            gp.wait_ge(s_b, 16)
            for c in range(T // CH):
                t = slice(c * CH, (c + 1) * CH)
                gp.wait_ge(s_o, c + 1)
                gp.tensor_tensor(heads(t), heads(t), bias[:, :].unsqueeze(1).unsqueeze(1).broadcast_to([P, CH, NH, HD]),
                                 ALU.add).then_inc(s_ob, 1)

        @block.scalar
        def _(act):
            act.wait_ge(s_const, 1)
            act.copy(g["time"][:, :, :], agg[:, :, O_T:VW])
            for c in range(T // CH):
                t = slice(c * CH, (c + 1) * CH)
                act.activation(x[:, t, :], x[:, t, :], ACT.Identity, bias=one_less[:, :]).then_inc(s_less, 1)
            for c in range(T // CH):
                t = slice(c * CH, (c + 1) * CH)
                act.wait_ge(s_ob, c + 1)
                act.activation(low[:, t, :], agg[:, t, 0:O_W], ACT.Exp).then_inc(s_exp, 1)


def input_weights(st, layer):
    width = H0 if layer == 0 else 2 * H1
    t = st.sb("w_in", [128, NE * KC, width])
    return dict(t=t, sem=st.sem("w_in"), loads=NE * KC if layer == 0 else 2 * NE * KC)


def load_input_weights(eng, a, w, layer, n):
    for name, c, width in ((("L0_ffn_W1_T", 0, H0),) if layer == 0 else (("L1_ffn_w1_T", 0, H1), ("L1_ffn_w3_T", H1, H1))):
        rows = a[name].rearrange("e (k p) f -> p (e k) f", p=128)
        eng.dma_start(w["t"][:, bass.ds(n, 1), c:c + width], rows[:, bass.ds(n, 1), :]).then_inc(w["sem"], 16)


def moe(nc, a, g, layer, w_in):
    with Stage(nc, f"M{layer}") as keep:
        w_out = dict(t=keep.sb("w_out", [128, NE, H0 // 128 if layer == 0 else H1C, D]), sem=keep.sem("w_out"),
                     loads=NE * 1 + 2 if layer == 0 else NE * 2)
        if layer == 0:
            w_out["b1"] = keep.sb("b1", [128, NE, H0 // 128])
            w_out["b2"] = keep.sb("b2", [SLOT, NE, D])
        tile_map = keep.sb("tile_map", [1, FT], I32)
        tile_row = keep.sb("tile_row", [1, FT], I32)
        route(nc, a, g, layer, g["slot"], g["prob"], tile_map, tile_row, w_out)
        (relu_experts if layer == 0 else gated_experts)(nc, g, w_in, w_out, tile_map, tile_row)


def load_output_weights(eng, a, w, layer, pace):
    if layer == 0:
        eng.dma_start(w["b1"][:, :, :].rearrange("p e c -> p (e c)"), a["L0_ffn_b1_cols"]).then_inc(w["sem"], 16)
        eng.dma_start(w["b2"][:, :, :], a["L0_ffn_b2"].unsqueeze(0).broadcast_to([SLOT, NE, D])).then_inc(w["sem"], 16)
    for e in range(NE):
        eng.wait_ge(pace, 3 * e + 1)
        if layer == 0:
            eng.dma_start(w["t"][:, e, :, :], a["L0_ffn_W2_T"][e].rearrange("(k p) f -> p k f", p=128)).then_inc(w["sem"], 16)
        else:
            full = (H1C - 1) * 128
            eng.dma_start(w["t"][:, e, 0:H1C - 1, :], a["L1_ffn_w2_T"][e, 0:full].rearrange("(k p) f -> p k f", p=128)
                          ).then_inc(w["sem"], 16)
            eng.dma_start(w["t"][0:H1 - full, e, H1C - 1, :], a["L1_ffn_w2_T"][e, full:H1]).then_inc(w["sem"], 16)


def route(nc, a, g, layer, slot, prob, tile_map, tile_row, w_out):
    bank, x = g["bank"], g["x"]
    R = 6
    ROUNDS, REST = 3, T - 3 * R
    with Stage(nc, f"R{layer}") as st:
        xn = st.sb("xn", [P, R, D])
        xT = st.sb("xT", [128, 2, KC, P])
        wg = st.sb("wg", [128, KC, NE])
        bg = st.sb("bg", [1, NE])
        sc = st.sb("sc", [P, 2, NE])
        sorted_ = st.sb("sorted", [P, 2, NE])
        order = st.sb("order", [P, 2, NE], U32)
        hot = st.sb("hot", [P, 2, TOPK, NE])
        both = st.sb("both", [P, 2, NE])
        acc = st.sb("acc", [P, 2, NE])
        place = st.sb("place", [P, 2, NE])
        own = st.sb("own", [P, 2, TOPK, NE])
        placef = st.sb("placef", [P, 2, TOPK])
        ids = st.sb("ids", [P, R, TOPK], I32)
        score = st.sb("score", [P, T, NE])
        top = st.sb("top", [P, T, TOPK])
        places = st.sb("places", [P, T, TOPK])
        expert = st.sb("expert", [P, T, TOPK])
        moved = st.sb("moved", [P, T * TOPK, NE])
        psum_p = st.sb("psum_p", [P, T])
        own_f = st.sb("own_f", [P, T * TOPK])
        region = st.sb("region", [128, NE])
        region_lane = st.sb("region_lane", [128, NE])
        zeros = st.sb("zeros", [128, D])
        pad_f = st.sb("pad_f", [128, NE])
        pad_i = st.sb("pad_i", [128, NE], I32)
        fulli = st.sb("fulli", [P, NE], I32)
        full = st.sb("full", [P, NE])
        ends = st.sb("ends", [P, NE])
        skip = st.sb("skip", [P, NE])
        past = st.sb("past", [1, FT, NE])
        jump = st.sb("jump", [1, FT, NE])
        two = st.sb("two", [1, 2, FT])
        s_w, s_const = st.sem("weights"), st.sem("const")
        (s_ln, s_var, s_rstd, s_xn, s_tr, s_xT, s_sc, s_sb, s_max, s_idx, s_hot, s_both, s_rank, s_place, s_own, s_pf,
         s_ids, s_acc, s_total, s_pad, s_map, s_p, s_exp, s_go, s_padded, s_held, s_slot) = (st.sem(n) for n in (
             "ln", "var", "rstd", "xn", "transposed", "xT", "scored", "score_sb", "max", "index", "hot", "both", "rank",
             "place", "own_place", "place_sum", "ids", "acc", "total", "pad", "map", "prob", "exp", "go", "padded", "held", "slot"))
        s_sent = st.sems("sent", R)
        block = st.block()

        @block.sync
        def _(sp):
            if layer == 0:
                sp.dma_start(wg[:, :, :], a["L0_ffn_Wg_T"].rearrange("(k p) f -> p k f", p=128)).then_inc(s_w, 16)
                sp.dma_start(bg[:, :], a["L0_ffn_bg"].unsqueeze(0)).then_inc(s_w, 16)
            else:
                sp.dma_start(wg[:, :, :], a["L1_ffn_router_w_T"].rearrange("(k p) f -> p k f", p=128)).then_inc(s_w, 16)
            load_output_weights(sp, a, w_out, layer, s_ids)

        @block.gpsimd
        def _(gp):
            gp.iota(region[:, :], [[REG, NE]], base=0, channel_multiplier=0,
                    allow_small_or_imprecise_dtypes=True).then_inc(s_const, 1)
            gp.iota(region_lane[:, :], [[REG, NE]], base=0, channel_multiplier=1,
                    allow_small_or_imprecise_dtypes=True).then_inc(s_const, 1)
            gp.memset(acc[:, :, :], 0.0).then_inc(s_const, 1)
            gp.memset(zeros[:, :], 0.0).then_inc(s_const, 1)
            gp.wait_ge(s_const, 4)

            def send(t, r, b):
                gp.wait_ge(s_ids, t + 1)
                gp.sem_inc(s_go, 1)
                for c in range(TOPK):
                    gp.indirect_dma_start(g["xs"], bass.IndirectOffsetOnAxis(ap=ids[:, b, c:c + 1], axis=0),
                                          xn[:, b, :], None).then_inc(s_sent[b], 16)
            over_rounds(gp, send, ROUNDS, R, REST)
            gp.wait_ge(s_pad, 3)
            for e in range(NE):
                gp.indirect_dma_start(g["xs"], bass.IndirectOffsetOnAxis(ap=pad_i[:, e:e + 1], axis=0),
                                      zeros[:, :], None).then_inc(s_padded, 16)
            gp.wait_ge(s_padded, 16 * NE)
            for b in range(R):
                gp.wait_ge(s_sent[b], (T - b + R - 1) // R * 16 * TOPK)


        @block.vector
        def _(v):
            close_stats(v, g["stats"], g["mv"], g["rstd"], s_ln, 0, s_var)
            v.wait_ge(s_const, 4)
            v.wait_ge(s_rstd, 1)
            number = g["bin_no"][0:P, 0:NE].unsqueeze(1).broadcast_to([P, TOPK, NE])

            def normalise(t, r, b):
                wait_count(v, s_sent[b], r * (16 * TOPK))
                v.tensor_scalar(xn[:, b, :], tile_of(x, t), tile_of(g["mv"], t)[:, 0:1], g["rstd"][:, bass.ds(t, 1)],
                                ALU.subtract, ALU.mult).then_inc(s_xn, 1)

            def step(t, r, b):
                now, last = inside(t, T), inside(t - 1, T)
                p, q = b % 2, 1 - b % 2
                if inside(t + 2, T):
                    normalise(t + 2, r if b + 2 < R else r + 1, (b + 2) % R)
                if now:
                    v.wait_ge(s_sc, t + 1)
                    v.tensor_copy(sc[:, p, :], bank[2 + p][0:P, 0:NE]).then_inc(s_sb, 1)
                if last:
                    v.wait_ge(s_rank, t)
                    v.tensor_tensor(place[:, q, :], bank[6 + q][0:P, 0:NE], region[0:P, :], ALU.add).then_inc(s_place, 1)
                if now:
                    v.wait_ge(s_sb, t + 1)
                    v.sem_inc(s_held, 1)
                    v.max(out=sorted_[:, p, :], in_=sc[:, p, :]).then_inc(s_max, 1)
                if last:
                    v.wait_ge(s_place, t)
                    v.tensor_tensor(own[:, q, :, :], hot[:, q, :, :], place[:, q, :].unsqueeze(1).broadcast_to([P, TOPK, NE]),
                                    ALU.mult).then_inc(s_own, 1)
                if now:
                    v.wait_ge(s_max, t + 1)
                    v.sem_inc(s_held, 1)
                    v.max_index(out=order[:, p, :], in_max=sorted_[:, p, :], in_values=sc[:, p, :]).then_inc(s_idx, 1)
                if last:
                    v.wait_ge(s_own, t)
                    v.tensor_reduce(placef[:, q, :], own[:, q, :, :], AXX, ALU.add).then_inc(s_pf, 1)
                if now:
                    v.wait_ge(s_idx, t + 1)
                    v.tensor_tensor(hot[:, p, :, :], order[:, p, 0:TOPK].unsqueeze(2).broadcast_to([P, TOPK, NE]), number,
                                    ALU.is_equal).then_inc(s_hot, 1)
                if last:
                    v.wait_ge(s_pf, t)
                    v.tensor_copy(tile_of(places, t - 1), placef[:, q, :])
                    v.tensor_copy(tile_of(expert, t - 1), order[:, q, 0:TOPK])
                    v.tensor_copy(ids[:, (b - 1) % R, :], placef[:, q, :]).then_inc(s_ids, 1)
                if now:
                    v.wait_ge(s_hot, t + 1)
                    v.tensor_tensor(both[:, p, :], hot[:, p, 0, :], hot[:, p, 1, :], ALU.add).then_inc(s_both, 1)
                    v.tensor_copy(tile_of(top, t), sorted_[:, p, 0:TOPK])
                    if layer == 1:
                        v.tensor_copy(tile_of(score, t), sc[:, p, :])
                    v.wait_ge(s_both, t + 1)
                    v.tensor_tensor(acc[:, p, :], acc[:, q, :], both[:, p, :], ALU.add).then_inc(s_acc, 1)
            normalise(0, 0, 0)
            normalise(1, 0, 1)
            over_rounds(v, step, ROUNDS, R, REST + 1)

            v.wait_ge(s_total, 1)
            v.tensor_tensor(pad_f[:, :], bank[0][:, 0:NE], region_lane[:, :], ALU.add).then_inc(s_pad, 1)
            v.tensor_scalar(fulli[:, :], bank[0][0:P, 0:NE], float(SLOT - 1), None, ALU.add).then_inc(s_map, 1)
            v.wait_ge(s_pad, 1)
            v.tensor_copy(pad_i[:, :], pad_f[:, :]).then_inc(s_pad, 1)
            v.wait_ge(s_pad, 2)
            v.sem_inc(s_pad, 1)
            v.wait_ge(s_map, 1)
            v.tensor_scalar(fulli[:, :], fulli[:, :], 7, 7, ALU.logical_shift_right, ALU.logical_shift_left).then_inc(s_map, 1)
            v.wait_ge(s_map, 2)
            v.tensor_copy(full[:, :], fulli[:, :]).then_inc(s_map, 1)
            v.wait_ge(s_map, 3)
            v.tensor_tensor_scan(ends[:, :], g["ones"][0:P, 0:1].broadcast_to([P, NE]), full[:, :], 0.0,
                                 ALU.mult, ALU.add).then_inc(s_map, 1)
            v.tensor_scalar(skip[:, :], full[:, :], -1.0, float(REG), ALU.mult, ALU.add).then_inc(s_map, 1)
            v.wait_ge(s_map, 5)
            at = g["tile_at"][0:1, 0:FT]
            v.tensor_tensor(past[:, :, :], at.unsqueeze(2).broadcast_to([1, FT, NE]),
                            ends[0:1, :].unsqueeze(1).broadcast_to([1, FT, NE]), ALU.is_ge).then_inc(s_map, 1)
            v.wait_ge(s_map, 6)
            v.tensor_tensor(jump[:, :, :], past[:, :, :], skip[0:1, :].unsqueeze(1).broadcast_to([1, FT, NE]),
                            ALU.mult).then_inc(s_map, 1)
            v.tensor_reduce(two[:, 0, :], past[:, :, 0:NE - 1], AXX, ALU.add).then_inc(s_map, 1)
            v.wait_ge(s_map, 8)
            v.tensor_copy(tile_map[:, :], two[:, 0, :]).then_inc(s_map, 1)
            v.tensor_reduce(two[:, 1, :], jump[:, :, :], AXX, ALU.add).then_inc(s_map, 1)
            v.wait_ge(s_map, 10)
            v.tensor_tensor(tile_row[:, :], two[:, 1, :], at, ALU.add).then_inc(s_map, 1)
            v.tensor_tensor(ends[:, :], ends[:, :], full[:, :], ALU.subtract).then_inc(s_slot, 1)
            v.tensor_tensor(moved[:, :, :], expert[:, :, :].rearrange("p t k -> p (t k)").unsqueeze(2).broadcast_to([P, T * TOPK, NE]),
                            g["bin_no"][0:P, 0:NE].unsqueeze(1).broadcast_to([P, T * TOPK, NE]), ALU.is_equal).then_inc(s_slot, 1)
            v.wait_ge(s_slot, 2)
            v.tensor_tensor(ends[:, :], ends[:, :], region[0:P, :], ALU.subtract).then_inc(s_slot, 1)
            v.wait_ge(s_slot, 3)
            v.tensor_tensor(moved[:, :, :], moved[:, :, :], ends[:, :].unsqueeze(1).broadcast_to([P, T * TOPK, NE]),
                            ALU.mult).then_inc(s_slot, 1)
            v.wait_ge(s_slot, 4)
            v.tensor_reduce(own_f[:, :], moved[:, :, :], AXX, ALU.add).then_inc(s_slot, 1)
            v.wait_ge(s_slot, 5)
            v.tensor_tensor(slot[:, :, :].rearrange("p t k -> p (t k)"), own_f[:, :],
                            places[:, :, :].rearrange("p t k -> p (t k)"), ALU.add).then_inc(s_slot, 1)

            if layer == 1:
                v.tensor_tensor(score[:, :, :], score[:, :, :], top[:, :, 0].unsqueeze(2).broadcast_to([P, T, NE]),
                                ALU.subtract).then_inc(s_p, 1)
            v.tensor_tensor(prob[:, :, :], top[:, :, :], top[:, :, 0].unsqueeze(2).broadcast_to([P, T, TOPK]),
                            ALU.subtract).then_inc(s_p, 1)
            n = 1 + layer
            v.wait_ge(s_exp, n)
            if layer == 1:
                v.tensor_reduce(psum_p[:, :], score[:, :, :], AXX, ALU.add).then_inc(s_p, 1)
                v.wait_ge(s_p, n + 1)
                v.reciprocal(psum_p[:, :], psum_p[:, :]).then_inc(s_p, 1)
                v.wait_ge(s_p, n + 2)
                v.tensor_tensor(prob[:, :, :], prob[:, :, :], psum_p[:, :].unsqueeze(2).broadcast_to([P, T, TOPK]),
                                ALU.mult).then_inc(s_p, 1)
                n += 3
                v.wait_ge(s_p, n)
            v.tensor_tensor(psum_p[:, :], prob[:, :, 0], prob[:, :, 1], ALU.add).then_inc(s_p, 1)
            v.wait_ge(s_p, n + 1)
            if layer == 1:
                v.tensor_scalar(psum_p[:, :], psum_p[:, :], 1e-9, None, ALU.add).then_inc(s_p, 1)
                n += 1
                v.wait_ge(s_p, n + 1)
            v.reciprocal(psum_p[:, :], psum_p[:, :]).then_inc(s_p, 1)
            v.wait_ge(s_p, n + 2)
            v.tensor_tensor(prob[:, :, :], prob[:, :, :], psum_p[:, :].unsqueeze(2).broadcast_to([P, T, TOPK]),
                            ALU.mult).then_inc(s_p, 1)

        @block.tensor
        def _(pe):
            pe.wait_ge(s_w, 32 - 16 * layer)

            def turn(t, b):
                wait_count(pe, s_xT, t - 1)
                pe.wait_ge(s_xn, t + 1)
                for c in range(KC):
                    mm = pe.transpose(bank[4 + b % 2][:, c * 128:c * 128 + P], xn[:, b, c * 128:(c + 1) * 128], g["ident"][0:P, 0:P])
                mm.then_inc(s_tr, 1)

            def score_tile(t, p):
                wait_count(pe, s_sb, t - 1)
                pe.wait_ge(s_xT, t + 1)
                for c in range(KC):
                    mm = pe.matmul(bank[2 + p][0:P, 0:NE], xT[:, p, c, :], wg[:, c, :], start=c == 0,
                                   stop=c == 1 and layer == 1)
                if layer == 0:
                    mm = pe.matmul(bank[2 + p][0:P, 0:NE], g["ones"][0:1, 0:P], bg[:, :], start=False, stop=True)
                mm.then_inc(s_sc, 1)

            def step(t, r, b):
                p = b % 2
                if inside(t + 1, T):
                    score_tile(t + 1, 1 - p)
                if inside(t + 2, T):
                    turn(t + 2, (b + 2) % R)
                wait_count(pe, s_place, t - 1)
                pe.wait_ge(s_both, t + 1)
                pe.matmul(bank[6 + p][0:P, 0:NE], g["before"][0:P, 0:P], both[:, p, :], start=True, stop=False)
                wait_count(pe, s_acc, t)
                pe.matmul(bank[6 + p][0:P, 0:NE], g["ones"][0:P, 0:P], acc[:, 1 - p, :], start=False, stop=True).then_inc(s_rank, 1)
            turn(0, 0)
            turn(1, 1)
            score_tile(0, 0)
            over_rounds(pe, step, ROUNDS, R, REST)
            pe.wait_ge(s_acc, T)
            pe.matmul(bank[0][:, 0:NE], g["ones"][0:P, :], acc[:, (T - 1) % 2, :], start=True, stop=True).then_inc(s_total, 1)

        @block.scalar
        def _(act):
            act.wait_ge(s_var, 1)
            act.activation(g["rstd"][:, :], g["rstd"][:, :], ACT.Sqrt).then_inc(s_rstd, 1)

            def turned(t, b):
                act.wait_ge(s_tr, t + 1)
                act.copy(xT[:, b, :, :], bank[4 + b][:, 0:256].rearrange("p (c q) -> p c q", c=2)[:, :, 0:P]).then_inc(s_xT, 1)
            over_tiles(act, turned)
            act.wait_ge(s_p, 1 + layer)
            if layer == 1:
                act.activation(score[:, :, :], score[:, :, :], ACT.Exp).then_inc(s_exp, 1)
            act.activation(prob[:, :, :], prob[:, :, :], ACT.Exp).then_inc(s_exp, 1)


def move_tiles(sp, g, tile_row, xt, y, s_x, s_tr, s_ys, s_st):
    ys = g["ys"].rearrange("(t p) f -> t p f", p=SLOT)

    def load(t, b):
        row = sp.value_load(tile_row[0:1, bass.ds(t, 1)], min_val=0, max_val=XS - SLOT)
        wait_count(sp, s_tr, t - 1)
        sp.dma_start(xt[:, b, :], g["xs"][bass.ds(row, SLOT), :]).then_inc(s_x[b], 16)

    def tile(t, b):
        if inside(t + 3, FT):
            load(t + 3, 1 - b)
        sp.wait_ge(s_ys, t + 1)
        sp.dma_start(ys[bass.ds(t, 1), :, :].rearrange("o p f -> (o p) f"), y[:, b, :]).then_inc(s_st[b], 16)
    for t in range(3):
        load(t, t % 2)
    over_tiles(sp, tile, FT, 4)
    sp.wait_ge(s_st[0], FT // 2 * 16)
    sp.wait_ge(s_st[1], FT // 2 * 16)


def relu_experts(nc, g, w_in, w_out, tile_map, tile_row):
    bank = g["bank"]
    HC = H0 // 128
    hb = [[bank[0], bank[1]], [bank[2], bank[3]]]
    xb, yb = bank[7], bank[6]
    with Stage(nc, "E0") as st:
        xt = st.sb("xt", [SLOT, 2, D])
        xT = st.sb("xT", [128, 2, KC, SLOT])
        w1 = st.sb("w1", [128, 2, KC, H0])
        hT = st.sb("hT", [128, 2, HC, SLOT])
        y = st.sb("y", [SLOT, 2, D])
        s_x, s_st = st.sems("x"), st.sems("stored")
        s_tr, s_xT, s_w1, s_h, s_hT, s_y, s_ys = (st.sem(n) for n in (
            "x_transposed", "xT", "w1", "h", "hT", "y", "y_sb"))
        block = st.block()

        @block.sync
        def _(sp):
            move_tiles(sp, g, tile_row, xt, y, s_x, s_tr, s_ys, s_st)


        @block.tensor
        def _(pe):
            def turn(t, b):
                pe.wait_ge(s_x[b], (t - b) * 8 + 16)
                wait_count(pe, s_xT, t)
                for c in range(KC):
                    mm = pe.transpose(xb[:, c * 128:(c + 1) * 128], xt[:, b, c * 128:(c + 1) * 128], g["ident"][:, :])
                mm.then_inc(s_tr, 1)

            def hidden(t, b):
                wait_count(pe, s_hT, t - 1)
                pe.wait_ge(s_w1, t + 1)
                pe.wait_ge(s_xT, t + 1)
                for m in range(HC):
                    for c in range(KC):
                        mm = pe.matmul(hb[b][m // 4][:, m % 4 * 128:(m % 4 + 1) * 128], w1[:, b, c, m * 128:(m + 1) * 128],
                                       xT[:, b, c, :], start=c == 0, stop=c == 1)
                mm.then_inc(s_h, 1)

            def step(t, b):
                if inside(t + 1, FT):
                    hidden(t + 1, 1 - b)
                if inside(t + 2, FT):
                    turn(t + 2, b)
                e = pe.value_load(tile_map[0:1, bass.ds(t, 1)], min_val=0, max_val=NE - 1)
                wait_count(pe, s_ys, t)
                pe.wait_ge(s_hT, t + 1)
                for n in range(HC):
                    mm = pe.matmul(yb[:, 0:D], hT[:, b, n, :], w_out["t"][:, bass.ds(e, 1), n, :].rearrange("p o f -> p (o f)"),
                                   start=n == 0, stop=n == HC - 1)
                mm.then_inc(s_y, 1)
            turn(0, 0)
            turn(1, 1)
            hidden(0, 0)
            pe.wait_ge(w_out["sem"], 16 * w_out["loads"])
            over_tiles(pe, step, FT, 4)

        @block.vector
        def _(v):
            def fix_weights(t, b):
                e = v.value_load(tile_map[0:1, bass.ds(t, 1)], min_val=0, max_val=NE - 1)
                wait_count(v, s_h, t - 1)
                v.tensor_copy(w1[:, b, :, :], w_in["t"][:, bass.ds(e * KC, KC), :]).then_inc(s_w1, 1)

            def step(t, b):
                if inside(t + 2, FT):
                    fix_weights(t + 2, b)
                e = v.value_load(tile_map[0:1, bass.ds(t, 1)], min_val=0, max_val=NE - 1)
                wait_count(v, s_st[b], (t - b) * 8)
                v.wait_ge(s_y, t + 1)
                v.tensor_tensor(y[:, b, :], yb[:, 0:D], tile_of(w_out["b2"], e), ALU.add).then_inc(s_ys, 1)
            v.wait_ge(w_in["sem"], 16 * w_in["loads"])
            fix_weights(0, 0)
            fix_weights(1, 1)
            v.wait_ge(w_out["sem"], 16 * w_out["loads"])
            over_tiles(v, step, FT, 4)

        @block.scalar
        def _(act):
            def turned(t, b):
                act.wait_ge(s_tr, t + 1)
                act.copy(xT[:, b, :, :], xb[:, 0:D].rearrange("p (c q) -> p c q", c=2)).then_inc(s_xT, 1)

            def relu(t, b):
                e = act.value_load(tile_map[0:1, bass.ds(t, 1)], min_val=0, max_val=NE - 1)
                wait_count(act, s_y, t - 1)
                act.wait_ge(s_h, t + 1)
                for n in range(HC):
                    o = act.activation(hT[:, b, n, :], hb[b][n // 4][:, n % 4 * 128:(n % 4 + 1) * 128], ACT.Relu,
                                       bias=tile_of(w_out["b1"], e)[:, n:n + 1])
                o.then_inc(s_hT, 1)

            def step(t, b):
                if inside(t + 1, FT):
                    relu(t + 1, 1 - b)
                if inside(t + 2, FT):
                    turned(t + 2, b)
            turned(0, 0)
            turned(1, 1)
            act.wait_ge(w_out["sem"], 16 * w_out["loads"])
            relu(0, 0)
            over_tiles(act, step, FT, 4)


def gated_experts(nc, g, w_in, w_out, tile_map, tile_row):
    bank = g["bank"]
    HB = bank[0:4]
    HC = H1C
    tb, xb, yb = [bank[4], bank[5]], bank[7], bank[6]
    half = H1 // 2
    chunks = [(c * 128, min(128, H1 - c * 128)) for c in range(HC)]
    with Stage(nc, "E1") as st:
        xt = st.sb("xt", [SLOT, 2, D])
        xT = st.sb("xT", [128, 2, KC, SLOT])
        h = st.sb("h", [SLOT, H1])
        hT = st.sb("hT", [128, 2, HC, SLOT])
        y = st.sb("y", [SLOT, 2, D])
        s_x, s_st = st.sems("x"), st.sems("stored")
        s_tr, s_xT, s_h, s_hs, s_hd, s_hTp, s_hT, s_y, s_ys = (st.sem(n) for n in (
            "x_transposed", "xT", "h", "h_gate", "h_sb", "h_transposed", "hT", "y", "y_sb"))
        block = st.block()

        @block.sync
        def _(sp):
            move_tiles(sp, g, tile_row, xt, y, s_x, s_tr, s_ys, s_st)


        @block.tensor
        def _(pe):
            def turn(t, b):
                pe.wait_ge(s_x[b], (t - b) * 8 + 16)
                wait_count(pe, s_xT, t)
                for c in range(KC):
                    mm = pe.transpose(xb[:, c * 128:(c + 1) * 128], xt[:, b, c * 128:(c + 1) * 128], g["ident"][:, :])
                mm.then_inc(s_tr, 1)

            def hidden(t, b):
                e = pe.value_load(tile_map[0:1, bass.ds(t, 1)], min_val=0, max_val=NE - 1)
                pe.wait_ge(s_xT, t + 1)
                for n in range(4):
                    for c in range(KC):
                        mm = pe.matmul(HB[n][:, 0:half], xT[:, b, c, :],
                                       w_in["t"][:, bass.ds(e * KC + c, 1), n * half:(n + 1) * half].rearrange("p o f -> p (o f)"),
                                       start=c == 0, stop=c == 1)
                mm.then_inc(s_h, 1)

            def tile(t, b):
                pe.wait_ge(s_hd, t + 1)
                wait_count(pe, s_hT, t)
                for n, (c0, w) in enumerate(chunks):
                    mm = pe.transpose(tb[n // 4][0:w, n % 4 * 128:n % 4 * 128 + SLOT], h[:, c0:c0 + w], g["ident"][:, :])
                mm.then_inc(s_hTp, 1)
                if inside(t + 2, FT):
                    turn(t + 2, b)
                if inside(t + 1, FT):
                    hidden(t + 1, 1 - b)
                e = pe.value_load(tile_map[0:1, bass.ds(t, 1)], min_val=0, max_val=NE - 1)
                wait_count(pe, s_ys, t)
                pe.wait_ge(s_hT, t + 1)
                for n, (c0, w) in enumerate(chunks):
                    mm = pe.matmul(yb[:, 0:D], hT[0:w, b, n, :], w_out["t"][0:w, bass.ds(e, 1), n, :].rearrange("p o f -> p (o f)"),
                                   start=n == 0, stop=n == HC - 1)
                mm.then_inc(s_y, 1)
            turn(0, 0)
            turn(1, 1)
            pe.wait_ge(w_in["sem"], 16 * w_in["loads"])
            hidden(0, 0)
            pe.wait_ge(w_out["sem"], 16 * w_out["loads"])
            over_tiles(pe, tile, FT, 4)

        @block.vector
        def _(v):
            def gate(t):
                wait_count(v, s_hTp, t)
                v.wait_ge(s_hs, t + 1)
                for n in range(2):
                    cols = slice(n * half, (n + 1) * half)
                    o = v.tensor_tensor(h[:, cols], h[:, cols], HB[2 + n][:, 0:half], ALU.mult)
                o.then_inc(s_hd, 1)

            def tile(t, b):
                if inside(t + 1, FT):
                    gate(t + 1)
                wait_count(v, s_st[b], (t - b) * 8)
                v.wait_ge(s_y, t + 1)
                v.tensor_copy(y[:, b, :], yb[:, 0:D]).then_inc(s_ys, 1)
            gate(0)
            over_tiles(v, tile, FT, 4)

        @block.scalar
        def _(act):
            def turned(t, b):
                act.wait_ge(s_tr, t + 1)
                act.copy(xT[:, b, :, :], xb[:, 0:D].rearrange("p (c q) -> p c q", c=2)).then_inc(s_xT, 1)

            def silu(t):
                wait_count(act, s_hTp, t)
                act.wait_ge(s_h, t + 1)
                for n in range(2):
                    o = act.activation(h[:, n * half:(n + 1) * half], HB[n][:, 0:half], ACT.Silu)
                o.then_inc(s_hs, 1)

            def tile(t, b):
                act.wait_ge(s_hTp, t + 1)
                w = H1 - (HC - 1) * 128
                act.copy(hT[:, b, 0:4, :], tb[0][:, :].rearrange("p (c q) -> p c q", c=4))
                act.copy(hT[:, b, 4, :], tb[1][:, 0:128])
                act.copy(hT[0:w, b, 5, :], tb[1][0:w, 128:256]).then_inc(s_hT, 1)
                if inside(t + 2, FT):
                    turned(t + 2, b)
                if inside(t + 1, FT):
                    silu(t + 1)
            turned(0, 0)
            turned(1, 1)
            silu(0)
            over_tiles(act, tile, FT, 4)


def combine(nc, g, out):
    x = g["x"]
    R = 4
    with Stage(nc, "C") as st:
        yg = st.sb("yg", [P, R, TOPK, D])
        ids = st.sb("ids", [P, R, TOPK], I32)
        s_y = st.sems("y", R)
        s_x0, s_x, s_ids, s_go, s_out = st.sem("x0"), st.sem("x"), st.sem("ids"), st.sem("go"), st.sem("out")
        block = st.block()

        @block.gpsimd
        def _(gp):
            def fetch(t, r, b):
                wait_count(gp, s_x, t - R + 1)
                gp.tensor_copy(ids[:, b, :], tile_of(g["slot"], t)).then_inc(s_ids, 1)
                gp.wait_ge(s_ids, t + 1)
                gp.sem_inc(s_go, 1)
                for c in range(TOPK):
                    gp.indirect_dma_start(yg[:, b, c, :], None, g["ys"],
                                          bass.IndirectOffsetOnAxis(ap=ids[:, b, c:c + 1], axis=0)).then_inc(s_y[b], 16)
            over_rounds(gp, fetch, T // R, R, T % R)

        @block.vector
        def _(v):
            def add(t, r, b):
                v.wait_ge(s_y[b], r * (16 * TOPK) + 16 * TOPK)
                v.scalar_tensor_tensor(out=tile_of(x, t), in0=yg[:, b, 0, :], scalar=tile_of(g["prob"], t)[:, 0:1],
                                       in1=tile_of(x, t), op0=ALU.mult, op1=ALU.add).then_inc(s_x0, 1)
                v.wait_ge(s_x0, t + 1)
                v.scalar_tensor_tensor(out=tile_of(x, t), in0=yg[:, b, 1, :], scalar=tile_of(g["prob"], t)[:, 1:2],
                                       in1=tile_of(x, t), op0=ALU.mult, op1=ALU.add).then_inc(s_x, 1)
            over_rounds(v, add, T // R, R, T % R)

        rows = out.rearrange("(t p) f -> t p f", p=P)

        @block.sync
        def _(sp):
            with sp.Fori(0, T) as t:
                sp.wait_ge(s_x, t + 1)
                sp.dma_start(rows[bass.ds(t, 1), :, :].rearrange("o p f -> (o p) f"), tile_of(x, t)).then_inc(s_out, 16)
            sp.wait_ge(s_out, T * 16)


L1H = 8
KV = L1H * HD


def update_weights(st):
    return dict(wd=st.sb("wd", [128, KC, HD]), wf=st.sb("wf", [2 * HD, HD]), wu=st.sb("wu", [HD, D]),
                bd=st.sb("bd", [HD, 1]), bf=st.sb("bf", [HD, 1]), bo=st.sb("bo", [P, 2, D]), sem=st.sem("weights"))


def load_update_weights(eng, a, w):
    for dst, src in ((w["wd"][:, :, :], a["L1_gnn_W_down_T"].rearrange("(k p) f -> p k f", p=128)),
                     (w["wf"][:, :], a["L1_gnn_W_fusion_T"]), (w["wu"][:, :], a["L1_gnn_W_up_T"]),
                     (w["bd"][:, :], a["L1_gnn_b_down_col"]), (w["bf"][:, :], a["L1_gnn_b_fusion_col"]),
                     (w["bo"][:, 0, :], a["L1_gnn_b_up"].unsqueeze(0).broadcast_to([P, D])),
                     (w["bo"][:, 1, :], a["L1_mix_b_out"].unsqueeze(0).broadcast_to([P, D]))):
        eng.dma_start(dst, src).then_inc(w["sem"], 16)


def l1_keys_values(nc, a, g, w_in, w_up):
    bank, x = g["bank"], g["x"]
    R = 4
    with Stage(nc, "K") as st:
        yg = st.sb("yg", [P, R, TOPK, D])
        ids = st.sb("ids", [P, R, TOPK], I32)
        pr = st.sb("pr", [P, R, TOPK])
        wkv = st.sb("wkv", [128, KC, 2 * KV])
        mean = st.sb("mean", [128, KC, 2 * L1H])
        wq = st.sb("wq", [128, KV // 128, D])
        wo = st.sb("wo", [128, KV // 128, D])
        xn = st.sb("xn", [P, 2, D])
        xT = st.sb("xT", [128, 2, KC, P])
        eps = st.sb("eps", [P, 1])
        halves = st.sb("halves", [P, 2, 6])
        mv = st.sb("mean_var", [P, 2, 2])
        root = st.sb("root", [P, 2, 1])
        sq = st.sb("sq", [P, 2 * KV])
        var = st.sb("var", [P, 2, 2 * L1H])
        kvn = st.sb("kvn", [P, 2, 2 * KV])
        dots = st.sb("dots", [128, KV // 128, 128])
        gm = st.sb("gm", [128, KV // 128, D])
        s_y = st.sems("y", R)
        s_ids, s_go, s_scaled, s_x0, s_x = (st.sem(n) for n in ("ids", "go", "scaled", "x0", "x"))
        s_w, s_cw, s_zero = st.sem("weights"), st.sem("centred"), st.sem("zero")
        s_bn, s_mv, s_rx, s_rstd, s_xn, s_tr, s_xT, s_kv, s_sq, s_v1, s_r1, s_inv, s_kvn, s_dot, s_dsb, s_g, s_gsb, s_c = (
            st.sem(n) for n in ("bn", "mean_var", "root", "rstd", "xn", "transposed", "xT", "kv", "squares", "kv_var",
                                "kv_root", "kv_rstd", "kv_normed", "dots", "dots_sb", "gm_psum", "gm", "c1"))
        block = st.block()

        @block.sync
        def _(sp):
            sp.dma_start(wkv[:, :, :], a["L1_mix_w_kv_T"].rearrange("(k p) f -> p k f", p=128)).then_inc(s_w, 16)
            sp.dma_start(wq[:, :, :], a["L1_mix_w_qkv"][0:KV].rearrange("(k p) f -> p k f", p=128)).then_inc(s_w, 16)
            sp.dma_start(wo[:, :, :], a["L1_mix_w_out_T"].rearrange("(k p) f -> p k f", p=128)).then_inc(s_w, 16)
            for n in range(NE * KC):
                sp.wait_ge(s_x, n + 2)
                load_input_weights(sp, a, w_in, 1, n)
            load_update_weights(sp, a, w_up)

        @block.gpsimd
        def _(gp):
            gp.memset(dots[:, :, :], 0.0).then_inc(s_zero, 1)
            gp.memset(eps[:, :], EPS).then_inc(s_zero, 1)

            def fetch(t, b):
                gp.tensor_copy(pr[:, b, :], tile_of(g["prob"], t))
                gp.tensor_copy(ids[:, b, :], tile_of(g["slot"], t)).then_inc(s_ids, 1)
                gp.wait_ge(s_ids, t + 1)
                gp.sem_inc(s_go, 1)
                for c in range(TOPK):
                    gp.indirect_dma_start(yg[:, b, c, :], None, g["ys"],
                                          bass.IndirectOffsetOnAxis(ap=ids[:, b, c:c + 1], axis=0)).then_inc(s_y[b], 16)

            def step(t, r, b):
                if inside(t + 2, T):
                    wait_count(gp, s_x, t - 1)
                    fetch(t + 2, (b + 2) % R)
                gp.wait_ge(s_scaled, t + 1)
                gp.tensor_tensor(yg[:, b, 0, :], yg[:, b, 0, :], yg[:, b, 1, :], ALU.add).then_inc(s_x0, 1)
                gp.wait_ge(s_x0, t + 1)
                gp.tensor_tensor(tile_of(x, t), tile_of(x, t), yg[:, b, 0, :], ALU.add).then_inc(s_x, 1)
            fetch(0, 0)
            fetch(1, 1)
            over_rounds(gp, step, T // R - 1, R, T % R + R)


        @block.vector
        def _(v):
            def statistics(t, b):
                v.wait_ge(s_x, t + 1)
                v.sem_inc(s_go, 1)
                v.bn_stats(halves[:, b, :], tile_of(x, t)).then_inc(s_bn, 1)

            def mean_var(t, b):
                v.wait_ge(s_bn, t + 1)
                v.sem_inc(s_go, 1)
                v.bn_aggr(mv[:, b, :], halves[:, b, :]).then_inc(s_mv, 1)

            def keep_mean(t, b):
                v.wait_ge(s_mv, t + 1)
                v.tensor_copy(g["mv"][:, bass.ds(t, 1), 0:1].rearrange("p o f -> p (o f)"), mv[:, b, 0:1])

            def invert(t, b):
                v.wait_ge(s_rx, t + 1)
                v.reciprocal(g["rstd"][:, bass.ds(t, 1)], root[:, b, :]).then_inc(s_rstd, 1)

            def normalise(t, b):
                wait_count(v, s_tr, t - 1)
                v.wait_ge(s_rstd, t + 1)
                v.tensor_scalar(xn[:, b, :], tile_of(x, t), tile_of(g["mv"], t)[:, 0:1], g["rstd"][:, bass.ds(t, 1)],
                                ALU.subtract, ALU.mult).then_inc(s_xn, 1)

            v.wait_ge(s_w, 48)
            heads = wkv[:, :, :].rearrange("p k (h f) -> p (k h) f", f=HD)
            m = mean[:, :, :].rearrange("p k h -> p (k h)")
            v.tensor_reduce(m, heads, AXX, ALU.add).then_inc(s_cw, 1)
            v.wait_ge(s_cw, 1)
            v.tensor_scalar(m, m, 1.0 / HD, None, ALU.mult).then_inc(s_cw, 1)
            v.wait_ge(s_cw, 2)
            v.tensor_tensor(heads, heads, m.unsqueeze(2).broadcast_to([128, KC * 2 * L1H, HD]), ALU.subtract).then_inc(s_cw, 1)
            for t in range(3):
                statistics(t, t % 2)
                if t == 2:
                    v.wait_ge(s_rx, 1)
                mean_var(t, t % 2)
                keep_mean(t, t % 2)
                invert(t, t % 2)
                if t < 2:
                    normalise(t, t)

            def step(t, b):
                if inside(t + 2, T):
                    normalise(t + 2, b)
                if inside(t + 3, T):
                    statistics(t + 3, 1 - b)
                    mean_var(t + 3, 1 - b)
                v.wait_ge(s_sq, t + 1)
                v.tensor_reduce(var[:, b, :], sq[:, :].rearrange("p (h f) -> p h f", f=HD), AXX, ALU.add).then_inc(s_v1, 1)
                if inside(t + 3, T):
                    invert(t + 3, 1 - b)
                    keep_mean(t + 3, 1 - b)
                v.wait_ge(s_r1, t + 1)
                v.reciprocal(var[:, b, :], var[:, b, :]).then_inc(s_inv, 1)
                v.wait_ge(s_inv, t + 1)
                wait_count(v, s_dot, t - 1)
                for n in range(2):
                    o = v.tensor_tensor(kvn[:, b, n * KV:(n + 1) * KV].rearrange("p (h f) -> p h f", f=HD),
                                        bank[2 * n + b][0:P, :].rearrange("p (h f) -> p h f", f=HD),
                                        var[:, b, n * L1H:(n + 1) * L1H].unsqueeze(2).broadcast_to([P, L1H, HD]), ALU.mult)
                o.then_inc(s_kvn, 1)
            over_tiles(v, step, T, 5)
            v.wait_ge(s_dot, T)
            v.wait_ge(s_zero, 2)
            for h in range(L1H):
                r = slice(h % 2 * HD, h % 2 * HD + HD)
                o = v.tensor_copy(dots[r, h // 2, r], bank[5][r, h // 2 * 128 + h % 2 * HD:h // 2 * 128 + h % 2 * HD + HD])
            o.then_inc(s_dsb, 1)

        @block.tensor
        def _(pe):
            pe.wait_ge(s_cw, 3)

            def turn(t, b):
                wait_count(pe, s_xT, t)
                pe.wait_ge(s_xn, t + 1)
                for c in range(KC):
                    mm = pe.transpose(bank[4][:, c * 128:c * 128 + P], xn[:, b, c * 128:(c + 1) * 128], g["ident"][0:P, 0:P])
                mm.then_inc(s_tr, 1)

            def keys(t, b, n):
                if n == 0:
                    pe.wait_ge(s_xT, t + 1)
                    wait_count(pe, s_kvn, t - 1)
                for c in range(KC):
                    mm = pe.matmul(bank[2 * n + b][0:P, :], xT[:, b, c, :], wkv[:, c, n * KV:(n + 1) * KV],
                                   start=c == 0, stop=c == 1)
                if n == 1:
                    mm.then_inc(s_kv, 1)

            def products(t, b):
                pe.wait_ge(s_kvn, t + 1)
                for j in range(KV // 128):
                    mm = pe.matmul(bank[5][:, j * 128:(j + 1) * 128], kvn[:, b, KV + j * 128:KV + (j + 1) * 128],
                                   kvn[:, b, j * 128:(j + 1) * 128], start=at_first(t) and j == 0, stop=at_last(t), skip_group_check=True)
                mm.then_inc(s_dot, 1)

            def step(t, b):
                if not at_last(t):
                    keys(t + 1, 1 - b, 0)
                if inside(t + 2, T):
                    turn(t + 2, b)
                if not at_last(t):
                    keys(t + 1, 1 - b, 1)
                if inside(t - 1, T):
                    products(t - 1, 1 - b)
            turn(0, 0)
            turn(1, 1)
            keys(0, 0, 0)
            keys(0, 0, 1)
            over_tiles(pe, step, T, 4)
            products(T - 1, (T - 1) % 2)
            pe.wait_ge(s_dsb, 1)
            for j in range(KV // 128):
                mm = pe.matmul(bank[6 + j // 2][:, j % 2 * D:(j % 2 + 1) * D], dots[:, j, :], wo[:, j, :], start=True, stop=True)
            mm.then_inc(s_g, 1)
            pe.wait_ge(s_gsb, 1)
            for m in range(KC):
                for j in range(KV // 128):
                    mm = pe.matmul(bank[m][:, 0:D], wq[:, j, m * 128:(m + 1) * 128], gm[:, j, :], start=j == 0, stop=j == 3)
            mm.then_inc(s_c, 1)

        @block.scalar
        def _(act):
            act.wait_ge(s_zero, 2)

            def scale(t, r, b):
                act.wait_ge(s_y[b], r * (16 * TOPK) + 16 * TOPK)
                for c in range(TOPK):
                    o = act.activation(yg[:, b, c, :], yg[:, b, c, :], ACT.Copy, scale=pr[:, b, c:c + 1])
                o.then_inc(s_scaled, 1)

            def roots(t, b):
                act.wait_ge(s_mv, t + 1)
                wait_count(act, s_rstd, t - 1)
                act.activation(root[:, b, :], mv[:, b, 1:2], ACT.Sqrt, bias=eps[:, :]).then_inc(s_rx, 1)

            def turned(t, b):
                act.wait_ge(s_tr, t + 1)
                act.copy(xT[:, b, :, :], bank[4][:, 0:256].rearrange("p (c q) -> p c q", c=2)[:, :, 0:P]).then_inc(s_xT, 1)

            def step(t, r, b):
                act.wait_ge(s_kv, t + 1)
                wait_count(act, s_v1, t)
                for n in range(2):
                    o = act.activation(sq[:, n * KV:(n + 1) * KV], bank[2 * n + b % 2][0:P, :], ACT.Square)
                o.then_inc(s_sq, 1)
                if inside(t + 3, T):
                    roots(t + 3, 1 - b % 2)
                act.wait_ge(s_v1, t + 1)
                act.activation(var[:, b % 2, :], var[:, b % 2, :], ACT.Sqrt, bias=eps[:, :], scale=1.0 / HD).then_inc(s_r1, 1)
                if inside(t + 2, T):
                    turned(t + 2, b % 2)
                if inside(t + 5, T):
                    scale(t + 5, r + 1 if b + 1 < R else r + 2, (b + 1) % R)
            for t in range(5):
                scale(t, t // R, t % R)
                if t < 3:
                    roots(t, t % 2)
            turned(0, 0)
            turned(1, 1)
            over_rounds(act, step, T // R - 1, R, T % R + R)
            act.wait_ge(s_g, 1)
            for j in range(2):
                o = act.copy(gm[:, 2 * j:2 * j + 2, :], bank[6 + j][:, :].rearrange("p (k f) -> p k f", k=2))
            o.then_inc(s_gsb, 1)
            act.wait_ge(s_c, 1)
            for m in range(KC):
                act.activation(g["c1"][:, m, :], bank[m][:, 0:D], ACT.Copy, scale=1.0 / N)


def l1_update(nc, a, g, w_up):
    bank, x = g["bank"], g["x"]
    with Stage(nc, "U") as st:
        wd, wf, wu, bd, bf, bo = (w_up[n] for n in ("wd", "wf", "wu", "bd", "bf", "bo"))
        xn = st.sb("xn", [P, 2, D])
        xb = st.sb("xb", [P, 2, D])
        xT = st.sb("xT", [128, 2, KC, P])
        tm = st.sb("tm", [P, 2, HD])
        rc = st.sb("rc", [P, T])
        nf = st.sb("nf", [2 * HD, 2, P])
        fu = st.sb("fu", [HD, 2, P])
        s_w = w_up["sem"]
        s_bo, s_xb, s_taken = st.sem("out_bias"), st.sem("xn_bias"), st.sem("taken")
        s_rc, s_xn, s_tr, s_xT, s_nf_ps, s_nf, s_fu_ps, s_fu, s_o, s_x0, s_x = (st.sem(n) for n in (
            "rcount", "xn", "transposed", "xT", "nf_psum", "nf", "fused_psum", "fused", "out", "x0", "x"))
        block = st.block()


        @block.vector
        def _(v):
            v.tensor_scalar(rc[:, :], g["time"][:, :, HD], 1.0, None, ALU.max).then_inc(s_rc, 1)
            v.wait_ge(s_rc, 1)
            v.reciprocal(rc[:, :], rc[:, :]).then_inc(s_rc, 1)
            v.wait_ge(s_rc, 2)

            def prepare(t, b):
                wait_count(v, s_tr, t - 1)
                wait_count(v, s_xb, t - 1)
                v.tensor_scalar(xn[:, b, :], tile_of(x, t), tile_of(g["mv"], t)[:, 0:1], g["rstd"][:, bass.ds(t, 1)],
                                ALU.subtract, ALU.mult)
                v.tensor_scalar(tm[:, b, :], tile_of(g["time"], t)[:, 0:HD], rc[:, bass.ds(t, 1)], None, ALU.mult).then_inc(s_xn, 1)

            def statistics(t):
                v.wait_ge(s_x, t + 1)
                v.sem_inc(s_taken, 1)
                v.bn_stats(tile_of(g["stats"], t), tile_of(x, t))

            def step(t, b):
                if inside(t + 2, T):
                    prepare(t + 2, b)
                if inside(t - 1, T):
                    statistics(t - 1)
                v.wait_ge(s_xb, t + 1)
                v.tensor_tensor(tile_of(x, t), tile_of(x, t), xb[:, b, :], ALU.add).then_inc(s_x0, 1)
                v.wait_ge(s_x0, t + 1)
                v.wait_ge(s_o, t + 1)
                v.tensor_tensor(tile_of(x, t), tile_of(x, t), bank[6 + b][0:P, 0:D], ALU.add).then_inc(s_x, 1)
            prepare(0, 0)
            prepare(1, 1)
            over_tiles(v, step, T, 4)
            statistics(T - 1)

        @block.gpsimd
        def _(gp):
            gp.wait_ge(s_w, 112)
            gp.tensor_tensor(bo[:, 0, :], bo[:, 0, :], bo[:, 1, :], ALU.add).then_inc(s_bo, 1)
            gp.wait_ge(s_bo, 1)

            def add_bias(t, b):
                wait_count(gp, s_x0, t - 1)
                gp.wait_ge(s_xn, t + 1)
                gp.tensor_tensor(xb[:, b, :], xn[:, b, :], bo[:, 0, :], ALU.add).then_inc(s_xb, 1)
            over_tiles(gp, add_bias)

        @block.tensor
        def _(pe):
            pe.wait_ge(s_w, 112)

            def turn(t, b):
                pe.wait_ge(s_xn, t + 1)
                for c in range(KC):
                    pe.transpose(bank[b][:, c * 128:c * 128 + P], xn[:, b, c * 128:(c + 1) * 128], g["ident"][0:P, 0:P])
                pe.transpose(bank[b][0:HD, 256:256 + P], tm[:, b, :], g["ident"][0:P, 0:P]).then_inc(s_tr, 1)

            def first(t, b):
                pe.wait_ge(s_xT, t + 1)
                for c in range(KC):
                    mm = pe.matmul(bank[2 + b][0:HD, 0:P], wd[:, c, :], xT[:, b, c, :], start=c == 0, stop=c == 1)
                mm.then_inc(s_nf_ps, 1)
                wait_count(pe, s_x, t - 1)
                for c in range(KC):
                    pe.matmul(bank[6 + b][0:P, 0:D], xT[:, b, c, :], g["c1"][:, c, :], start=c == 0, stop=False)

            def step(t, b):
                pe.wait_ge(s_nf, t + 1)
                pe.matmul(bank[4 + b][0:HD, 0:P], wf[:, :], nf[:, b, :], start=True, stop=True).then_inc(s_fu_ps, 1)
                if inside(t + 1, T):
                    first(t + 1, 1 - b)
                if inside(t + 2, T):
                    turn(t + 2, b)
                pe.wait_ge(s_fu, t + 1)
                pe.matmul(bank[6 + b][0:P, 0:D], fu[:, b, :], wu[:, :], start=False, stop=True).then_inc(s_o, 1)
            turn(0, 0)
            turn(1, 1)
            first(0, 0)
            over_tiles(pe, step, T, 4)

        @block.scalar
        def _(act):
            act.wait_ge(s_w, 112)

            def turned(t, b):
                act.wait_ge(s_tr, t + 1)
                act.copy(nf[HD:2 * HD, b, :], bank[b][0:HD, 256:256 + P])
                act.copy(xT[:, b, :, :], bank[b][:, 0:256].rearrange("p (c q) -> p c q", c=2)[:, :, 0:P]).then_inc(s_xT, 1)

            def features(t, b):
                act.wait_ge(s_nf_ps, t + 1)
                act.activation(nf[0:HD, b, :], bank[2 + b][0:HD, 0:P], ACT.Relu, bias=bd[:, :]).then_inc(s_nf, 1)

            def step(t, b):
                act.wait_ge(s_fu_ps, t + 1)
                act.activation(fu[:, b, :], bank[4 + b][0:HD, 0:P], ACT.Relu, bias=bf[:, :]).then_inc(s_fu, 1)
                if inside(t + 1, T):
                    features(t + 1, 1 - b)
                if inside(t + 2, T):
                    turned(t + 2, b)
            turned(0, 0)
            turned(1, 1)
            features(0, 0)
            over_tiles(act, step, T, 4)




_INS = ['x', 'src', 'dst', 'edge_attr_32', 'L0_gnn_W', 'L0_gnn_Wl', 'L0_gnn_Wr', 'L0_gnn_b', 'L0_mix_w_qkv',
        'L0_mix_b_qkv', 'L0_mix_norm_g', 'L0_mix_norm_b', 'L0_mix_w_fc1', 'L0_mix_b_fc1', 'L0_mix_w_fc2',
        'L0_mix_b_fc2', 'L0_ffn_Wg', 'L0_ffn_bg', 'L0_ffn_W1', 'L0_ffn_b1', 'L0_ffn_W2', 'L0_ffn_b2',
        'L1_gnn_W_down', 'L1_gnn_b_down', 'L1_gnn_W_time', 'L1_gnn_b_time', 'L1_gnn_W_fusion',
        'L1_gnn_b_fusion', 'L1_gnn_W_up', 'L1_gnn_b_up', 'L1_mix_w_qkv', 'L1_mix_w_out', 'L1_mix_b_out',
        'L1_ffn_router_w', 'L1_ffn_w1', 'L1_ffn_w2', 'L1_ffn_w3']


def layouts(x):
    import numpy as np

    def cols(b):
        return np.ascontiguousarray(b.reshape(-1, 128).T)

    def T(w):
        return np.ascontiguousarray(np.swapaxes(w, -1, -2))

    keep = ['x', 'src', 'dst', 'edge_attr_32', 'L0_gnn_W', 'L0_gnn_b', 'L0_mix_w_qkv', 'L0_mix_b_qkv',
            'L0_mix_w_fc1', 'L0_mix_w_fc2', 'L0_mix_b_fc2', 'L0_ffn_bg', 'L0_ffn_b2', 'L1_gnn_b_time',
            'L1_gnn_b_up', 'L1_mix_w_qkv', 'L1_mix_b_out', 'L0_ffn_b1']
    a = {n: np.ascontiguousarray(x[n]) for n in keep}
    a['L0_gnn_W_T'] = T(x['L0_gnn_W'])
    a['L0_gnn_Wl_T'] = T(x['L0_gnn_Wl'])
    a['L0_gnn_Wr_T'] = T(x['L0_gnn_Wr'])
    a['L0_mix_w_q_T'] = T(x['L0_mix_w_qkv'][:, :D])
    a['L0_mix_b_q_cols'] = cols(x['L0_mix_b_qkv'][:D])
    for n in ('L0_mix_norm_g', 'L0_mix_norm_b', 'L0_mix_b_fc1'):
        a[n + '_cols'] = cols(x[n])
    a['L0_ffn_b1_cols'] = np.ascontiguousarray(x['L0_ffn_b1'].reshape(-1, 128).T)
    for n in ('L0_ffn_Wg', 'L0_ffn_W1', 'L0_ffn_W2', 'L1_gnn_W_down', 'L1_gnn_W_time', 'L1_gnn_W_fusion',
              'L1_gnn_W_up', 'L1_mix_w_out', 'L1_ffn_router_w', 'L1_ffn_w1', 'L1_ffn_w2', 'L1_ffn_w3'):
        a[n + '_T'] = T(x[n])
    a['L1_mix_w_kv_T'] = T(x['L1_mix_w_qkv'][512:])
    for n in ('L1_gnn_b_down', 'L1_gnn_b_fusion'):
        a[n + '_col'] = np.ascontiguousarray(x[n].reshape(64, 1))
    return a


def kernel(**inputs):
    import numpy as _np
    import concourse.bacc as _bacc
    from concourse import mybir as _mybir
    from concourse.bass_utils import run_bass_kernel_spmd as _run

    nc = _bacc.Bacc("TRN2", target_bir_lowering=False, num_devices=1)
    laid = layouts({n: _np.asarray(inputs[n]) for n in _INS})
    arrays, aps = {}, {}
    for name, v in laid.items():
        arrays[f"in_{name}"] = v
        aps[name] = nc.dram_tensor(f"in_{name}", v.shape, _mybir.dt.from_np(v.dtype), kind="ExternalInput").ap()
    out = nc.dram_tensor("out_dram", (N, D), F32, kind="ExternalOutput").ap()
    build(nc, aps, out)
    r = _run(nc, [arrays], core_ids=[0])
    return r.results[0]["out_dram"]
```
